# Optimizing a Trainium2 kernel written in Bass

```python
import numpy as np
import jax
import jax.numpy as jnp

def _softmax(x, axis=-1):
    return jax.nn.softmax(x, axis=axis)

def _gelu(x):
    return jax.nn.gelu(x, approximate=True)

def _silu(x):
    return jax.nn.silu(x)

def _sigmoid(x):
    return jax.nn.sigmoid(x)

def _layernorm(x, axis=-1, eps=1e-05):
    m = jnp.mean(x, axis=axis, keepdims=True)
    v = jnp.var(x, axis=axis, keepdims=True)
    return (x - m) / jnp.sqrt(v + eps)

def _scatter_add(tgt, idx, src, axis=0):
    return tgt.at[idx].add(src)

def _segment_sum(src, seg, n):
    return jax.ops.segment_sum(src, seg, n)
kernel_name = 'mk_sandwich_d1_jaxref_r8_a03e63'

def setup_inputs(seed: int=0):
    np.random.seed(seed)
    _w = jnp.asarray

    def _L0_attn_setup():
        import jax, jax.numpy as jnp
        import numpy as np
        import math
        B, T, C, H = (2, 256, 128, 16)
        HD = C // H
        SCALE = 1.0 / math.sqrt(HD)

        def _e8_head_dirs(n_heads: int) -> np.ndarray:
            roots = []
            for i in range(8):
                for j in range(i + 1, 8):
                    for si in (-1.0, 1.0):
                        for sj in (-1.0, 1.0):
                            r = np.zeros(8, dtype=np.float32)
                            r[i] = si
                            r[j] = sj
                            roots.append(r)
            roots = np.stack(roots)
            roots = roots / np.linalg.norm(roots, axis=1, keepdims=True)
            return roots[:n_heads]
        key = jax.random.key(seed)
        k1, k2, k3, k4 = jax.random.split(key, 4)
        x = jax.random.normal(k1, (B, T, C), dtype=jnp.float32)
        w_qkv = jax.random.normal(k2, (C, 3 * C), dtype=jnp.float32) * (1.0 / math.sqrt(C))
        w_out = jax.random.normal(k3, (C, C), dtype=jnp.float32) * (1.0 / math.sqrt(C))
        head_scales = jax.random.normal(k4, (H,), dtype=jnp.float32) * 0.1
        head_dirs = jnp.asarray(_e8_head_dirs(H))
        return {'x': x, 'w_qkv': w_qkv, 'w_out': w_out, 'head_scales': head_scales, 'head_dirs': head_dirs}
    _L0_attn_in = _L0_attn_setup()

    def _L0_ffn_setup():
        import jax, jax.numpy as jnp
        import numpy as np
        D_MODEL = 128
        HIDDEN = 512
        NUM_ROUTED = 7
        TOP_K = 2

        def _swiglu(x_flat, wg, wu, wd):
            g = jnp.einsum('nd,edh->enh', x_flat, wg)
            u = jnp.einsum('nd,edh->enh', x_flat, wu)
            h = jax.nn.silu(g) * u
            return jnp.einsum('enh,ehd->end', h, wd)
        key = jax.random.key(seed)
        ks = jax.random.split(key, 8)
        s = 0.02
        return {'x': jax.random.normal(ks[0], (4, 256, D_MODEL), jnp.float32), 'router_w': jax.random.normal(ks[1], (NUM_ROUTED, D_MODEL), jnp.float32) * s, 'w_gate': jax.random.normal(ks[2], (NUM_ROUTED, D_MODEL, HIDDEN), jnp.float32) * s, 'w_up': jax.random.normal(ks[3], (NUM_ROUTED, D_MODEL, HIDDEN), jnp.float32) * s, 'w_down': jax.random.normal(ks[4], (NUM_ROUTED, HIDDEN, D_MODEL), jnp.float32) * s, 'sw_gate': jax.random.normal(ks[5], (1, D_MODEL, HIDDEN), jnp.float32) * s, 'sw_up': jax.random.normal(ks[6], (1, D_MODEL, HIDDEN), jnp.float32) * s, 'sw_down': jax.random.normal(ks[7], (1, HIDDEN, D_MODEL), jnp.float32) * s}
    _L0_ffn_in = _L0_ffn_setup()
    _d = {'L0_attn_x': _L0_attn_in['x'], 'L0_attn_w_qkv': _L0_attn_in['w_qkv'], 'L0_attn_w_out': _L0_attn_in['w_out'], 'L0_attn_head_scales': _L0_attn_in['head_scales'], 'L0_attn_head_dirs': _L0_attn_in['head_dirs'], 'L0_ffn_router_w': _L0_ffn_in['router_w'], 'L0_ffn_w_gate': _L0_ffn_in['w_gate'], 'L0_ffn_w_up': _L0_ffn_in['w_up'], 'L0_ffn_w_down': _L0_ffn_in['w_down'], 'L0_ffn_sw_gate': _L0_ffn_in['sw_gate'], 'L0_ffn_sw_up': _L0_ffn_in['sw_up'], 'L0_ffn_sw_down': _L0_ffn_in['sw_down']}
    _x0 = _d['L0_attn_x']
    _d['L0_attn_x'] = jax.random.normal(jax.random.fold_in(jax.random.key(seed), 1), (2, 1024, 128), dtype=_x0.dtype)
    del _x0
    return _d

def reference(L0_attn_x, L0_attn_w_qkv, L0_attn_w_out, L0_attn_head_scales, L0_attn_head_dirs, L0_ffn_router_w, L0_ffn_w_gate, L0_ffn_w_up, L0_ffn_w_down, L0_ffn_sw_gate, L0_ffn_sw_up, L0_ffn_sw_down):

    def _L0_attn_ref(x, w_qkv, w_out, head_scales, head_dirs):
        import jax, jax.numpy as jnp
        import numpy as np
        import math
        B, T, C, H = (2, 256, 128, 16)
        HD = C // H
        SCALE = 1.0 / math.sqrt(HD)

        def _e8_head_dirs(n_heads: int) -> np.ndarray:
            roots = []
            for i in range(8):
                for j in range(i + 1, 8):
                    for si in (-1.0, 1.0):
                        for sj in (-1.0, 1.0):
                            r = np.zeros(8, dtype=np.float32)
                            r[i] = si
                            r[j] = sj
                            roots.append(r)
            roots = np.stack(roots)
            roots = roots / np.linalg.norm(roots, axis=1, keepdims=True)
            return roots[:n_heads]
        Bx, Tx, Cx = x.shape
        qkv = (x @ w_qkv).reshape(Bx, Tx, 3, H, HD)
        qkv = jnp.transpose(qkv, (2, 0, 3, 1, 4))
        q, k, v = (qkv[0], qkv[1], qkv[2])
        scores = jnp.einsum('bhqd,bhkd->bhqk', q, k) * SCALE
        causal = jnp.tril(jnp.ones((Tx, Tx), dtype=bool))
        scores = jnp.where(causal[None, None], scores, -jnp.inf)
        q_proj = jnp.einsum('bhtd,hd->bht', q[..., :8], head_dirs)
        k_proj = jnp.einsum('bhtd,hd->bht', k[..., :8], head_dirs)
        geo_bias = q_proj[..., :, None] * k_proj[..., None, :]
        scores = scores + head_scales[None, :, None, None] * geo_bias
        attn = jax.nn.softmax(scores, axis=-1)
        out = jnp.einsum('bhqk,bhkd->bhqd', attn, v)
        out = jnp.transpose(out, (0, 2, 1, 3)).reshape(Bx, Tx, Cx)
        return out @ w_out

    def _L0_ffn_ref(x, router_w, w_gate, w_up, w_down, sw_gate, sw_up, sw_down):
        import jax, jax.numpy as jnp
        import numpy as np
        D_MODEL = 128
        HIDDEN = 512
        NUM_ROUTED = 7
        TOP_K = 2

        def _swiglu(x_flat, wg, wu, wd):
            g = jnp.einsum('nd,edh->enh', x_flat, wg)
            u = jnp.einsum('nd,edh->enh', x_flat, wu)
            h = jax.nn.silu(g) * u
            return jnp.einsum('enh,ehd->end', h, wd)
        orig_shape = x.shape
        x_flat = x.reshape(-1, orig_shape[-1])
        N = x_flat.shape[0]
        logits = x_flat @ router_w.T
        top_vals, top_idx = jax.lax.top_k(logits, TOP_K)
        top_w = jax.nn.softmax(top_vals, axis=-1)
        combine = jnp.sum(jax.nn.one_hot(top_idx, NUM_ROUTED, dtype=x.dtype) * top_w[..., None], axis=1)
        routed_out = _swiglu(x_flat, w_gate, w_up, w_down)
        mixed = jnp.einsum('end,ne->nd', routed_out, combine)
        shared_out = _swiglu(x_flat, sw_gate, sw_up, sw_down)
        mixed = mixed + jnp.mean(shared_out, axis=0)
        return mixed.reshape(orig_shape)
    x = L0_attn_x
    x = x + _layernorm(_L0_attn_ref(_layernorm(x, axis=-1), L0_attn_w_qkv, L0_attn_w_out, L0_attn_head_scales, L0_attn_head_dirs), axis=-1)
    x = x + _layernorm(_L0_ffn_ref(_layernorm(x, axis=-1), L0_ffn_router_w, L0_ffn_w_gate, L0_ffn_w_up, L0_ffn_w_down, L0_ffn_sw_gate, L0_ffn_sw_up, L0_ffn_sw_down), axis=-1)
    return x

_drawn_inputs = setup_inputs


def setup_inputs(seed=0):
    import zlib

    import numpy as np

    out = dict(_drawn_inputs(seed))
    spreads = {}
    factors = {}
    for name, (base, spread) in spreads.items():
        noise = np.random.default_rng([zlib.crc32(name.encode()), seed]).standard_normal(out[name].shape)
        drawn = base * np.exp(spread * noise) if base else spread * noise
        out[name] = jnp.asarray(drawn.astype(out[name].dtype))
    for name, factor in factors.items():
        out[name] = (out[name] * factor).astype(out[name].dtype)
    return out
```

```python
from contextlib import ExitStack

import numpy as np

import concourse.bass as bass
from concourse import mybir

F32 = mybir.dt.float32
BF16 = mybir.dt.bfloat16
U32 = mybir.dt.uint32
ALU = mybir.AluOpType
ACT = mybir.ActivationFunctionType
AX = mybir.AxisListType

B, T, C, H = 2, 1024, 128, 16
HD = C // H
SCALE = 1.0 / float(np.sqrt(HD))
P = 128
KT = T // P
NT = B * KT
HG = 4
NG = H // HG
GROUPS = B * NG
HQ = 32
COMBOS = ((0, 0), (0, 1), (0, 2), (1, 0), (1, 1), (2, 0))
KR = HD * len(COMBOS)
MR = KR + 3
BANK = 512
NEG = -3.0e38
ONES_BITS = float(np.array([0x3F803F80], np.uint32).view(np.float32)[0])
EPS = 1e-5
E, HID = 7, 512
NE = E + 1
HT = HID // P
TILES = (2 * B * T + E * (P - 1)) // P
TILES += TILES % 2
ROUTE = 64
CH = BANK // P
STACKS = 3
CREDIT = 2
BURST = 256
SKEW = 4
LOADS = 2 * len(COMBOS) + 1
RING = 3


class Count:

    def __init__(self):
        self.base, self.n, self.outer = 0, 0, []

    def one(self):
        self.n += 1
        return 1

    def now(self):
        return self.base + self.n

    def enter(self, i, per_turn):
        self.outer.append((self.base, self.n, per_turn))
        self.base, self.n = self.base + self.n + i * per_turn, 0

    def leave(self, turns):
        base, n, per_turn = self.outer.pop()
        assert self.n == per_turn, (self.n, per_turn)
        self.base, self.n = base, n + per_turn * turns


def units():
    return [(j, h) for j in range(KT) for h in range(HG)]


def pieces(width):
    return [(a, min(a + BANK, width)) for a in range(0, width, BANK)]


PIECES_BEFORE = [0]
for _j, _h in units():
    PIECES_BEFORE.append(PIECES_BEFORE[-1] + len(pieces(T - P * _j)))
PIECES = PIECES_BEFORE[-1]
TURNED = ((0, 3), (3, 6), (6, 8))
SLOTS = PIECES + len(TURNED)
assert PIECES % RING == 0 and SLOTS % RING == 0


def program(nc, x, wqkv, wq_t, dirs, scales, w_out, router_t, w_gate, w_up, w_down, out):
    ctx = ExitStack()
    with ctx:
        def sb(name, shape, dt=F32):
            return ctx.enter_context(nc.sbuf_tensor(name, shape, dt))

        front = ctx.enter_context(ExitStack())

        def sb_front(name, shape, dt=F32):
            return front.enter_context(nc.sbuf_tensor(name, shape, dt))

        def sem(name):
            return ctx.enter_context(nc.semaphore(name))

        q_parts = nc.dram_tensor("q_parts", [3, GROUPS, HG * HD, T], BF16, kind="Internal").ap()
        k_parts = nc.dram_tensor("k_parts", [3, GROUPS, HG * HD, T], BF16, kind="Internal").ap()

        sorted_rows = nc.dram_tensor("sorted_rows", [TILES * P, C], F32, kind="Internal").ap()
        sorted_results = nc.dram_tensor("sorted_results", [TILES * P, C], F32, kind="Internal").ap()

        x_sb = sb("x_sb", [P, NT, C])
        w_out_sb = sb("w_out_sb", [C, C])
        router_sb = sb("router_sb", [C, E])
        ident = sb("ident", [P, P])
        ident_b = sb("ident_b", [P, P], BF16)
        o_raw = sb("o_raw", [P, GROUPS, KT, HG, HD + 1])
        stats = sb("stats", [P, NT, 6])
        mean_var = sb("mean_var", [P, NT, 2])
        var_eps = sb("var_eps", [P, NT])
        std = sb("std", [P, NT])
        rstd = sb("rstd", [P, NT])

        xn_stage = sb_front("xn_stage", [P, 2, CH, C])
        xn_t = sb_front("xn_t", [C, 2, BANK])
        wqkv_sb = sb_front("wqkv_sb", [C, 3 * C])
        wq_t_sb = sb_front("wq_t_sb", [C, C])
        wq_fold = sb_front("wq_fold", [C, C])
        dirs_sb = sb_front("dirs_sb", [1, C])
        scales_sb = sb_front("scales_sb", [1, H])
        dirs_scaled = sb_front("dirs_scaled", [1, C])
        zeros = sb_front("zeros", [P, P])
        mask_qk = sb_front("mask_qk", [P, P], BF16)
        mask_kq = sb_front("mask_kq", [P, P], BF16)
        same_head = sb_front("same_head", [C, H, HD])
        fold = sb_front("fold", [C, C])
        parts = sb_front("parts", [C, 2, 2, 3, BANK], BF16)
        rest = sb_front("rest", [C, 2, 2, BANK])
        zero_rows = sb_front("zero_rows", [MR - KR, HG * T], BF16)
        v_all = sb_front("v_all", [P, GROUPS, KT, HG * HD])
        q_st = [sb_front(f"q_st{r}", [P, HG, T], BF16) for r in range(STACKS)]
        k_st = [sb_front(f"k_st{r}", [P, HG, T], BF16) for r in range(STACKS)]
        v_pad = [sb_front(f"v_pad{r}", [P, KT, HG, HQ]) for r in range(STACKS)]
        mx_part = [sb_front(f"mx_part{r}", [P, HG * KT, 2]) for r in range(STACKS)]
        mx = sb_front("mx", [P, HG * KT])
        mx_t = sb_front("mx_t", [P, HG * KT])
        mx_neg = sb_front("mx_neg", [P, HG * KT])
        mx_rest = sb_front("mx_rest", [P, HG * KT])
        mx_rows = [sb_front(f"mx_rows{r}", [P, 3, HG * KT], BF16) for r in range(STACKS)]
        probs = [sb_front(f"probs{i}", [P, HG, T]) for i in range(2)]
        o_cols = sb_front("o_cols", [P, T])

        banks = ctx.enter_context(nc.psum_tensor("banks", [P, 8 * BANK], F32))

        def bank(i, n=1):
            return banks[:, i * BANK:(i + n) * BANK]

        max_bank = [bank(i) for i in range(RING)]
        score_bank = [bank(RING + i) for i in range(RING)]
        o_bank = [bank(6), bank(7)]

        x_loaded = sem("x_loaded")
        weights_loaded = sem("weights_loaded")
        consts_ready = sem("consts_ready")
        pool_steps = sem("pool_steps")
        vector_steps = sem("vector_steps")
        scalar_steps = sem("scalar_steps")
        dirs_scaled_ready = sem("dirs_scaled_ready")
        outer_ready = sem("outer_ready")
        fold_ready = sem("fold_ready")
        wq_folded = sem("wq_folded")
        wq_fold_ready = sem("wq_fold_ready")
        var_ready = sem("var_ready")
        std_ready = sem("std_ready")
        xn_ready = sem("xn_ready")
        xn_transposed = sem("xn_transposed")
        xn_t_ready = sem("xn_t_ready")
        q_projected = sem("q_projected")
        k_projected = sem("k_projected")
        v_projected = sem("v_projected")
        high_ready = sem("high_ready")
        v_stored = sem("v_stored")
        parts_ready = sem("parts_ready")
        parts_stored = sem("parts_stored")
        stacks_padded = sem("stacks_padded")
        stacks_loaded = [sem(f"stacks_loaded{r}") for r in range(STACKS)]
        v_padded = sem("v_padded")
        rows_zeroed = sem("rows_zeroed")
        max_filled = sem("max_filled")
        max_taken = sem("max_taken")
        rows_split = sem("rows_split")
        rows_ready = sem("rows_ready")
        slot_filled = sem("slot_filled")
        slot_taken = sem("slot_taken")
        pv_done = sem("pv_done")
        o_taken = sem("o_taken")

        block = front.enter_context(nc.Block())

        TURNS, PER_TURN = 2, STACKS

        @block.sync
        def _(sp):
            sp.sem_inc(parts_stored, 1)
            for b in range(B):
                sp.dma_start(x_sb[:, b * KT:(b + 1) * KT, :],
                             x[b].rearrange("(t p) c -> p t c", p=P)).then_inc(x_loaded, 16)
            for dst, src in ((dirs_sb[:, :], dirs), (scales_sb[:, :], scales), (wq_t_sb[:, :], wq_t),
                             (wqkv_sb[:, :], wqkv), (w_out_sb[:, :], w_out), (router_sb[:, :], router_t)):
                sp.dma_start(dst, src).then_inc(weights_loaded, 16)

            with sp.Fori(0, B) as b:
                for half in range(2):
                    sp.wait_ge(parts_ready, b * 2 + half + 1 + CREDIT)
                    for qk, dst in ((0, q_parts), (1, k_parts)):
                        for part in range(3):
                            sp.dma_start(
                                dst[part, bass.ds(b * NG, NG), :, half * BANK:(half + 1) * BANK]
                                .rearrange("g c t -> (g c) t"),
                                parts[:, half, qk, part, :]).then_inc(parts_stored, 16)

            def load_stacks(turn, u):
                n, r = turn * STACKS + u, u % STACKS
                for row, (pq, pk) in enumerate(COMBOS):
                    for dst, src, part in ((q_st[r], q_parts, pq), (k_st[r], k_parts, pk)):
                        sp.dma_start(dst[row * HD:(row + 1) * HD, :, :],
                                     src[part, bass.ds(n, 1), :, :].rearrange("g (h d) t -> d (g h) t", d=HD)
                                     ).then_inc(stacks_loaded[r], 16)
                sp.dma_start(q_st[r][KR:MR, :, :].rearrange("r h t -> r (h t)"), zero_rows[:, :]
                             ).then_inc(stacks_loaded[r], 16)

            def send_rows(n, r):
                sp.wait_ge(rows_split, n + 1)
                for part in range(3):
                    for b in range(4):
                        sp.dma_start(
                            q_st[r][KR + part:KR + part + 1, :, :].rearrange(
                                "o h (i b c) -> o b (h i) c", i=KT, c=32)[:, b, :, :],
                            mx_rows[r][b * 32:(b + 1) * 32, part, :]).then_inc(rows_ready, 16)

            sp.wait_ge(consts_ready, 1)
            sp.wait_ge(stacks_padded, 2 * STACKS)
            sp.wait_ge(parts_stored, 16 * 6 * 4 + 1)
            load_stacks(0, 0)
            load_stacks(0, 1)
            send_rows(0, 0)
            with sp.Fori(0, TURNS) as turn:
                for u in range(PER_TURN):
                    n = turn * PER_TURN + u
                    sp.wait_ge(pv_done, n * KT + CREDIT)
                    load_stacks(turn, u + 2)
                    send_rows(n + 1, (u + 1) % STACKS)
            send_rows(GROUPS - 1, (GROUPS - 1) % STACKS)

        @block.gpsimd
        def _(pool):
            nc.gpsimd.memset(zeros[:, :], 0.0).then_inc(pool_steps, 1)
            nc.gpsimd.memset(same_head[:, :, :], 1.0).then_inc(pool_steps, 1)
            pool.wait_ge(pool_steps, 2)
            nc.gpsimd.affine_select(out=ident[:, :], in_=zeros[:, :], compare_op=ALU.not_equal, fill=1.0,
                                    base=0, pattern=[[-1, P]], channel_multiplier=1).then_inc(pool_steps, 1)
            nc.gpsimd.affine_select(out=ident_b[:, :], in_=zeros[:, :], compare_op=ALU.not_equal, fill=1.0,
                                    base=0, pattern=[[-1, P]], channel_multiplier=1).then_inc(pool_steps, 1)
            nc.gpsimd.affine_select(out=mask_qk[:, :], in_=zeros[:, :], compare_op=ALU.is_ge, fill=NEG,
                                    base=0, pattern=[[-1, P]], channel_multiplier=1).then_inc(pool_steps, 1)
            nc.gpsimd.affine_select(out=mask_kq[:, :], in_=zeros[:, :], compare_op=ALU.is_ge, fill=NEG,
                                    base=0, pattern=[[1, P]], channel_multiplier=-1).then_inc(pool_steps, 1)
            nc.gpsimd.affine_select(out=same_head[:, :, :], in_=same_head[:, :, :], compare_op=ALU.is_ge,
                                    fill=0.0, base=0, pattern=[[-HD, H], [0, HD]],
                                    channel_multiplier=1).then_inc(pool_steps, 1)
            pool.wait_ge(pool_steps, 7)
            nc.gpsimd.affine_select(out=same_head[:, :, :], in_=same_head[:, :, :], compare_op=ALU.is_ge,
                                    fill=0.0, base=HD - 1, pattern=[[HD, H], [0, HD]],
                                    channel_multiplier=-1).then_inc(pool_steps, 1)
            pool.wait_ge(pool_steps, 8)
            nc.gpsimd.memset(zero_rows[:, :], 0.0).then_inc(pool_steps, 1)
            for r in range(STACKS):
                nc.gpsimd.memset(v_pad[r][:, :, :, :], 0.0).then_inc(pool_steps, 1)
                nc.gpsimd.memset(mx_part[r][:, :, :], NEG).then_inc(pool_steps, 1)
            pool.wait_ge(pool_steps, 9 + 2 * STACKS)
            for r in range(STACKS):
                nc.gpsimd.memset(v_pad[r][:, :, :, HD:HD + 1], 1.0).then_inc(pool_steps, 1)
            pool.wait_ge(pool_steps, 9 + 3 * STACKS)
            nc.gpsimd.memset(zeros[:, 0:1], 0.0).then_inc(consts_ready, 1)

            for r in range(STACKS):
                nc.gpsimd.memset(q_st[r][:, :, :].bitcast(F32), 0.0).then_inc(stacks_padded, 1)
                nc.gpsimd.memset(k_st[r][:, :, :].bitcast(F32), ONES_BITS).then_inc(stacks_padded, 1)

            def pad_v(n, r):
                nc.gpsimd.tensor_copy(
                    v_pad[r][:, :, :, 0:HD],
                    v_all[:, bass.ds(n, 1), :, :].rearrange("p g k (h d) -> p (g k) h d", d=HD)
                ).then_inc(v_padded, 1)

            pool.wait_ge(v_stored, 4 + CREDIT)
            pad_v(0, 0)
            pad_v(1, 1)
            with pool.Fori(0, TILES) as k:
                nc.gpsimd.dma_start(sorted_rows[bass.ds(k * P, P), :], zeros[:, :]).then_inc(rows_zeroed, 16)
            with pool.Fori(0, TURNS) as turn:
                for u in range(PER_TURN):
                    n = turn * PER_TURN + u
                    pool.wait_ge(pv_done, n * KT + CREDIT)
                    pad_v(n + 2, (u + 2) % STACKS)
            pool.wait_ge(rows_zeroed, 16 * TILES)

        @block.tensor
        def _(pe):
            pe.sem_inc(pv_done, CREDIT)
            pe.sem_inc(xn_transposed, CREDIT)
            pe.wait_ge(weights_loaded, 16 * 6)
            pe.wait_ge(dirs_scaled_ready, 1)
            nc.tensor.matmul(bank(0)[:, 0:C], dirs_sb[:, :], dirs_scaled[:, :], start=True, stop=True
                             ).then_inc(outer_ready, 1)
            pe.wait_ge(fold_ready, 1)
            nc.tensor.matmul(bank(1)[:, 0:C], wq_t_sb[:, :], fold[:, :], start=True, stop=True
                             ).then_inc(wq_folded, 1)
            pe.wait_ge(wq_fold_ready, 1)
            pe.wait_ge(consts_ready, 1)
            with pe.Fori(0, B) as b:
                for half in range(2):
                    done = b * 2 + half
                    bt, bq, bk, bv = (bank(4 * half + i) for i in range(4))
                    pe.wait_ge(xn_ready, done + 1)
                    pe.wait_ge(xn_t_ready, done + 1)
                    for j in range(CH):
                        last = nc.tensor.transpose(bt[:, j * P:(j + 1) * P], xn_stage[:, half, j, :],
                                                   ident[:, :])
                    last.then_inc(xn_transposed, 1)
                for half in range(2):
                    done = b * 2 + half
                    bt, bq, bk, bv = (bank(4 * half + i) for i in range(4))
                    pe.wait_ge(xn_t_ready, done + 1 + CREDIT)
                    pe.wait_ge(parts_ready, done + 1)
                    nc.tensor.matmul(bq, wq_fold[:, :], xn_t[:, half, :], start=True, stop=True
                                     ).then_inc(q_projected, 1)
                    nc.tensor.matmul(bk, wqkv_sb[:, C:2 * C], xn_t[:, half, :], start=True, stop=True
                                     ).then_inc(k_projected, 1)
                    pe.wait_ge(v_stored, done + 1)
                    for j in range(CH):
                        last = nc.tensor.matmul(bv[:, j * P:(j + 1) * P],
                                                xn_t[:, half, j * P:(j + 1) * P],
                                                wqkv_sb[:, 2 * C:3 * C], start=True, stop=True)
                    last.then_inc(v_projected, 1)

            def max_unit(turn, u, idx):
                m, r = turn * STACKS + u, u % STACKS
                j, h = units()[idx]
                i = KT - 1 - j
                width = T - P * j
                if idx == 0:
                    pe.wait_ge(stacks_loaded[r], (turn + (u // STACKS + 1)) * (16 * LOADS))
                for piece, (a, z) in enumerate(pieces(width)):
                    k = PIECES_BEFORE[idx] + piece
                    dst = max_bank[k % RING]
                    pe.wait_ge(max_taken, m * PIECES + k + 1)
                    last = nc.tensor.matmul(dst[:, 0:z - a], q_st[r][:, h, i * P:(i + 1) * P],
                                            k_st[r][:, h, a:z], start=True, stop=(z < width))
                    if z == width:
                        last = nc.tensor.matmul(dst[:, z - a - P:z - a], ident_b[:, :], mask_qk[:, :],
                                                start=False, stop=True)
                    last.then_inc(max_filled, 1)
                    yield

            def score_unit(n, r, idx):
                j, h = units()[idx]
                for piece, (a, z) in enumerate(pieces(T - P * j)):
                    k = PIECES_BEFORE[idx] + piece
                    dst = score_bank[k % RING]
                    pe.wait_ge(slot_taken, n * SLOTS + k + 1)
                    last = nc.tensor.matmul(dst[:, 0:z - a], k_st[r][:, h, j * P:(j + 1) * P],
                                            q_st[r][:, h, j * P + a:j * P + z],
                                            start=True, stop=(a > 0))
                    if a == 0:
                        last = nc.tensor.matmul(dst[:, 0:P], ident_b[:, :], mask_kq[:, :],
                                                start=False, stop=True)
                    last.then_inc(slot_filled, 1)
                    yield

            def bursts(j):
                return [(max(j * P, a), a + BURST) for a in range(0, T, BURST) if a + BURST > j * P]

            def weighted_values(n, r, j, which):
                for k in which:
                    if k >= len(bursts(j)):
                        continue
                    a, z = bursts(j)[k]
                    if k == 0:
                        pe.wait_ge(slot_taken, n * SLOTS + PIECES_BEFORE[HG * (j + 1)] + RING)
                    if j == 0 and k == 0:
                        pe.wait_ge(o_taken, n * 2 + 1)
                        pe.wait_ge(v_padded, n + 1)
                    c = a // BANK
                    for h in range(HG):
                        last = nc.tensor.matmul(
                            o_bank[c][h * HQ:(h + 1) * HQ, a - c * BANK:z - c * BANK],
                            v_pad[r][:, j, h, :], probs[j % 2][:, h, a - j * P:z - j * P],
                            start=(j == 0 and a % BANK == 0), stop=(j == (c + 1) * CH - 1),
                            skip_group_check=True)
                    if k == len(bursts(j)) - 1:
                        last.then_inc(pv_done, 1)

            def group(turn, u, ahead):
                n, r = turn * STACKS + u, u % STACKS
                pe.wait_ge(rows_ready, (n + 1) * (16 * 12))
                todo = [(turn, u + 1, i) for i in range(SKEW, KT * HG)] if ahead > 0 else []
                if ahead > 1:
                    todo += [(turn, u + 2, i) for i in range(SKEW)]
                for idx in range(KT * HG):
                    first = max_unit(*todo.pop(0)) if todo and idx < KT * HG - 2 else iter(())
                    for _ in score_unit(n, r, idx):
                        next(first, None)
                    for _ in first:
                        pass
                    if idx >= HG:
                        weighted_values(n, r, idx // HG - 1, [idx % HG])
                weighted_values(n, r, KT - 1, range(HG))
                for unit in todo:
                    for _ in max_unit(*unit):
                        pass
                pe.wait_ge(o_taken, n * 2 + 3)
                for s, (t0, t1) in enumerate(TURNED):
                    dst = score_bank[(PIECES + s) % RING]
                    pe.wait_ge(slot_taken, n * SLOTS + PIECES + s + 1)
                    for t in range(t0, t1):
                        last = nc.tensor.transpose(dst[:, (t - t0) * P:(t - t0 + 1) * P],
                                                   o_cols[:, t * P:(t + 1) * P], ident[:, :])
                    last.then_inc(slot_filled, 1)

            pe.wait_ge(parts_ready, 4 + CREDIT)
            pe.wait_ge(v_stored, 4 + CREDIT)
            for u, idx in [(0, i) for i in range(KT * HG)] + [(1, i) for i in range(SKEW)]:
                for _ in max_unit(0, u, idx):
                    pass
            with pe.Fori(0, TURNS) as turn:
                for u in range(PER_TURN):
                    group(turn, u, 2)
            group(TURNS, 0, 1)
            group(TURNS, 1, 0)

        @block.scalar
        def _(act):
            act.sem_inc(xn_t_ready, CREDIT)
            act.sem_inc(v_stored, CREDIT)
            act.sem_inc(o_taken, 1)
            act.sem_inc(slot_taken, RING)
            act.wait_ge(var_ready, 1)
            nc.scalar.activation(std[:, :], var_eps[:, :], ACT.Sqrt).then_inc(std_ready, 1)
            with act.Fori(0, B) as b:
                act.wait_ge(parts_stored, b * (16 * 6 * 2) + 1)
                for half in range(2):
                    act.wait_ge(xn_transposed, b * 2 + half + 1 + CREDIT)
                    nc.scalar.activation(xn_t[:, half, :], bank(4 * half), ACT.Copy).then_inc(xn_t_ready, 1)
                for half in range(2):
                    bt, bq, bk, bv = (bank(4 * half + i) for i in range(4))
                    act.wait_ge(q_projected, b * 2 + half + 1)
                    nc.scalar.activation(parts[:, half, 0, 0, :], bq, ACT.Copy).then_inc(high_ready, 1)
                    act.wait_ge(k_projected, b * 2 + half + 1)
                    nc.scalar.activation(parts[:, half, 1, 0, :], bk, ACT.Copy).then_inc(high_ready, 1)
                    act.wait_ge(v_projected, b * 2 + half + 1)
                    for j in range(CH):
                        last = nc.scalar.activation(
                            v_all[:, bass.ds(b * NG, NG), half * CH + j, :],
                            bv[:, j * P:(j + 1) * P].rearrange("p (g c) -> p g c", g=NG), ACT.Copy)
                    last.then_inc(v_stored, 1)

            def group(n):
                for idx, (j, h) in enumerate(units()):
                    if h == 0:
                        act.wait_ge(pv_done, n * KT + j + 1)
                    for piece, (a, z) in enumerate(pieces(T - P * j)):
                        k = PIECES_BEFORE[idx] + piece
                        act.wait_ge(slot_filled, n * SLOTS + k + 1)
                        nc.scalar.activation(probs[j % 2][:, h, a:z], score_bank[k % RING][:, 0:z - a],
                                             ACT.Exp).then_inc(slot_taken, 1)
                act.wait_ge(pv_done, n * KT + KT + CREDIT)
                for c in range(2):
                    nc.scalar.activation(o_cols[:, c * BANK:(c + 1) * BANK], o_bank[c], ACT.Copy
                                         ).then_inc(o_taken, 1)
                for s, (t0, t1) in enumerate(TURNED):
                    act.wait_ge(slot_filled, n * SLOTS + PIECES + s + 1)
                    nc.scalar.activation(
                        o_raw[:, bass.ds(n, 1), t0:t1, :, :].rearrange("p g j h d -> p (g j h) d"),
                        score_bank[(PIECES + s) % RING][:, 0:(t1 - t0) * P].rearrange(
                            "p (j d) -> p j d", d=HQ)[:, :, 0:HD + 1],
                        ACT.Copy).then_inc(slot_taken, 1)

            with act.Fori(0, TURNS) as turn:
                for u in range(PER_TURN):
                    group(turn * PER_TURN + u)
            group(GROUPS - 2)
            group(GROUPS - 1)

        @block.vector
        def _(dve):
            step = Count()
            dve.sem_inc(parts_ready, CREDIT)
            dve.sem_inc(max_taken, RING)
            dve.wait_ge(weights_loaded, 16 * 6)
            nc.vector.tensor_tensor(dirs_scaled[:, :].rearrange("o (h d) -> o h d", d=HD),
                                    dirs_sb[:, :].rearrange("o (h d) -> o h d", d=HD),
                                    scales_sb[:, :].unsqueeze(2).broadcast_to([1, H, HD]),
                                    ALU.mult).then_inc(dirs_scaled_ready, 1)
            dve.wait_ge(x_loaded, 32)
            for t in range(NT):
                nc.vector.bn_stats(stats[:, t, :], x_sb[:, t, :]).then_inc(vector_steps, step.one())
            dve.wait_ge(vector_steps, step.now())
            for t in range(NT):
                nc.vector.bn_aggr(mean_var[:, t, :], stats[:, t, :]).then_inc(vector_steps, step.one())
            dve.wait_ge(vector_steps, step.now())
            nc.vector.tensor_scalar(var_eps[:, :], mean_var[:, :, 1], EPS, None, ALU.add
                                    ).then_inc(var_ready, 1)
            dve.wait_ge(outer_ready, 1)
            dve.wait_ge(consts_ready, 1)
            nc.vector.tensor_tensor(fold[:, :], bank(0)[:, 0:C],
                                    same_head[:, :, :].rearrange("p h d -> p (h d)"), ALU.mult
                                    ).then_inc(vector_steps, step.one())
            dve.wait_ge(vector_steps, step.now())
            nc.vector.scalar_tensor_tensor(fold[:, :], ident[:, :], SCALE, fold[:, :], ALU.mult, ALU.add
                                           ).then_inc(fold_ready, 1)
            dve.wait_ge(wq_folded, 1)
            nc.vector.tensor_copy(wq_fold[:, :], bank(1)[:, 0:C]).then_inc(wq_fold_ready, 1)
            dve.wait_ge(std_ready, 1)
            nc.vector.reciprocal(rstd[:, :], std[:, :]).then_inc(vector_steps, step.one())
            dve.wait_ge(vector_steps, step.now())
            with dve.Fori(0, B) as b:
                step.enter(b, 8)
                for half in range(2):
                    dve.wait_ge(xn_transposed, b * 2 + half + 1)
                    for j in range(CH):
                        t = b * KT + half * CH + j
                        last = nc.vector.tensor_scalar(
                            xn_stage[:, half, j, :],
                            x_sb[:, bass.ds(t, 1), :].rearrange("p t c -> p (t c)"),
                            mean_var[:, bass.ds(t, 1), 0], rstd[:, bass.ds(t, 1)],
                            ALU.subtract, ALU.mult)
                    last.then_inc(xn_ready, 1)
                for half in range(2):
                    for qk in range(2):
                        src = bank(4 * half + 1 + qk)
                        high, mid, low = (parts[:, half, qk, i, :] for i in range(3))
                        left = rest[:, half, qk, :]
                        dve.wait_ge(high_ready, b * 4 + half * 2 + qk + 1)
                        nc.vector.tensor_tensor(left, src, high, ALU.subtract
                                                ).then_inc(vector_steps, step.one())
                        dve.wait_ge(vector_steps, step.now())
                        nc.vector.tensor_copy(mid, left).then_inc(vector_steps, step.one())
                        dve.wait_ge(vector_steps, step.now())
                        last = nc.vector.tensor_tensor(low, left, mid, ALU.subtract)
                    last.then_inc(parts_ready, 1)
                step.leave(B)

            def max_unit(m, r, idx):
                j, h = units()[idx]
                i = KT - 1 - j
                for s, (a, z) in enumerate(pieces(T - P * j)):
                    k = PIECES_BEFORE[idx] + s
                    dve.wait_ge(max_filled, m * PIECES + k + 1)
                    nc.vector.tensor_reduce(mx_part[r][:, h * KT + i, s:s + 1], max_bank[k % RING][:, 0:z - a],
                                            AX.X, ALU.max).then_inc(max_taken, 1)

            def split_maxima(m, r):
                dve.wait_ge(max_taken, m * PIECES + PIECES + RING)
                nc.vector.tensor_reduce(mx[:, :], mx_part[r][:, :, :], AX.X, ALU.max
                                        ).then_inc(vector_steps, step.one())
                dve.wait_ge(vector_steps, step.now())
                nc.vector.transpose(mx_t[:, :], mx[:, :]).then_inc(vector_steps, step.one())
                dve.wait_ge(vector_steps, step.now())
                nc.vector.tensor_scalar(mx_neg[:, :], mx_t[:, :], -1.0, None, ALU.mult
                                        ).then_inc(vector_steps, step.one())
                dve.wait_ge(vector_steps, step.now())
                nc.vector.tensor_copy(mx_rows[r][:, 0, :], mx_neg[:, :]).then_inc(vector_steps, step.one())
                dve.wait_ge(vector_steps, step.now())
                nc.vector.tensor_tensor(mx_rest[:, :], mx_neg[:, :], mx_rows[r][:, 0, :], ALU.subtract
                                        ).then_inc(vector_steps, step.one())
                dve.wait_ge(vector_steps, step.now())
                nc.vector.tensor_copy(mx_rows[r][:, 1, :], mx_rest[:, :]).then_inc(vector_steps, step.one())
                dve.wait_ge(vector_steps, step.now())
                nc.vector.tensor_tensor(mx_rows[r][:, 2, :], mx_rest[:, :], mx_rows[r][:, 1, :], ALU.subtract
                                        ).then_inc(rows_split, 1)

            for idx in range(KT * HG):
                max_unit(0, 0, idx)
            split_maxima(0, 0)
            for idx in range(SKEW):
                max_unit(1, 1, idx)
            with dve.Fori(0, TURNS) as turn:
                step.enter(turn, 6 * PER_TURN)
                for u in range(PER_TURN):
                    n = turn * PER_TURN + u
                    for idx in range(SKEW, KT * HG):
                        max_unit(n + 1, (u + 1) % STACKS, idx)
                    split_maxima(n + 1, (u + 1) % STACKS)
                    for idx in range(SKEW):
                        max_unit(n + 2, (u + 2) % STACKS, idx)
                step.leave(TURNS)
            for idx in range(SKEW, KT * HG):
                max_unit(GROUPS - 1, (GROUPS - 1) % STACKS, idx)
            split_maxima(GROUPS - 1, (GROUPS - 1) % STACKS)

        front.close()
        w_g = sb("w_g", [C, NE, HID])
        w_u = sb("w_u", [C, NE, HID])
        w_d = sb("w_d", [P, NE, HT, C])
        x2 = sb("x2", [P, NT, C])
        x2_t = sb("x2_t", [C, NT, P])
        mixed = sb("mixed", [P, NT, C])
        weight = sb("weight", [P, 2, NT])
        slot_u = sb("slot_u", [P, 2, NT], U32)
        tile_expert = sb("tile_expert", [1, TILES], U32)
        upper = sb("upper", [P, P], BF16)
        ones_b = sb("ones_b", [P, P], BF16)
        zeros2 = sb("zeros2", [P, P])

        post = ctx.enter_context(ExitStack())

        def sb_post(name, shape, dt=F32):
            return post.enter_context(nc.sbuf_tensor(name, shape, dt))

        den = sb_post("den", [P, 2, NG, CH, HG])
        attn = sb_post("attn", [P, 2, CH, C])
        attn_t = sb_post("attn_t", [C, 2, BANK])
        proj = sb_post("proj", [P, NT, C])
        logits = sb_post("logits", [P, NT, 8])
        top = sb_post("top", [P, NT, 8])
        top_at = sb_post("top_at", [P, NT, 8], U32)
        iota = sb_post("iota", [P, ROUTE])
        top_at_f = sb_post("top_at_f", [P, NT, 2])
        gap = sb_post("gap", [P, NT])
        gap_exp = sb_post("gap_exp", [P, NT])
        gap_sum = sb_post("gap_sum", [P, NT])
        pick = [sb_post(f"pick{i}", [P, E, NT]) for i in range(2)]
        picked = sb_post("picked", [P, E, NT], BF16)
        before = [sb_post(f"before{i}", [P, E, KT + NT]) for i in range(2)]
        over = sb_post("over", [P, E, NT])
        tiles = sb_post("tiles", [P, E])
        ends = [sb_post(f"ends{i}", [P, 4 + E]) for i in range(2)]
        slot_in = sb_post("slot_in", [P, E, NT])
        slot_all = sb_post("slot_all", [P, E, NT])
        slot_pick = [sb_post(f"slot_pick{i}", [P, E, NT]) for i in range(2)]
        slot_f = sb_post("slot_f", [P, 2, NT])
        passed = sb_post("passed", [1, TILES, E])
        tile_f = sb_post("tile_f", [1, TILES])
        thresholds = sb_post("thresholds", [P, NT])

        route_consts = sem("route_consts")
        experts_loaded = sem("experts_loaded")
        attn_ready = sem("attn_ready")
        attn_transposed = sem("attn_transposed")
        attn_t_ready = sem("attn_t_ready")
        projected = sem("projected")
        proj_ready = sem("proj_ready")
        post_var_ready = sem("post_var_ready")
        post_std_ready = sem("post_std_ready")
        x2_ready = sem("x2_ready")
        x2_transposed = sem("x2_transposed")
        x2_t_ready = sem("x2_t_ready")
        logits_done = sem("logits_done")
        gap_ready = sem("gap_ready")
        gap_exp_ready = sem("gap_exp_ready")
        picked_ready = sem("picked_ready")
        counted = sem("counted")
        post_steps = sem("post_steps")

        with nc.Block() as block:
            at_bank, pr_bank = [bank(0), bank(1)], [bank(2), bank(3)]
            xt_bank, lg_bank, rank_bank, total_bank = bank(4, 4), bank(0), bank(1), bank(2)

            @block.sync
            def _(sp):
                for e in [E] + list(range(E)):
                    sp.dma_start(w_g[:, e, :], w_gate[e]).then_inc(experts_loaded, 16)
                    sp.dma_start(w_u[:, e, :], w_up[e]).then_inc(experts_loaded, 16)
                    sp.dma_start(w_d[:, e, :, :], w_down[e].rearrange("(t p) c -> p t c", p=P)
                                 ).then_inc(experts_loaded, 16)

            @block.gpsimd
            def _(pool):
                nc.gpsimd.iota(iota[:, :], pattern=[[1, ROUTE]], base=0, channel_multiplier=0,
                               allow_small_or_imprecise_dtypes=True).then_inc(route_consts, 1)
                nc.gpsimd.iota(thresholds[:, :], pattern=[[P, NT]], base=0, channel_multiplier=0,
                               allow_small_or_imprecise_dtypes=True).then_inc(route_consts, 1)
                nc.gpsimd.memset(zeros2[:, :], 0.0).then_inc(route_consts, 1)
                nc.gpsimd.memset(ones_b[:, :], 1.0).then_inc(route_consts, 1)
                pool.wait_ge(route_consts, 4)
                nc.gpsimd.affine_select(out=upper[:, :], in_=zeros2[:, :], compare_op=ALU.is_ge, fill=1.0,
                                        base=0, pattern=[[-1, P]], channel_multiplier=1
                                        ).then_inc(route_consts, 1)

            @block.tensor
            def _(pe):
                pe.sem_inc(attn_transposed, CREDIT)
                with pe.Fori(0, B) as b:
                    for half in range(2):
                        pe.wait_ge(attn_ready, b * 2 + half + 1)
                        for j in range(CH):
                            last = nc.tensor.transpose(at_bank[half][:, j * P:(j + 1) * P],
                                                       attn[:, half, j, :], ident[:, :])
                        last.then_inc(attn_transposed, 1)
                    for half in range(2):
                        pe.wait_ge(attn_t_ready, b * 2 + half + 1)
                        pe.wait_ge(proj_ready, b * 2 + half + 1)
                        for j in range(CH):
                            last = nc.tensor.matmul(pr_bank[half][:, j * P:(j + 1) * P],
                                                    attn_t[:, half, j * P:(j + 1) * P], w_out_sb[:, :],
                                                    start=True, stop=True)
                        last.then_inc(projected, 1)
                for q in range(NT // CH):
                    pe.wait_ge(x2_ready, q + 1)
                    for t in range(q * CH, (q + 1) * CH):
                        last = nc.tensor.transpose(xt_bank[:, t * P:(t + 1) * P], x2[:, t, :], ident[:, :])
                    last.then_inc(x2_transposed, 1)
                for q in range(NT // CH):
                    pe.wait_ge(x2_t_ready, q + 1)
                    for t in range(q * CH, (q + 1) * CH):
                        last = nc.tensor.matmul(lg_bank[:, t * 8:t * 8 + E], x2_t[:, t, :], router_sb[:, :],
                                                start=True, stop=True)
                last.then_inc(logits_done, 1)
                pe.wait_ge(picked_ready, 1)
                pe.wait_ge(route_consts, 5)
                flat = picked[:, :, :].rearrange("p e t -> p (e t)")
                nc.tensor.matmul(rank_bank[:, 0:E * NT], upper[:, :], flat, start=True, stop=True
                                 ).then_inc(counted, 1)
                nc.tensor.matmul(total_bank[:, 0:E * NT], ones_b[:, :], flat, start=True, stop=True
                                 ).then_inc(counted, 1)

            @block.scalar
            def _(act):
                act.sem_inc(proj_ready, CREDIT)
                with act.Fori(0, B) as b:
                    for half in range(2):
                        act.wait_ge(attn_transposed, b * 2 + half + 1 + CREDIT)
                        nc.scalar.activation(attn_t[:, half, :], at_bank[half], ACT.Copy
                                             ).then_inc(attn_t_ready, 1)
                    for half in range(2):
                        act.wait_ge(projected, b * 2 + half + 1)
                        nc.scalar.activation(
                            proj[:, bass.ds(b * KT + half * CH, CH), :].rearrange("p t c -> p (t c)"),
                            pr_bank[half], ACT.Copy).then_inc(proj_ready, 1)
                for ln in range(2):
                    act.wait_ge(post_var_ready, ln + 1)
                    nc.scalar.activation(std[:, :], var_eps[:, :], ACT.Sqrt).then_inc(post_std_ready, 1)
                for q in range(NT // CH):
                    act.wait_ge(x2_transposed, q + 1)
                    nc.scalar.activation(x2_t[:, q * CH:(q + 1) * CH, :].rearrange("p t c -> p (t c)"),
                                         xt_bank[:, q * BANK:(q + 1) * BANK], ACT.Copy
                                         ).then_inc(x2_t_ready, 1)
                act.wait_ge(gap_ready, 1)
                nc.scalar.activation(gap_exp[:, :], gap[:, :], ACT.Exp).then_inc(gap_exp_ready, 1)

            @block.vector
            def _(dve):
                step = Count()
                nc.vector.memset(logits[:, :, E:8], NEG).then_inc(post_steps, step.one())
                for buf in before + ends:
                    nc.vector.memset(buf[:], 0.0).then_inc(post_steps, step.one())
                with dve.Fori(0, B) as b:
                    step.enter(b, 2 * NG)
                    for half in range(2):
                        def o_at(g):
                            return o_raw[:, bass.ds(b * NG + g, 1), half * CH:(half + 1) * CH, :, :].rearrange(
                                "p a j h d -> p (a j h) d")

                        dve.wait_ge(attn_transposed, b * 2 + half + 1)
                        for g in range(NG):
                            nc.vector.reciprocal(den[:, half, g, :, :].rearrange("p j h -> p (j h)"),
                                                 o_at(g)[:, :, HD]).then_inc(post_steps, step.one())
                        dve.wait_ge(post_steps, step.now())
                        for g in range(NG):
                            for j in range(CH):
                                last = nc.vector.tensor_tensor(
                                    attn[:, half, j, g * HG * HD:(g + 1) * HG * HD].rearrange(
                                        "p (h d) -> p h d", d=HD),
                                    o_at(g)[:, j * HG:(j + 1) * HG, 0:HD],
                                    den[:, half, g, j, :].unsqueeze(2).broadcast_to([P, HG, HD]), ALU.mult)
                        last.then_inc(attn_ready, 1)
                    step.leave(B)

                def layer_norm(src, ln):
                    for t in range(NT):
                        nc.vector.bn_stats(stats[:, t, :], src[:, t, :]).then_inc(post_steps, step.one())
                    dve.wait_ge(post_steps, step.now())
                    for t in range(NT):
                        nc.vector.bn_aggr(mean_var[:, t, :], stats[:, t, :]).then_inc(post_steps, step.one())
                    dve.wait_ge(post_steps, step.now())
                    nc.vector.tensor_scalar(var_eps[:, :], mean_var[:, :, 1], EPS, None, ALU.add
                                            ).then_inc(post_var_ready, 1)
                    dve.wait_ge(post_std_ready, ln + 1)
                    nc.vector.reciprocal(rstd[:, :], std[:, :]).then_inc(post_steps, step.one())
                    dve.wait_ge(post_steps, step.now())

                dve.wait_ge(proj_ready, 4 + CREDIT)
                layer_norm(proj, 0)
                for t in range(NT):
                    nc.vector.tensor_scalar(proj[:, t, :], proj[:, t, :], mean_var[:, t, 0:1],
                                            rstd[:, t:t + 1], ALU.subtract, ALU.mult
                                            ).then_inc(post_steps, step.one())
                dve.wait_ge(post_steps, step.now())
                nc.vector.tensor_tensor(x_sb[:, :, :], x_sb[:, :, :], proj[:, :, :], ALU.add
                                        ).then_inc(post_steps, step.one())
                dve.wait_ge(post_steps, step.now())
                layer_norm(x_sb, 1)
                for t in range(NT):
                    last = nc.vector.tensor_scalar(x2[:, t, :], x_sb[:, t, :], mean_var[:, t, 0:1],
                                                   rstd[:, t:t + 1], ALU.subtract, ALU.mult)
                    if t % CH == CH - 1:
                        last.then_inc(x2_ready, 1)
                dve.wait_ge(logits_done, 1)
                nc.vector.tensor_copy(logits[:, :, 0:E],
                                      lg_bank[:, 0:NT * 8].rearrange("p (t e) -> p t e", e=8)[:, :, 0:E]
                                      ).then_inc(post_steps, step.one())
                dve.wait_ge(post_steps, step.now())
                for t in range(NT):
                    nc.vector.max(top[:, t, :], logits[:, t, :]).then_inc(post_steps, step.one())
                dve.wait_ge(post_steps, step.now())
                nc.vector.tensor_tensor(gap[:, :], top[:, :, 1], top[:, :, 0], ALU.subtract
                                        ).then_inc(gap_ready, 1)
                for t in range(NT):
                    nc.vector.max_index(top_at[:, t, :], top[:, t, :], logits[:, t, :]
                                        ).then_inc(post_steps, step.one())
                dve.wait_ge(post_steps, step.now())
                nc.vector.tensor_copy(top_at_f[:, :, :], top_at[:, :, 0:2]).then_inc(post_steps, step.one())
                dve.wait_ge(post_steps, step.now())
                dve.wait_ge(route_consts, 5)
                for i in range(2):
                    nc.vector.tensor_tensor(
                        pick[i][:, :, :], iota[:, 0:E].unsqueeze(2).broadcast_to([P, E, NT]),
                        top_at_f[:, :, i].unsqueeze(1).broadcast_to([P, E, NT]), ALU.is_equal
                    ).then_inc(post_steps, step.one())
                dve.wait_ge(post_steps, step.now())
                nc.vector.tensor_tensor(picked[:, :, :], pick[0][:, :, :], pick[1][:, :, :], ALU.add
                                        ).then_inc(picked_ready, 1)
                dve.wait_ge(gap_exp_ready, 1)
                nc.vector.tensor_scalar(gap_sum[:, :], gap_exp[:, :], 1.0, None, ALU.add
                                        ).then_inc(post_steps, step.one())
                dve.wait_ge(post_steps, step.now())
                nc.vector.reciprocal(weight[:, 0, :], gap_sum[:, :]).then_inc(post_steps, step.one())
                dve.wait_ge(post_steps, step.now())
                nc.vector.tensor_tensor(weight[:, 1, :], gap_exp[:, :], weight[:, 0, :], ALU.mult
                                        ).then_inc(post_steps, step.one())
                dve.wait_ge(counted, 2)
                nc.vector.tensor_copy(before[0][:, :, KT:], total_bank[:, 0:E * NT].rearrange(
                    "p (e t) -> p e t", e=E)).then_inc(post_steps, step.one())
                for i, shift in enumerate((1, 2, 4, 8)):
                    src, dst = before[i % 2], before[(i + 1) % 2]
                    dve.wait_ge(post_steps, step.now())
                    nc.vector.tensor_tensor(dst[:, :, KT:], src[:, :, KT:], src[:, :, KT - shift:KT + NT - shift],
                                            ALU.add).then_inc(post_steps, step.one())
                dve.wait_ge(post_steps, step.now())
                sums = before[0]
                nc.vector.tensor_tensor(over[:, :, :], sums[:, :, KT + NT - 1:KT + NT].broadcast_to([P, E, NT]),
                                        thresholds[:, :].unsqueeze(1).broadcast_to([P, E, NT]), ALU.is_gt
                                        ).then_inc(post_steps, step.one())
                nc.vector.tensor_tensor(slot_in[:, :, :], rank_bank[:, 0:E * NT].rearrange(
                    "p (e t) -> p e t", e=E), sums[:, :, KT - 1:KT + NT - 1], ALU.add
                                        ).then_inc(post_steps, step.one())
                dve.wait_ge(post_steps, step.now())
                nc.vector.tensor_reduce(ends[0][:, 4:], over[:, :, :], AX.X, ALU.add
                                        ).then_inc(post_steps, step.one())
                for i, shift in enumerate((1, 2, 4)):
                    src, dst = ends[i % 2], ends[(i + 1) % 2]
                    dve.wait_ge(post_steps, step.now())
                    nc.vector.tensor_tensor(dst[:, 4:], src[:, 4:], src[:, 4 - shift:4 + E - shift], ALU.add
                                            ).then_inc(post_steps, step.one())
                dve.wait_ge(post_steps, step.now())
                end = ends[1]
                nc.vector.tensor_tensor(passed[:, :, :], iota[0:1, 0:TILES].unsqueeze(2).broadcast_to([1, TILES, E]),
                                        end[0:1, 4:].unsqueeze(1).broadcast_to([1, TILES, E]), ALU.is_ge
                                        ).then_inc(post_steps, step.one())
                nc.vector.scalar_tensor_tensor(slot_all[:, :, :], end[:, 3:3 + E].unsqueeze(2).broadcast_to([P, E, NT]),
                                               float(P), slot_in[:, :, :], ALU.mult, ALU.add
                                               ).then_inc(post_steps, step.one())
                dve.wait_ge(post_steps, step.now())
                nc.vector.tensor_reduce(tile_f[:, :], passed[:, :, :], AX.X, ALU.add
                                        ).then_inc(post_steps, step.one())
                for i in range(2):
                    nc.vector.tensor_tensor(slot_pick[i][:, :, :], slot_all[:, :, :], pick[i][:, :, :], ALU.mult
                                            ).then_inc(post_steps, step.one())
                dve.wait_ge(post_steps, step.now())
                nc.vector.tensor_scalar(tile_expert[:, :], tile_f[:, :], float(E - 1), None, ALU.min
                                        ).then_inc(post_steps, step.one())
                for i in range(2):
                    nc.vector.tensor_reduce(slot_f[:, i, :], slot_pick[i][:, :, :].rearrange("p e t -> p t e"),
                                            AX.X, ALU.add).then_inc(post_steps, step.one())
                dve.wait_ge(post_steps, step.now())
                nc.vector.tensor_copy(slot_u[:, :, :], slot_f[:, :, :]).then_inc(post_steps, step.one())
        post.close()

        s_gate = [sb(f"s_gate{i}", [P, BANK]) for i in range(2)]
        s_hidden = [sb(f"s_hidden{i}", [P, HT, BANK]) for i in range(2)]
        rows = [sb(f"rows{i}", [P, C]) for i in range(2)]
        rows_t = [sb(f"rows_t{i}", [C, P]) for i in range(2)]
        gate = [sb(f"gate{i}", [P, HID]) for i in range(2)]
        hidden = [sb(f"hidden{i}", [P, HID]) for i in range(2)]
        hidden_t = [sb(f"hidden_t{i}", [P, HT, P]) for i in range(2)]
        result = [sb(f"result{i}", [P, C]) for i in range(2)]
        back = [sb(f"back{i}", [P, NT, C]) for i in range(2)]

        scattered = sem("scattered")
        s_gate_done = sem("s_gate_done")
        s_up_done = sem("s_up_done")
        s_gate_ready = sem("s_gate_ready")
        s_hidden_ready = sem("s_hidden_ready")
        s_down_done = sem("s_down_done")
        s_down_taken = sem("s_down_taken")
        rows_loaded = [sem(f"rows_loaded{i}") for i in range(2)]
        rows_turned = sem("rows_turned")
        rows_t_ready = sem("rows_t_ready")
        gate_done = sem("gate_done")
        up_done = sem("up_done")
        gate_ready = sem("gate_ready")
        hidden_ready = sem("hidden_ready")
        hidden_turned = sem("hidden_turned")
        hidden_t_ready = sem("hidden_t_ready")
        down_done = sem("down_done")
        result_ready = sem("result_ready")
        result_stored = [sem(f"result_stored{i}") for i in range(2)]
        gathered = [sem(f"gathered{i}") for i in range(NT)]
        mix_steps = sem("mix_steps")
        fin_var = sem("fin_var")
        fin_std = sem("fin_std")
        half_done = sem("half_done")
        out_stored = sem("out_stored")
        CHUNKS = NT // CH

        with nc.Block() as block:
            g_bank, u_bank = [bank(0), bank(1)], [bank(2), bank(3)]
            turn_bank, d_bank, t_bank = [bank(4), bank(5)], bank(6), bank(7)

            @block.gpsimd
            def _(pool):
                for t in range(NT):
                    for i in range(2):
                        nc.gpsimd.indirect_dma_start(
                            sorted_rows, bass.IndirectOffsetOnAxis(ap=slot_u[:, i, t:t + 1], axis=0),
                            x2[:, t, :], None).then_inc(scattered, 16)
                for i in range(2):
                    pool.wait_ge(result_stored[i], 16 * (TILES // 2) + 1)
                for t in range(NT):
                    for i in range(2):
                        nc.gpsimd.indirect_dma_start(
                            back[i][:, t, :], None, sorted_results,
                            bass.IndirectOffsetOnAxis(ap=slot_u[:, i, t:t + 1], axis=0)
                        ).then_inc(gathered[t], 16)

            @block.sync
            def _(sp):
                sp.wait_ge(scattered, 16 * 2 * NT)

                def load_rows(pair, u):
                    k, i = pair * 2 + u, u % 2
                    sp.wait_ge(rows_turned, k + 1)
                    sp.dma_start(rows[i][:, :], sorted_rows[bass.ds(k * P, P), :]
                                 ).then_inc(rows_loaded[i], 16)

                def store_result(pair, u):
                    k, i = pair * 2 + u, u % 2
                    sp.wait_ge(result_ready, k + 1 + 1)
                    sp.dma_start(sorted_results[bass.ds(k * P, P), :], result[i][:, :]
                                 ).then_inc(result_stored[i], 16)

                for i in range(2):
                    sp.sem_inc(result_stored[i], 1)
                    load_rows(0, i)
                with sp.Fori(0, TILES // 2 - 1) as pair:
                    for u in range(2):
                        load_rows(pair, u + 2)
                        store_result(pair, u)
                for u in range(2):
                    store_result(TILES // 2 - 1, u)
                for h in range(2):
                    sp.wait_ge(half_done, h + 1)
                    sp.dma_start(out[h].rearrange("(t p) c -> p t c", p=P),
                                 mixed[:, h * KT:(h + 1) * KT, :]).then_inc(out_stored, 16)
                sp.wait_ge(out_stored, 16 * 2)

            @block.tensor
            def _(pe):
                pe.sem_inc(s_down_done, 1)
                pe.sem_inc(rows_turned, CREDIT)
                pe.wait_ge(experts_loaded, 16 * 3 * NE)
                with pe.Fori(0, CHUNKS) as q:
                    x_at = x2_t[:, bass.ds(q * CH, CH), :].rearrange("c t p -> c (t p)")
                    for t in range(HT):
                        pe.wait_ge(s_hidden_ready, q * HT + t + 1)
                        nc.tensor.matmul(g_bank[t % 2], w_g[:, E, t * P:(t + 1) * P], x_at,
                                         start=True, stop=True).then_inc(s_gate_done, 1)
                        nc.tensor.matmul(u_bank[t % 2], w_u[:, E, t * P:(t + 1) * P], x_at,
                                         start=True, stop=True).then_inc(s_up_done, 1)
                    pe.wait_ge(s_hidden_ready, q * HT + HT + CREDIT)
                    pe.wait_ge(s_down_taken, q + 1)
                    for j in range(CH):
                        for t in range(HT):
                            last = nc.tensor.matmul(
                                d_bank[:, j * P:(j + 1) * P],
                                s_hidden[0][:, t, j * P:(j + 1) * P], w_d[:, E, t, :],
                                start=(t == 0), stop=(t == HT - 1))
                    last.then_inc(s_down_done, 1)

                pe.wait_ge(s_hidden_ready, CHUNKS * HT + CREDIT)
                pe.wait_ge(s_down_taken, CHUNKS + 1)

                def expert_of(k):
                    return pe.value_load(tile_expert[0:1, bass.ds(k, 1)], min_val=0, max_val=E - 1)

                def turn(pair, u):
                    k, i = pair * 2 + u, u % 2
                    pe.wait_ge(rows_loaded[i], (pair + (u // 2 + 1)) * 16)
                    pe.wait_ge(rows_t_ready, k + 1)
                    nc.tensor.transpose(t_bank[:, i * P:(i + 1) * P], rows[i][:, :], ident[:, :]
                                        ).then_inc(rows_turned, 1)

                def up(pair, u):
                    k, i = pair * 2 + u, u % 2
                    e = expert_of(k)
                    pe.wait_ge(rows_t_ready, k + 1 + 1)
                    pe.wait_ge(hidden_ready, k + 1)
                    nc.tensor.matmul(g_bank[i], rows_t[i][:, :],
                                     w_g[:, bass.ds(e, 1), :].rearrange("c e h -> c (e h)"),
                                     start=True, stop=True).then_inc(gate_done, 1)
                    nc.tensor.matmul(u_bank[i], rows_t[i][:, :],
                                     w_u[:, bass.ds(e, 1), :].rearrange("c e h -> c (e h)"),
                                     start=True, stop=True).then_inc(up_done, 1)

                def down(pair, u):
                    k, i = pair * 2 + u, u % 2
                    e = expert_of(k)
                    pe.wait_ge(hidden_ready, k + 1 + CREDIT)
                    pe.wait_ge(hidden_t_ready, k + 1)
                    for t in range(HT):
                        last = nc.tensor.transpose(turn_bank[i][:, t * P:(t + 1) * P],
                                                   hidden[i][:, t * P:(t + 1) * P], ident[:, :])
                    last.then_inc(hidden_turned, 1)
                    return e

                def project(pair, u, e):
                    k, i = pair * 2 + u, u % 2
                    pe.wait_ge(hidden_t_ready, k + 1 + CREDIT)
                    pe.wait_ge(result_ready, k + 1)
                    for t in range(HT):
                        last = nc.tensor.matmul(d_bank[:, 0:P], hidden_t[i][:, t, :],
                                                w_d[:, bass.ds(e, 1), t, :].rearrange("p e c -> p (e c)"),
                                                start=(t == 0), stop=(t == HT - 1))
                    last.then_inc(down_done, 1)

                turn(0, 0)
                up(0, 0)
                turn(0, 1)
                with pe.Fori(0, TILES // 2 - 1) as pair:
                    for u in range(2):
                        up(pair, u + 1)
                        e = down(pair, u)
                        turn(pair, u + 2)
                        project(pair, u, e)
                last_pair = TILES // 2 - 1
                up(last_pair, 1)
                for u in range(2):
                    project(last_pair, u, down(last_pair, u))

            @block.scalar
            def _(act):
                act.sem_inc(rows_t_ready, 1)
                act.sem_inc(hidden_t_ready, CREDIT)
                with act.Fori(0, CHUNKS) as q:
                    for t in range(HT):
                        act.wait_ge(s_gate_done, q * HT + t + 1)
                        act.wait_ge(s_hidden_ready, q * HT + t + 1)
                        nc.scalar.activation(s_gate[t % 2][:, :], g_bank[t % 2], ACT.Silu
                                             ).then_inc(s_gate_ready, 1)

                def copy_rows(pair, u):
                    k, i = pair * 2 + u, u % 2
                    act.wait_ge(rows_turned, k + 1 + CREDIT)
                    nc.scalar.activation(rows_t[i][:, :], t_bank[:, i * P:(i + 1) * P], ACT.Copy
                                         ).then_inc(rows_t_ready, 1)

                def gate_rows(pair, u):
                    k, i = pair * 2 + u, u % 2
                    act.wait_ge(gate_done, k + 1)
                    act.wait_ge(hidden_ready, k + 1)
                    nc.scalar.activation(gate[i][:, :], g_bank[i], ACT.Silu).then_inc(gate_ready, 1)

                def copy_hidden(pair, u):
                    k, i = pair * 2 + u, u % 2
                    act.wait_ge(hidden_turned, k + 1)
                    nc.scalar.activation(hidden_t[i][:, :, :].rearrange("p t c -> p (t c)"), turn_bank[i],
                                         ACT.Copy).then_inc(hidden_t_ready, 1)

                copy_rows(0, 0)
                gate_rows(0, 0)
                copy_rows(0, 1)
                with act.Fori(0, TILES // 2 - 1) as pair:
                    for u in range(2):
                        gate_rows(pair, u + 1)
                        copy_hidden(pair, u)
                        copy_rows(pair, u + 2)
                last_pair = TILES // 2 - 1
                gate_rows(last_pair, 1)
                for u in range(2):
                    copy_hidden(last_pair, u)
                for h in range(2):
                    act.wait_ge(fin_var, h + 1)
                    nc.scalar.activation(std[:, h * KT:(h + 1) * KT], var_eps[:, h * KT:(h + 1) * KT], ACT.Sqrt
                                         ).then_inc(fin_std, 1)

            @block.vector
            def _(dve):
                step = Count()
                dve.sem_inc(s_hidden_ready, CREDIT)
                dve.sem_inc(s_down_taken, 1)
                dve.sem_inc(hidden_ready, CREDIT)
                dve.sem_inc(result_ready, 1)
                with dve.Fori(0, CHUNKS) as q:
                    dve.wait_ge(s_down_done, q + 1)
                    for t in range(HT):
                        dve.wait_ge(s_gate_ready, q * HT + t + 1)
                        dve.wait_ge(s_up_done, q * HT + t + 1)
                        nc.vector.tensor_tensor(s_hidden[0][:, t, :], u_bank[t % 2], s_gate[t % 2][:, :],
                                                ALU.mult).then_inc(s_hidden_ready, 1)
                    dve.wait_ge(s_down_done, q + 2)
                    nc.vector.tensor_scalar(
                        mixed[:, bass.ds(q * CH, CH), :],
                        d_bank.rearrange("p (t c) -> p t c", c=C), 1.0, None, ALU.mult
                    ).then_inc(s_down_taken, 1)

                def multiply(pair, u):
                    k, i = pair * 2 + u, u % 2
                    dve.wait_ge(gate_ready, k + 1)
                    dve.wait_ge(up_done, k + 1)
                    nc.vector.tensor_tensor(hidden[i][:, :], u_bank[i], gate[i][:, :], ALU.mult
                                            ).then_inc(hidden_ready, 1)

                def take_result(pair, u):
                    k, i = pair * 2 + u, u % 2
                    dve.wait_ge(down_done, k + 1)
                    dve.wait_ge(result_stored[i], pair * 16 + 1)
                    nc.vector.tensor_copy(result[i][:, :], d_bank[:, 0:P]).then_inc(result_ready, 1)

                multiply(0, 0)
                with dve.Fori(0, TILES // 2 - 1) as pair:
                    for u in range(2):
                        multiply(pair, u + 1)
                        take_result(pair, u)
                last_pair = TILES // 2 - 1
                multiply(last_pair, 1)
                for u in range(2):
                    take_result(last_pair, u)

                for h in range(2):
                    for i in range(2):
                        for t in range(h * KT, (h + 1) * KT):
                            if i == 0:
                                dve.wait_ge(gathered[t], 32)
                            nc.vector.scalar_tensor_tensor(
                                mixed[:, t, :], back[i][:, t, :], weight[:, i, t:t + 1], mixed[:, t, :],
                                ALU.mult, ALU.add).then_inc(mix_steps, step.one())
                        dve.wait_ge(mix_steps, step.now())
                    for t in range(h * KT, (h + 1) * KT):
                        nc.vector.bn_stats(stats[:, t, :], mixed[:, t, :]).then_inc(mix_steps, step.one())
                    dve.wait_ge(mix_steps, step.now())
                    for t in range(h * KT, (h + 1) * KT):
                        nc.vector.bn_aggr(mean_var[:, t, :], stats[:, t, :]).then_inc(mix_steps, step.one())
                    dve.wait_ge(mix_steps, step.now())
                    part = slice(h * KT, (h + 1) * KT)
                    nc.vector.tensor_scalar(var_eps[:, part], mean_var[:, part, 1], EPS, None, ALU.add
                                            ).then_inc(fin_var, 1)
                    dve.wait_ge(fin_std, h + 1)
                    nc.vector.reciprocal(rstd[:, part], std[:, part]).then_inc(mix_steps, step.one())
                    dve.wait_ge(mix_steps, step.now())
                    for t in range(h * KT, (h + 1) * KT):
                        nc.vector.tensor_scalar(mixed[:, t, :], mixed[:, t, :], mean_var[:, t, 0:1],
                                                rstd[:, t:t + 1], ALU.subtract, ALU.mult
                                                ).then_inc(mix_steps, step.one())
                    dve.wait_ge(mix_steps, step.now())
                    nc.vector.tensor_tensor(mixed[:, part, :], mixed[:, part, :], x_sb[:, part, :], ALU.add
                                            ).then_inc(half_done, 1)


def kernel(**inputs):
    import concourse.bacc as bacc
    from concourse.bass_utils import run_bass_kernel_spmd

    a = {k: np.asarray(v) for k, v in inputs.items()}
    wqkv = a["L0_attn_w_qkv"]
    arrays = {
        "x": a["L0_attn_x"],
        "wqkv": wqkv,
        "wq_t": wqkv[:, :C].T,
        "dirs": a["L0_attn_head_dirs"].reshape(1, H * HD),
        "scales": a["L0_attn_head_scales"].reshape(1, H),
        "w_out": a["L0_attn_w_out"],
        "router_t": a["L0_ffn_router_w"].T,
        "w_gate": np.concatenate([a["L0_ffn_w_gate"], a["L0_ffn_sw_gate"]]),
        "w_up": np.concatenate([a["L0_ffn_w_up"], a["L0_ffn_sw_up"]]),
        "w_down": np.concatenate([a["L0_ffn_w_down"], a["L0_ffn_sw_down"]]),
    }
    arrays = {f"in_{k}": np.ascontiguousarray(v) for k, v in arrays.items()}
    nc = bacc.Bacc("TRN2", target_bir_lowering=False, num_devices=1)
    args = [nc.dram_tensor(k, v.shape, mybir.dt.from_np(v.dtype), kind="ExternalInput").ap()
            for k, v in arrays.items()]
    out = nc.dram_tensor("out", (B, T, C), F32, kind="ExternalOutput").ap()
    program(nc, *args, out)
    r = run_bass_kernel_spmd(nc, [arrays], core_ids=[0])
    return r.results[0]["out"]
```

```python
from contextlib import ExitStack

import numpy as np

import concourse.bass as bass
from concourse import mybir

F32 = mybir.dt.float32
BF16 = mybir.dt.bfloat16
U32 = mybir.dt.uint32
ALU = mybir.AluOpType
ACT = mybir.ActivationFunctionType
AX = mybir.AxisListType

B, T, C, H = 2, 1024, 128, 16
HD = C // H
SCALE = 1.0 / float(np.sqrt(HD))
P = 128
KT = T // P
NT = B * KT
HG = 4
NG = H // HG
GROUPS = B * NG
HQ = 32
COMBOS = ((0, 0), (0, 1), (0, 2), (1, 0), (1, 1), (2, 0))
KR = HD * len(COMBOS)
MR = KR + 3
BANK = 512
NEG = -3.0e38
ONES_BITS = float(np.array([0x3F803F80], np.uint32).view(np.float32)[0])
EPS = 1e-5
E, HID = 7, 512
NE = E + 1
HT = HID // P
TILES = (2 * B * T + E * (P - 1)) // P
TILES += TILES % 2
PACK = 6
WORDS = -(-TILES // PACK)
PADDED = (WORDS + 1) * PACK
TAIL = 2
assert (TILES - TAIL) % PACK == 0 and PACK % 2 == 0
CH = BANK // P
STACKS = 3
CREDIT = 2
BURST = 256
SKEW = 8
LOADS = 2 * len(COMBOS) + 1
KEPT = 5
RING = 3


EARLY = 1.5
LEAD = 1024


class Count:

    def __init__(self):
        self.base, self.n, self.outer = 0, 0, []

    def one(self):
        self.n += 1
        return 1

    def now(self):
        return self.base + self.n

    def enter(self, i, per_turn):
        self.outer.append((self.base, self.n, per_turn))
        self.base, self.n = self.base + self.n + i * per_turn, 0

    def leave(self, turns):
        base, n, per_turn = self.outer.pop()
        assert self.n == per_turn, (self.n, per_turn)
        self.base, self.n = base, n + per_turn * turns


def units():
    return [(j, h) for j in range(KT) for h in range(HG)]


def pieces(width):
    return [(a, min(a + BANK, width)) for a in range(0, width, BANK)]


def bursts(j):
    return [(max(j * P, a), a + BURST) for a in range(0, T, BURST) if a + BURST > j * P]


SCORE_WORK = [T - P * j + P + (4 * BURST if j > 0 and h < len(bursts(j - 1)) else 0) for j, h in units()]

PIECES_BEFORE = [0]
for _j, _h in units():
    PIECES_BEFORE.append(PIECES_BEFORE[-1] + len(pieces(T - P * _j)))
PIECES = PIECES_BEFORE[-1]
TURNED = ((0, 3), (3, 6), (6, 8))
SLOTS = PIECES + len(TURNED)
assert PIECES % RING == 0 and SLOTS % RING == 0


def program(nc, x, wqkv, wq_t, dirs, scales, w_out, router_t, w_gate, w_up, w_down, out):
    ctx = ExitStack()
    with ctx:
        def sb(name, shape, dt=F32):
            return ctx.enter_context(nc.sbuf_tensor(name, shape, dt))

        front = ctx.enter_context(ExitStack())

        def sb_front(name, shape, dt=F32):
            return front.enter_context(nc.sbuf_tensor(name, shape, dt))

        def sem(name):
            return ctx.enter_context(nc.semaphore(name))

        q_parts = nc.dram_tensor("q_parts", [3, GROUPS, HG * HD, T], BF16, kind="Internal").ap()
        k_parts = nc.dram_tensor("k_parts", [3, GROUPS, HG * HD, T], BF16, kind="Internal").ap()

        tokens = nc.dram_tensor("tokens", [B * T, C], F32, kind="Internal").ap()
        results = nc.dram_tensor("results", [2 * B * T + TILES * P, C], F32, kind="Internal").ap()

        x_sb = sb("x_sb", [P, NT, C])
        w_out_sb = sb("w_out_sb", [C, C])
        router_sb = sb("router_sb", [C, E])
        ident = sb("ident", [P, P])
        ident_b = sb("ident_b", [P, P], BF16)
        attn = sb("attn", [P, KT, (1 + GROUPS) * HG * HD])
        stats = sb("stats", [P, NT, 6])
        mean_var = sb("mean_var", [P, NT, 2])
        var_eps = sb("var_eps", [P, NT])
        std = sb("std", [P, NT])
        rstd = sb("rstd", [P, NT])

        xn_stage = sb_front("xn_stage", [P, 2, CH, C])
        xn_t = sb_front("xn_t", [C, 2, BANK])
        wqkv_sb = sb_front("wqkv_sb", [C, 3 * C])
        wq_t_sb = sb_front("wq_t_sb", [C, C])
        wq_fold = sb_front("wq_fold", [C, C])
        dirs_sb = sb_front("dirs_sb", [1, C])
        scales_sb = sb_front("scales_sb", [1, H])
        dirs_scaled = sb_front("dirs_scaled", [1, C])
        zeros = sb_front("zeros", [P, P])
        mask_qk = sb_front("mask_qk", [P, P], BF16)
        mask_kq = sb_front("mask_kq", [P, P], BF16)
        same_head = sb_front("same_head", [C, H, HD])
        fold = sb_front("fold", [C, C])
        parts = sb_front("parts", [C, 2, 2, 3, BANK], BF16)
        rest = sb_front("rest", [C, 2, 2, BANK])
        zero_rows = sb_front("zero_rows", [MR - KR, HG * T], BF16)
        v_all = sb_front("v_all", [P, GROUPS, KT, HG * HD])
        q_st = [sb_front(f"q_st{r}", [P, HG, T], BF16) for r in range(STACKS)]
        k_st = [sb_front(f"k_st{r}", [P, HG, T], BF16) for r in range(STACKS)]
        v_pad = [sb_front(f"v_pad{r}", [P, KT, HG, HQ]) for r in range(STACKS)]
        mx_part = [sb_front(f"mx_part{r}", [P, HG * KT, 2]) for r in range(STACKS)]
        mx = sb_front("mx", [P, HG * KT])
        mx_t = sb_front("mx_t", [P, HG * KT])
        mx_neg = sb_front("mx_neg", [P, HG * KT])
        mx_rest = sb_front("mx_rest", [P, HG * KT])
        mx_rows = [sb_front(f"mx_rows{r}", [P, 3, HG * KT], BF16) for r in range(STACKS)]
        probs = [sb_front(f"probs{i}", [P, HG, T]) for i in range(2)]
        o_cols = sb_front("o_cols", [P, T])
        o_raw = sb_front("o_raw", [P, 1 + GROUPS, KT * HG, HD + 1])
        den = sb_front("den", [P, KT * HG])

        banks = ctx.enter_context(nc.psum_tensor("banks", [P, 8 * BANK], F32))

        def bank(i, n=1):
            return banks[:, i * BANK:(i + n) * BANK]

        max_bank = [bank(i) for i in range(RING)]
        score_bank = [bank(RING + i) for i in range(RING)]
        o_bank = [bank(6), bank(7)]

        x_loaded = sem("x_loaded")
        weights_loaded = sem("weights_loaded")
        consts_ready = sem("consts_ready")
        pool_steps = sem("pool_steps")
        vector_steps = sem("vector_steps")
        scalar_steps = sem("scalar_steps")
        dirs_scaled_ready = sem("dirs_scaled_ready")
        outer_ready = sem("outer_ready")
        fold_ready = sem("fold_ready")
        wq_folded = sem("wq_folded")
        wq_fold_ready = sem("wq_fold_ready")
        var_ready = sem("var_ready")
        std_ready = sem("std_ready")
        xn_ready = sem("xn_ready")
        xn_transposed = sem("xn_transposed")
        xn_t_ready = sem("xn_t_ready")
        q_projected = sem("q_projected")
        k_projected = sem("k_projected")
        v_projected = sem("v_projected")
        high_ready = sem("high_ready")
        v_stored = sem("v_stored")
        parts_ready = sem("parts_ready")
        parts_stored = sem("parts_stored")
        stacks_padded = sem("stacks_padded")
        stacks_loaded = [sem(f"stacks_loaded{r}") for r in range(STACKS)]
        v_padded = sem("v_padded")
        max_filled = sem("max_filled")
        max_taken = sem("max_taken")
        rows_split = sem("rows_split")
        rows_ready = sem("rows_ready")
        slot_filled = sem("slot_filled")
        slot_taken = sem("slot_taken")
        pv_done = sem("pv_done")
        o_taken = sem("o_taken")

        block = front.enter_context(nc.Block())

        TURNS, PER_TURN = 2, STACKS

        @block.sync
        def _(sp):
            sp.sem_inc(parts_stored, 1)
            for b in range(B):
                sp.dma_start(x_sb[:, b * KT:(b + 1) * KT, :],
                             x[b].rearrange("(t p) c -> p t c", p=P)).then_inc(x_loaded, 16)
            for dst, src in ((dirs_sb[:, :], dirs), (scales_sb[:, :], scales), (wq_t_sb[:, :], wq_t),
                             (wqkv_sb[:, :], wqkv), (w_out_sb[:, :], w_out), (router_sb[:, :], router_t)):
                sp.dma_start(dst, src).then_inc(weights_loaded, 16)

            with sp.Fori(0, B) as b:
                for half in range(2):
                    sp.wait_ge(parts_ready, b * 2 + half + 1 + CREDIT)
                    for qk, dst in ((0, q_parts), (1, k_parts)):
                        for part in range(3):
                            sp.dma_start(
                                dst[part, bass.ds(b * NG, NG), :, half * BANK:(half + 1) * BANK]
                                .rearrange("g c t -> (g c) t"),
                                parts[:, half, qk, part, :]).then_inc(parts_stored, 16)

            def load_stacks(turn, u):
                n, r = turn * STACKS + u, u % STACKS
                for row, (pq, pk) in enumerate(COMBOS):
                    for dst, src, part in ((q_st[r], q_parts, pq), (k_st[r], k_parts, pk)):
                        sp.dma_start(dst[row * HD:(row + 1) * HD, :, :],
                                     src[part, bass.ds(n, 1), :, :].rearrange("g (h d) t -> d (g h) t", d=HD)
                                     ).then_inc(stacks_loaded[r], 16)
                sp.dma_start(q_st[r][KR:MR, :, :].rearrange("r h t -> r (h t)"), zero_rows[:, :]
                             ).then_inc(stacks_loaded[r], 16)

            def send_rows(n, r):
                sp.wait_ge(rows_split, n + 1)
                for part in range(3):
                    for b in range(4):
                        sp.dma_start(
                            q_st[r][KR + part:KR + part + 1, :, :].rearrange(
                                "o h (i b c) -> o b (h i) c", i=KT, c=32)[:, b, :, :],
                            mx_rows[r][b * 32:(b + 1) * 32, part, :]).then_inc(rows_ready, 16)

            sp.wait_ge(consts_ready, 1)
            sp.wait_ge(stacks_padded, 2 * STACKS)
            sp.wait_ge(parts_stored, 16 * 6 * 4 + 1)
            load_stacks(0, 0)
            load_stacks(0, 1)
            send_rows(0, 0)
            with sp.Fori(0, TURNS) as turn:
                for u in range(PER_TURN):
                    n = turn * PER_TURN + u
                    sp.wait_ge(pv_done, n * KT + CREDIT)
                    load_stacks(turn, u + 2)
                    send_rows(n + 1, (u + 1) % STACKS)
            send_rows(GROUPS - 1, (GROUPS - 1) % STACKS)

        @block.gpsimd
        def _(pool):
            nc.gpsimd.memset(zeros[:, :], 0.0).then_inc(pool_steps, 1)
            nc.gpsimd.memset(same_head[:, :, :], 1.0).then_inc(pool_steps, 1)
            pool.wait_ge(pool_steps, 2)
            nc.gpsimd.affine_select(out=ident[:, :], in_=zeros[:, :], compare_op=ALU.not_equal, fill=1.0,
                                    base=0, pattern=[[-1, P]], channel_multiplier=1).then_inc(pool_steps, 1)
            nc.gpsimd.affine_select(out=ident_b[:, :], in_=zeros[:, :], compare_op=ALU.not_equal, fill=1.0,
                                    base=0, pattern=[[-1, P]], channel_multiplier=1).then_inc(pool_steps, 1)
            nc.gpsimd.affine_select(out=mask_qk[:, :], in_=zeros[:, :], compare_op=ALU.is_ge, fill=NEG,
                                    base=0, pattern=[[-1, P]], channel_multiplier=1).then_inc(pool_steps, 1)
            nc.gpsimd.affine_select(out=mask_kq[:, :], in_=zeros[:, :], compare_op=ALU.is_ge, fill=NEG,
                                    base=0, pattern=[[1, P]], channel_multiplier=-1).then_inc(pool_steps, 1)
            nc.gpsimd.affine_select(out=same_head[:, :, :], in_=same_head[:, :, :], compare_op=ALU.is_ge,
                                    fill=0.0, base=0, pattern=[[-HD, H], [0, HD]],
                                    channel_multiplier=1).then_inc(pool_steps, 1)
            pool.wait_ge(pool_steps, 7)
            nc.gpsimd.affine_select(out=same_head[:, :, :], in_=same_head[:, :, :], compare_op=ALU.is_ge,
                                    fill=0.0, base=HD - 1, pattern=[[HD, H], [0, HD]],
                                    channel_multiplier=-1).then_inc(pool_steps, 1)
            pool.wait_ge(pool_steps, 8)
            nc.gpsimd.memset(zero_rows[:, :], 0.0).then_inc(pool_steps, 1)
            for r in range(STACKS):
                nc.gpsimd.memset(v_pad[r][:, :, :, :], 0.0).then_inc(pool_steps, 1)
                nc.gpsimd.memset(mx_part[r][:, :, :], NEG).then_inc(pool_steps, 1)
            pool.wait_ge(pool_steps, 9 + 2 * STACKS)
            for r in range(STACKS):
                nc.gpsimd.memset(v_pad[r][:, :, :, HD:HD + 1], 1.0).then_inc(pool_steps, 1)
            pool.wait_ge(pool_steps, 9 + 3 * STACKS)
            nc.gpsimd.memset(zeros[:, 0:1], 0.0).then_inc(consts_ready, 1)

            for r in range(STACKS):
                nc.gpsimd.memset(q_st[r][:, :, :].bitcast(F32), 0.0).then_inc(stacks_padded, 1)
                nc.gpsimd.memset(k_st[r][:, :, :].bitcast(F32), ONES_BITS).then_inc(stacks_padded, 1)

            def pad_v(n, r):
                nc.gpsimd.tensor_copy(
                    v_pad[r][:, :, :, 0:HD],
                    v_all[:, bass.ds(n, 1), :, :].rearrange("p g k (h d) -> p (g k) h d", d=HD)
                ).then_inc(v_padded, 1)

            pool.wait_ge(v_stored, 4 + CREDIT)
            pad_v(0, 0)
            pad_v(1, 1)
            with pool.Fori(0, TURNS) as turn:
                for u in range(PER_TURN):
                    n = turn * PER_TURN + u
                    pool.wait_ge(pv_done, n * KT + CREDIT)
                    pad_v(n + 2, (u + 2) % STACKS)

        @block.tensor
        def _(pe):
            pe.sem_inc(pv_done, CREDIT)
            pe.sem_inc(xn_transposed, CREDIT)
            pe.wait_ge(weights_loaded, 16 * 6)
            pe.wait_ge(dirs_scaled_ready, 1)
            nc.tensor.matmul(bank(0)[:, 0:C], dirs_sb[:, :], dirs_scaled[:, :], start=True, stop=True
                             ).then_inc(outer_ready, 1)
            pe.wait_ge(fold_ready, 1)
            nc.tensor.matmul(bank(1)[:, 0:C], wq_t_sb[:, :], fold[:, :], start=True, stop=True
                             ).then_inc(wq_folded, 1)
            pe.wait_ge(wq_fold_ready, 1)
            pe.wait_ge(consts_ready, 1)
            with pe.Fori(0, B) as b:
                for half in range(2):
                    done = b * 2 + half
                    bt, bq, bk, bv = (bank(4 * half + i) for i in range(4))
                    pe.wait_ge(xn_ready, done + 1)
                    pe.wait_ge(xn_t_ready, done + 1)
                    for j in range(CH):
                        last = nc.tensor.transpose(bt[:, j * P:(j + 1) * P], xn_stage[:, half, j, :],
                                                   ident[:, :])
                    last.then_inc(xn_transposed, 1)
                for half in range(2):
                    done = b * 2 + half
                    bt, bq, bk, bv = (bank(4 * half + i) for i in range(4))
                    pe.wait_ge(xn_t_ready, done + 1 + CREDIT)
                    pe.wait_ge(parts_ready, done + 1)
                    nc.tensor.matmul(bq, wq_fold[:, :], xn_t[:, half, :], start=True, stop=True
                                     ).then_inc(q_projected, 1)
                    nc.tensor.matmul(bk, wqkv_sb[:, C:2 * C], xn_t[:, half, :], start=True, stop=True
                                     ).then_inc(k_projected, 1)
                    pe.wait_ge(v_stored, done + 1)
                    for j in range(CH):
                        last = nc.tensor.matmul(bv[:, j * P:(j + 1) * P],
                                                xn_t[:, half, j * P:(j + 1) * P],
                                                wqkv_sb[:, 2 * C:3 * C], start=True, stop=True)
                    last.then_inc(v_projected, 1)

            def max_unit(turn, u, idx):
                m, r = turn * STACKS + u, u % STACKS
                j, h = units()[idx]
                i = KT - 1 - j
                width = T - P * j
                if idx == 0:
                    pe.wait_ge(stacks_loaded[r], (turn + (u // STACKS + 1)) * (16 * LOADS))
                for piece, (a, z) in enumerate(pieces(width)):
                    k = PIECES_BEFORE[idx] + piece
                    dst = max_bank[k % RING]
                    pe.wait_ge(max_taken, m * PIECES + k + 1)
                    last = nc.tensor.matmul(dst[:, 0:z - a], q_st[r][:, h, i * P:(i + 1) * P],
                                            k_st[r][:, h, a:z], start=True, stop=(z < width))
                    if z == width:
                        last = nc.tensor.matmul(dst[:, z - a - P:z - a], ident_b[:, :], mask_qk[:, :],
                                                start=False, stop=True)
                    last.then_inc(max_filled, 1)
                    yield

            def score_unit(n, r, idx):
                j, h = units()[idx]
                for piece, (a, z) in enumerate(pieces(T - P * j)):
                    k = PIECES_BEFORE[idx] + piece
                    dst = score_bank[k % RING]
                    pe.wait_ge(slot_taken, n * SLOTS + k + 1)
                    last = nc.tensor.matmul(dst[:, 0:z - a], k_st[r][:, h, j * P:(j + 1) * P],
                                            q_st[r][:, h, j * P + a:j * P + z],
                                            start=True, stop=(a > 0))
                    if a == 0:
                        last = nc.tensor.matmul(dst[:, 0:P], ident_b[:, :], mask_kq[:, :],
                                                start=False, stop=True)
                    last.then_inc(slot_filled, 1)
                    yield

            def weighted_values(n, r, j, which):
                for k in which:
                    if k >= len(bursts(j)):
                        continue
                    a, z = bursts(j)[k]
                    if k == 0:
                        pe.wait_ge(slot_taken, n * SLOTS + PIECES_BEFORE[HG * (j + 1)] + RING)
                    if j == 0 and k == 0:
                        pe.wait_ge(o_taken, n * 2 + 1)
                        pe.wait_ge(v_padded, n + 1)
                    c = a // BANK
                    for h in range(HG):
                        last = nc.tensor.matmul(
                            o_bank[c][h * HQ:(h + 1) * HQ, a - c * BANK:z - c * BANK],
                            v_pad[r][:, j, h, :], probs[j % 2][:, h, a - j * P:z - j * P],
                            start=(j == 0 and a % BANK == 0), stop=(j == (c + 1) * CH - 1),
                            skip_group_check=True)
                    if k == len(bursts(j)) - 1:
                        last.then_inc(pv_done, 1)

            def group(turn, u, ahead):
                n, r = turn * STACKS + u, u % STACKS
                pe.wait_ge(rows_ready, (n + 1) * (16 * 12))
                todo = [(turn, u + 1, i) for i in range(SKEW, KT * HG)] if ahead > 0 else []
                if ahead > 1:
                    todo += [(turn, u + 2, i) for i in range(SKEW)]
                sizes = [z - a for _, _, i in todo for a, z in pieces(T - P * units()[i][0])]
                kept = KEPT if ahead > 1 else 0
                share = sum(sizes) / sum(SCORE_WORK) * (1.0 if ahead > 1 else EARLY)
                stream = (None for unit in todo for _ in max_unit(*unit))
                work, given = 0, 0
                for idx in range(KT * HG):
                    unit = score_unit(n, r, idx)
                    for part in range(len(pieces(T - P * units()[idx][0]))):
                        next(unit)
                        work += SCORE_WORK[idx] / len(pieces(T - P * units()[idx][0]))
                        if given < len(sizes) - kept and sum(sizes[:given + 1]) <= work * share + LEAD:
                            next(stream)
                            given += 1
                    if idx >= HG:
                        weighted_values(n, r, idx // HG - 1, [idx % HG])
                    while given < len(sizes) - kept and sum(sizes[:given + 1]) <= work * share + LEAD:
                        next(stream)
                        given += 1
                weighted_values(n, r, KT - 1, range(HG))
                for _ in sizes[given:len(sizes) - len(TURNED)]:
                    next(stream)
                pe.wait_ge(o_taken, n * 2 + 3)
                for s, (t0, t1) in enumerate(TURNED):
                    next(stream, None)
                    dst = score_bank[(PIECES + s) % RING]
                    pe.wait_ge(slot_taken, n * SLOTS + PIECES + s + 1)
                    for t in range(t0, t1):
                        last = nc.tensor.transpose(dst[:, (t - t0) * P:(t - t0 + 1) * P],
                                                   o_cols[:, t * P:(t + 1) * P], ident[:, :])
                    last.then_inc(slot_filled, 1)
                for _ in stream:
                    pass

            pe.wait_ge(parts_ready, 4 + CREDIT)
            pe.wait_ge(v_stored, 4 + CREDIT)
            for u, idx in [(0, i) for i in range(KT * HG)] + [(1, i) for i in range(SKEW)]:
                for _ in max_unit(0, u, idx):
                    pass
            with pe.Fori(0, TURNS) as turn:
                for u in range(PER_TURN):
                    group(turn, u, 2)
            group(TURNS, 0, 1)
            group(TURNS, 1, 0)

        @block.scalar
        def _(act):
            act.sem_inc(xn_t_ready, CREDIT)
            act.sem_inc(v_stored, CREDIT)
            act.sem_inc(o_taken, 1)
            act.sem_inc(slot_taken, RING)
            act.wait_ge(var_ready, 1)
            nc.scalar.activation(std[:, :], var_eps[:, :], ACT.Sqrt).then_inc(std_ready, 1)
            with act.Fori(0, B) as b:
                act.wait_ge(parts_stored, b * (16 * 6 * 2) + 1)
                for half in range(2):
                    act.wait_ge(xn_transposed, b * 2 + half + 1 + CREDIT)
                    nc.scalar.activation(xn_t[:, half, :], bank(4 * half), ACT.Copy).then_inc(xn_t_ready, 1)
                for half in range(2):
                    bt, bq, bk, bv = (bank(4 * half + i) for i in range(4))
                    act.wait_ge(q_projected, b * 2 + half + 1)
                    nc.scalar.activation(parts[:, half, 0, 0, :], bq, ACT.Copy).then_inc(high_ready, 1)
                    act.wait_ge(k_projected, b * 2 + half + 1)
                    nc.scalar.activation(parts[:, half, 1, 0, :], bk, ACT.Copy).then_inc(high_ready, 1)
                    act.wait_ge(v_projected, b * 2 + half + 1)
                    for j in range(CH):
                        last = nc.scalar.activation(
                            v_all[:, bass.ds(b * NG, NG), half * CH + j, :],
                            bv[:, j * P:(j + 1) * P].rearrange("p (g c) -> p g c", g=NG), ACT.Copy)
                    last.then_inc(v_stored, 1)

            def group(n):
                for idx, (j, h) in enumerate(units()):
                    if h == 0:
                        act.wait_ge(pv_done, n * KT + j + 1)
                    for piece, (a, z) in enumerate(pieces(T - P * j)):
                        k = PIECES_BEFORE[idx] + piece
                        act.wait_ge(slot_filled, n * SLOTS + k + 1)
                        nc.scalar.activation(probs[j % 2][:, h, a:z], score_bank[k % RING][:, 0:z - a],
                                             ACT.Exp).then_inc(slot_taken, 1)
                act.wait_ge(pv_done, n * KT + KT + CREDIT)
                for c in range(2):
                    nc.scalar.activation(o_cols[:, c * BANK:(c + 1) * BANK], o_bank[c], ACT.Copy
                                         ).then_inc(o_taken, 1)
                for s, (t0, t1) in enumerate(TURNED):
                    act.wait_ge(slot_filled, n * SLOTS + PIECES + s + 1)
                    nc.scalar.activation(
                        o_raw[:, bass.ds(n + 1, 1), t0 * HG:t1 * HG, :].rearrange("p g j d -> p (g j) d"),
                        score_bank[(PIECES + s) % RING][:, 0:(t1 - t0) * P].rearrange(
                            "p (j d) -> p j d", d=HQ)[:, :, 0:HD + 1],
                        ACT.Copy).then_inc(slot_taken, 1)

            with act.Fori(0, TURNS) as turn:
                for u in range(PER_TURN):
                    group(turn * PER_TURN + u)
            group(GROUPS - 2)
            group(GROUPS - 1)

        @block.vector
        def _(dve):
            step = Count()
            dve.sem_inc(parts_ready, CREDIT)
            dve.sem_inc(max_taken, RING)
            dve.wait_ge(weights_loaded, 16 * 6)
            nc.vector.tensor_tensor(dirs_scaled[:, :].rearrange("o (h d) -> o h d", d=HD),
                                    dirs_sb[:, :].rearrange("o (h d) -> o h d", d=HD),
                                    scales_sb[:, :].unsqueeze(2).broadcast_to([1, H, HD]),
                                    ALU.mult).then_inc(dirs_scaled_ready, 1)
            dve.wait_ge(x_loaded, 32)
            for t in range(NT):
                nc.vector.bn_stats(stats[:, t, :], x_sb[:, t, :]).then_inc(vector_steps, step.one())
            dve.wait_ge(vector_steps, step.now())
            for t in range(NT):
                nc.vector.bn_aggr(mean_var[:, t, :], stats[:, t, :]).then_inc(vector_steps, step.one())
            dve.wait_ge(vector_steps, step.now())
            nc.vector.tensor_scalar(var_eps[:, :], mean_var[:, :, 1], EPS, None, ALU.add
                                    ).then_inc(var_ready, 1)
            dve.wait_ge(outer_ready, 1)
            dve.wait_ge(consts_ready, 1)
            nc.vector.tensor_tensor(fold[:, :], bank(0)[:, 0:C],
                                    same_head[:, :, :].rearrange("p h d -> p (h d)"), ALU.mult
                                    ).then_inc(vector_steps, step.one())
            dve.wait_ge(vector_steps, step.now())
            nc.vector.scalar_tensor_tensor(fold[:, :], ident[:, :], SCALE, fold[:, :], ALU.mult, ALU.add
                                           ).then_inc(fold_ready, 1)
            dve.wait_ge(wq_folded, 1)
            nc.vector.tensor_copy(wq_fold[:, :], bank(1)[:, 0:C]).then_inc(wq_fold_ready, 1)
            dve.wait_ge(std_ready, 1)
            nc.vector.reciprocal(rstd[:, :], std[:, :]).then_inc(vector_steps, step.one())
            dve.wait_ge(vector_steps, step.now())
            with dve.Fori(0, B) as b:
                step.enter(b, 8)
                for half in range(2):
                    dve.wait_ge(xn_transposed, b * 2 + half + 1)
                    for j in range(CH):
                        t = b * KT + half * CH + j
                        last = nc.vector.tensor_scalar(
                            xn_stage[:, half, j, :],
                            x_sb[:, bass.ds(t, 1), :].rearrange("p t c -> p (t c)"),
                            mean_var[:, bass.ds(t, 1), 0], rstd[:, bass.ds(t, 1)],
                            ALU.subtract, ALU.mult)
                    last.then_inc(xn_ready, 1)
                for half in range(2):
                    for qk in range(2):
                        src = bank(4 * half + 1 + qk)
                        high, mid, low = (parts[:, half, qk, i, :] for i in range(3))
                        left = rest[:, half, qk, :]
                        dve.wait_ge(high_ready, b * 4 + half * 2 + qk + 1)
                        nc.vector.tensor_tensor(left, src, high, ALU.subtract
                                                ).then_inc(vector_steps, step.one())
                        dve.wait_ge(vector_steps, step.now())
                        nc.vector.tensor_copy(mid, left).then_inc(vector_steps, step.one())
                        dve.wait_ge(vector_steps, step.now())
                        last = nc.vector.tensor_tensor(low, left, mid, ALU.subtract)
                    last.then_inc(parts_ready, 1)
                step.leave(B)

            def max_unit(m, r, idx):
                j, h = units()[idx]
                i = KT - 1 - j
                for s, (a, z) in enumerate(pieces(T - P * j)):
                    k = PIECES_BEFORE[idx] + s
                    dve.wait_ge(max_filled, m * PIECES + k + 1)
                    nc.vector.tensor_reduce(mx_part[r][:, h * KT + i, s:s + 1], max_bank[k % RING][:, 0:z - a],
                                            AX.X, ALU.max).then_inc(max_taken, 1)

            def split_maxima(m, r):
                dve.wait_ge(max_taken, m * PIECES + PIECES + RING)
                nc.vector.tensor_reduce(mx[:, :], mx_part[r][:, :, :], AX.X, ALU.max
                                        ).then_inc(vector_steps, step.one())
                dve.wait_ge(vector_steps, step.now())
                nc.vector.transpose(mx_t[:, :], mx[:, :]).then_inc(vector_steps, step.one())
                dve.wait_ge(vector_steps, step.now())
                nc.vector.tensor_scalar(mx_neg[:, :], mx_t[:, :], -1.0, None, ALU.mult
                                        ).then_inc(vector_steps, step.one())
                dve.wait_ge(vector_steps, step.now())
                nc.vector.tensor_copy(mx_rows[r][:, 0, :], mx_neg[:, :]).then_inc(vector_steps, step.one())
                dve.wait_ge(vector_steps, step.now())
                nc.vector.tensor_tensor(mx_rest[:, :], mx_neg[:, :], mx_rows[r][:, 0, :], ALU.subtract
                                        ).then_inc(vector_steps, step.one())
                dve.wait_ge(vector_steps, step.now())
                nc.vector.tensor_copy(mx_rows[r][:, 1, :], mx_rest[:, :]).then_inc(vector_steps, step.one())
                dve.wait_ge(vector_steps, step.now())
                nc.vector.tensor_tensor(mx_rows[r][:, 2, :], mx_rest[:, :], mx_rows[r][:, 1, :], ALU.subtract
                                        ).then_inc(rows_split, 1)

            def normalise(slot):
                raw = o_raw[:, bass.ds(slot, 1), :, :].rearrange("p g j d -> p (g j) d")
                dve.wait_ge(vector_steps, step.now())
                dve.wait_ge(slot_taken, slot * SLOTS + RING)
                nc.vector.reciprocal(den[:, :], raw[:, :, HD]).then_inc(vector_steps, step.one())
                dve.wait_ge(vector_steps, step.now())
                nc.vector.tensor_tensor(
                    attn[:, :, bass.ds(slot * (HG * HD), HG * HD)].rearrange("p t (h d) -> p t h d", d=HD),
                    raw[:, :, 0:HD].rearrange("p (t h) d -> p t h d", h=HG),
                    den[:, :].rearrange("p (t h) -> p t h", h=HG).unsqueeze(3).broadcast_to([P, KT, HG, HD]),
                    ALU.mult
                ).then_inc(vector_steps, step.one())

            nc.vector.memset(o_raw[:, 0, :, :], 1.0).then_inc(vector_steps, step.one())
            for idx in range(KT * HG):
                max_unit(0, 0, idx)
            split_maxima(0, 0)
            for idx in range(SKEW):
                max_unit(1, 1, idx)
            with dve.Fori(0, TURNS) as turn:
                step.enter(turn, 8 * PER_TURN)
                for u in range(PER_TURN):
                    n = turn * PER_TURN + u
                    for idx in range(SKEW, KT * HG):
                        if idx == SKEW + HG:
                            normalise(n)
                        max_unit(n + 1, (u + 1) % STACKS, idx)
                    split_maxima(n + 1, (u + 1) % STACKS)
                    for idx in range(SKEW):
                        max_unit(n + 2, (u + 2) % STACKS, idx)
                step.leave(TURNS)
            for idx in range(SKEW, KT * HG):
                if idx == SKEW + HG:
                    normalise(GROUPS - 2)
                max_unit(GROUPS - 1, (GROUPS - 1) % STACKS, idx)
            split_maxima(GROUPS - 1, (GROUPS - 1) % STACKS)
            normalise(GROUPS - 1)
            normalise(GROUPS)

        front.close()
        w_g = sb("w_g", [C, NE, HID])
        w_u = sb("w_u", [C, NE, HID])
        w_d = sb("w_d", [P, NE, HT, C])
        proj = sb("proj", [P, NT, C])
        attn_t = sb("attn_t", [C, 2, BANK])
        x2 = sb("x2", [P, NT, C])
        x2_t = sb("x2_t", [C, NT, P])
        mixed = sb("mixed", [P, NT, C])
        weight = sb("weight", [P, 2, NT])
        upper = sb("upper", [P, P], BF16)
        ones_b = sb("ones_b", [P, P], BF16)
        zeros2 = sb("zeros2", [P, P])
        logits = sb("logits", [P, NT, 8])
        top = sb("top", [P, NT, 8])
        top_at = sb("top_at", [P, NT, 8], U32)
        iota = sb("iota", [P, P])
        iota_p = sb("iota_p", [P, 1])
        iota_ct = sb("iota_ct", [P, 2 * NT])
        spare_at = sb("spare_at", [P, TILES])
        thresholds = sb("thresholds", [P, NT])
        top_at_f = sb("top_at_f", [P, NT, 2])
        gap = sb("gap", [P, NT])
        gap_exp = sb("gap_exp", [P, NT])
        gap_sum = sb("gap_sum", [P, NT])
        pick = [sb(f"pick{i}", [P, E, NT]) for i in range(2)]
        picked = sb("picked", [P, E, NT], BF16)
        before = [sb(f"before{i}", [P, E, KT + NT]) for i in range(2)]
        over = sb("over", [P, E, NT])
        ends = [sb(f"ends{i}", [P, 4 + E]) for i in range(2)]
        slot_in = sb("slot_in", [P, E, NT])
        slot_all = sb("slot_all", [P, E, NT])
        slot_pick = [sb(f"slot_pick{i}", [P, E, NT]) for i in range(2)]
        slot_f = sb("slot_f", [P, 2, NT])
        slot_u = sb("slot_u", [P, 2 * NT], U32)
        slot_part = sb("slot_part", [P, 2, 2 * NT], U32)
        slot_part_f = sb("slot_part_f", [P, 2, 2 * NT])
        row_hot = sb("row_hot", [P, 2 * NT, P], BF16)
        tile_hot = sb("tile_hot", [P, 2 * NT, 3, TILES], BF16)
        table = sb("table", [P, 3, TILES])
        spare = sb("spare", [P, TILES])
        place_f = sb("place_f", [P, TILES])
        place_u = sb("place_u", [P, TILES], U32)
        source = sb("source", [P, TILES], U32)
        target = sb("target", [P, TILES], U32)
        passed = sb("passed", [1, PADDED, E])
        tile_f = sb("tile_f", [1, PADDED])
        words_f = sb("words_f", [1, WORDS])
        words = sb("words", [1, WORDS], U32)
        s_gate = [sb(f"s_gate{i}", [P, BANK]) for i in range(2)]
        s_up = [sb(f"s_up{i}", [P, BANK]) for i in range(2)]
        s_hidden = [sb(f"s_hidden{i}", [P, HT, BANK]) for i in range(2)]
        source_now = [sb(f"source_now{i}", [P, 1], U32) for i in range(2)]
        target_now = [sb(f"target_now{i}", [P, 1], U32) for i in range(2)]
        rows = [sb(f"rows{i}", [P, C]) for i in range(2)]
        rows_t = [sb(f"rows_t{i}", [C, P]) for i in range(2)]
        gate = [sb(f"gate{i}", [P, HID]) for i in range(2)]
        hidden = [sb(f"hidden{i}", [P, HID]) for i in range(2)]
        hidden_t = [sb(f"hidden_t{i}", [P, HT, P]) for i in range(2)]
        result = [sb(f"result{i}", [P, C]) for i in range(2)]
        back = [sb(f"back{i}", [P, NT, C]) for i in range(2)]

        route_consts = sem("route_consts")
        shared_loaded = sem("shared_loaded")
        experts_loaded = sem("experts_loaded")
        attn_transposed = sem("attn_transposed")
        attn_t_ready = sem("attn_t_ready")
        projected = sem("projected")
        proj_ready = sem("proj_ready")
        post_var_ready = sem("post_var_ready")
        post_std_ready = sem("post_std_ready")
        x2_ready = sem("x2_ready")
        x2_transposed = sem("x2_transposed")
        x2_t_ready = sem("x2_t_ready")
        tokens_stored = sem("tokens_stored")
        logits_done = sem("logits_done")
        gap_ready = sem("gap_ready")
        gap_exp_ready = sem("gap_exp_ready")
        picked_ready = sem("picked_ready")
        counted = sem("counted")
        hot_ready = sem("hot_ready")
        table_done = sem("table_done")
        places_ready = sem("places_ready")
        words_ready = sem("words_ready")
        steps = sem("steps")
        s_gate_done = sem("s_gate_done")
        s_up_done = sem("s_up_done")
        s_gate_ready = sem("s_gate_ready")
        s_up_ready = sem("s_up_ready")
        s_hidden_ready = sem("s_hidden_ready")
        s_down_done = sem("s_down_done")
        s_down_taken = sem("s_down_taken")
        rows_loaded = [sem(f"rows_loaded{i}") for i in range(2)]
        copied = sem("copied")
        offsets_in_place = sem("offsets_in_place")
        rows_turned = sem("rows_turned")
        rows_t_ready = sem("rows_t_ready")
        gate_done = sem("gate_done")
        up_done = sem("up_done")
        gate_ready = sem("gate_ready")
        hidden_ready = sem("hidden_ready")
        hidden_turned = sem("hidden_turned")
        hidden_t_ready = sem("hidden_t_ready")
        down_done = sem("down_done")
        result_ready = sem("result_ready")
        result_stored = [sem(f"result_stored{i}") for i in range(2)]
        returned = [sem(f"returned{h}") for h in range(B)]
        fin_var = sem("fin_var")
        fin_std = sem("fin_std")
        half_done = sem("half_done")
        out_stored = sem("out_stored")
        CHUNKS = NT // CH
        QC = KT // CH
        PAIRS = (TILES - TAIL) // 2
        LAST = TILES - TAIL

        with nc.Block() as block:
            at_bank, pr_bank = [bank(0), bank(1)], [bank(2), bank(3)]
            g_bank, u_bank = [bank(0), bank(1)], [bank(2), bank(3)]
            xt_bank = turn_bank = [bank(4), bank(5)]
            d_bank, t_bank = bank(6), bank(7)
            cut = NT * 8
            lg_bank, t_out = t_bank[:, 0:cut], t_bank[:, 2 * P:2 * P + 3 * TILES]
            total_bank = t_bank[:, cut:cut + E * NT]
            rank_bank = t_bank[:, 2 * P + 3 * TILES:2 * P + 3 * TILES + E * NT]

            @block.sync
            def _(sp):
                for e in [E] + list(range(E)):
                    loaded = shared_loaded if e == E else experts_loaded
                    sp.dma_start(w_g[:, e, :], w_gate[e]).then_inc(loaded, 16)
                    sp.dma_start(w_u[:, e, :], w_up[e]).then_inc(loaded, 16)
                    sp.dma_start(w_d[:, e, :, :], w_down[e].rearrange("(t p) c -> p t c", p=P)
                                 ).then_inc(loaded, 16)
                for b in range(B):
                    sp.wait_ge(x2_ready, (b + 1) * QC)
                    sp.dma_start(tokens[b * T:(b + 1) * T, :].rearrange("(t p) c -> p t c", p=P),
                                 x2[:, b * KT:(b + 1) * KT, :]).then_inc(tokens_stored, 16)
                for i in range(2):
                    sp.wait_ge(result_stored[i], 16 * (TILES // 2))
                for b in range(B):
                    for i in range(2):
                        at = i * B * T + b * T
                        sp.dma_start(back[i][:, b * KT:(b + 1) * KT, :],
                                     results[at:at + T, :].rearrange("(t p) c -> p t c", p=P)
                                     ).then_inc(returned[b], 16)
                for b in range(B):
                    sp.wait_ge(half_done, b + 1)
                    sp.dma_start(out[b].rearrange("(t p) c -> p t c", p=P),
                                 mixed[:, b * KT:(b + 1) * KT, :]).then_inc(out_stored, 16)
                sp.wait_ge(out_stored, 16 * B)

            @block.gpsimd
            def _(pool):
                for dst, pattern, base, down in ((iota[:, :], [[1, P]], 0, 0), (iota_p[:, :], [[0, 1]], 0, 1),
                                                 (iota_ct[:, :], [[1, 2 * NT]], 0, 0),
                                                 (spare_at[:, :], [[P, TILES]], 2 * B * T, 1),
                                                 (thresholds[:, :], [[P, NT]], 0, 0)):
                    nc.gpsimd.iota(dst, pattern=pattern, base=base, channel_multiplier=down,
                                   allow_small_or_imprecise_dtypes=True).then_inc(route_consts, 1)
                nc.gpsimd.memset(zeros2[:, :], 0.0).then_inc(route_consts, 1)
                nc.gpsimd.memset(ones_b[:, :], 1.0).then_inc(route_consts, 1)
                pool.wait_ge(route_consts, 7)
                nc.gpsimd.affine_select(out=upper[:, :], in_=zeros2[:, :], compare_op=ALU.is_ge, fill=1.0,
                                        base=0, pattern=[[-1, P]], channel_multiplier=1
                                        ).then_inc(route_consts, 1)
                with pool.Fori(0, CHUNKS // 2) as pair:
                    for u in range(2):
                        q = pair * 2 + u
                        pool.wait_ge(s_down_done, q + 1)
                        for t in range(HT):
                            pool.wait_ge(s_up_ready, q * HT + t + 1)
                            nc.gpsimd.tensor_tensor(s_hidden[u][:, t, :], s_up[t % 2][:, :],
                                                    s_gate[t % 2][:, :], ALU.mult
                                                    ).then_inc(s_hidden_ready, 1)

                def gather(pair, u, count):
                    k, i = pair * 2 + u, u % 2
                    pool.wait_ge(rows_turned, k + 1)
                    nc.gpsimd.tensor_copy(source_now[i][:, :], source[:, bass.ds(k, 1)]).then_inc(copied, 1)
                    pool.wait_ge(copied, count)
                    pool.sem_inc(offsets_in_place, 1)
                    nc.gpsimd.indirect_dma_start(
                        rows[i][:, :], None, tokens,
                        bass.IndirectOffsetOnAxis(ap=source_now[i][:, 0:1], axis=0)
                    ).then_inc(rows_loaded[i], 16)

                def scatter(pair, u, count):
                    k, i = pair * 2 + u, u % 2
                    pool.wait_ge(result_ready, k + 1 + 1)
                    nc.gpsimd.tensor_copy(target_now[i][:, :], target[:, bass.ds(k, 1)]).then_inc(copied, 1)
                    pool.wait_ge(copied, count)
                    pool.sem_inc(offsets_in_place, 1)
                    nc.gpsimd.indirect_dma_start(
                        results, bass.IndirectOffsetOnAxis(ap=target_now[i][:, 0:1], axis=0),
                        result[i][:, :], None).then_inc(result_stored[i], 16)

                pool.wait_ge(tokens_stored, 16 * B)
                pool.wait_ge(places_ready, 2)
                AHEAD = 4
                for u in range(AHEAD):
                    gather(0, u, u + 1)
                with pool.Fori(0, PAIRS - 1) as pair:
                    for u in range(2):
                        gather(pair, u + AHEAD, pair * 4 + (AHEAD + 2 * u + 1))
                        scatter(pair, u, pair * 4 + (AHEAD + 2 * u + 2))
                for u in range(AHEAD):
                    scatter(PAIRS - 1, u, (PAIRS - 1) * 4 + AHEAD + u + 1)

            @block.tensor
            def _(pe):
                pe.sem_inc(s_down_done, 2)
                pe.sem_inc(rows_turned, CREDIT)
                for b in range(B):
                    for half in range(2):
                        pe.wait_ge(attn_t_ready, b * 2 + half + 1)
                        for j in range(CH):
                            first = HG * HD + b * C
                            last = nc.tensor.transpose(at_bank[half][:, j * P:(j + 1) * P],
                                                       attn[:, half * CH + j, first:first + C], ident[:, :])
                        last.then_inc(attn_transposed, 1)
                    for half in range(2):
                        pe.wait_ge(attn_t_ready, b * 2 + half + 1 + CREDIT)
                        pe.wait_ge(proj_ready, b * 2 + half + 1)
                        for j in range(CH):
                            last = nc.tensor.matmul(pr_bank[half][:, j * P:(j + 1) * P],
                                                    attn_t[:, half, j * P:(j + 1) * P], w_out_sb[:, :],
                                                    start=True, stop=True)
                        last.then_inc(projected, 1)

                def turn_tokens(q):
                    pe.wait_ge(x2_ready, q + 1)
                    if q >= 2:
                        pe.wait_ge(x2_t_ready, q - 1)
                    for j in range(CH):
                        last = nc.tensor.transpose(xt_bank[q % 2][:, j * P:(j + 1) * P],
                                                   x2[:, q * CH + j, :], ident[:, :])
                    last.then_inc(x2_transposed, 1)

                def route(q):
                    pe.wait_ge(x2_t_ready, q + 1)
                    for t in range(q * CH, (q + 1) * CH):
                        last = nc.tensor.matmul(lg_bank[:, t * 8:t * 8 + E], x2_t[:, t, :], router_sb[:, :],
                                                start=True, stop=True)
                    last.then_inc(logits_done, 1)

                def shared_up(q, ts):
                    x_at = x2_t[:, q * CH:(q + 1) * CH, :].rearrange("c t p -> c (t p)")
                    for t in ts:
                        if q * HT + t >= 2:
                            pe.wait_ge(s_up_ready, q * HT + t - 1)
                        nc.tensor.matmul(g_bank[t % 2], w_g[:, E, t * P:(t + 1) * P], x_at,
                                         start=True, stop=True).then_inc(s_gate_done, 1)
                        nc.tensor.matmul(u_bank[t % 2], w_u[:, E, t * P:(t + 1) * P], x_at,
                                         start=True, stop=True).then_inc(s_up_done, 1)

                def shared_down(q):
                    pe.wait_ge(s_hidden_ready, (q + 1) * HT)
                    if q >= 1:
                        pe.wait_ge(s_down_taken, q)
                    for j in range(CH):
                        for t in range(HT):
                            last = nc.tensor.matmul(
                                d_bank[:, j * P:(j + 1) * P],
                                s_hidden[q % 2][:, t, j * P:(j + 1) * P], w_d[:, E, t, :],
                                start=(t == 0), stop=(t == HT - 1))
                    last.then_inc(s_down_done, 1)

                for b in range(B):
                    turn_tokens(b * QC)
                    turn_tokens(b * QC + 1)
                    route(b * QC)
                    route(b * QC + 1)
                    if b == 0:
                        pe.wait_ge(shared_loaded, 16 * 3)
                        shared_up(0, range(HT))
                shared_up(1, [0])
                shared_down(0)
                shared_up(1, [1])
                pe.wait_ge(picked_ready, 1)
                pe.wait_ge(route_consts, 8)
                flat = picked[:, :, :].rearrange("p e t -> p (e t)")
                nc.tensor.matmul(rank_bank, upper[:, :], flat, start=True, stop=True).then_inc(counted, 1)
                nc.tensor.matmul(total_bank, ones_b[:, :], flat, start=True, stop=True).then_inc(counted, 1)
                shared_up(1, [2, 3])
                shared_up(2, [0])
                shared_down(1)
                shared_up(2, [1, 2, 3])
                for k in range(2 * NT):
                    if k % NT == 0:
                        pe.wait_ge(hot_ready, k // NT + 1)
                    last = nc.tensor.matmul(t_out, row_hot[:, k, :],
                                            tile_hot[:, k, :, :].rearrange("p v a -> p (v a)"),
                                            start=(k == 0), stop=(k == 2 * NT - 1))
                last.then_inc(table_done, 1)
                shared_up(3, [0])
                shared_down(2)
                shared_up(3, [1, 2, 3])
                shared_down(3)

                pe.wait_ge(experts_loaded, 16 * 3 * E)
                pe.wait_ge(s_up_ready, CHUNKS * HT)
                pe.wait_ge(s_down_taken, CHUNKS)
                pe.wait_ge(words_ready, 1)
                pe.wait_ge(places_ready, 2)

                def word(turn):
                    return pe.value_load(words[0:1, bass.ds(turn, 1)], min_val=0, max_val=8 ** (PACK + 1) - 1)

                def digit(w, u):
                    return (w >> (3 * u)) & 7

                def turn(k, u):
                    i = u % 2
                    pe.wait_ge(rows_loaded[i], (k // 2 + (u // 2 + 1)) * 16 if isinstance(k, int)
                               else k * 8 + (u // 2 + 1) * 16)
                    pe.wait_ge(rows_t_ready, k + (u + 1))
                    nc.tensor.transpose(t_bank[:, i * P:(i + 1) * P], rows[i][:, :], ident[:, :]
                                        ).then_inc(rows_turned, 1)

                def turn_hidden(k, u):
                    i = u % 2
                    pe.wait_ge(hidden_ready, k + (u + 1 + CREDIT))
                    pe.wait_ge(hidden_t_ready, k + (u + 1))
                    for t in range(HT):
                        last = nc.tensor.transpose(turn_bank[i][:, t * P:(t + 1) * P],
                                                   hidden[i][:, t * P:(t + 1) * P], ident[:, :])
                    last.then_inc(hidden_turned, 1)

                def up(k, u, e):
                    i = u % 2
                    pe.wait_ge(rows_t_ready, k + (u + 1 + 1))
                    pe.wait_ge(hidden_ready, k + (u + 1))
                    nc.tensor.matmul(g_bank[i], rows_t[i][:, :],
                                     w_g[:, bass.ds(e, 1), :].rearrange("c e h -> c (e h)"),
                                     start=True, stop=True).then_inc(gate_done, 1)
                    nc.tensor.matmul(u_bank[i], rows_t[i][:, :],
                                     w_u[:, bass.ds(e, 1), :].rearrange("c e h -> c (e h)"),
                                     start=True, stop=True).then_inc(up_done, 1)

                def project(k, u, e):
                    i = u % 2
                    pe.wait_ge(hidden_t_ready, k + (u + 1 + CREDIT))
                    pe.wait_ge(result_ready, k + (u + 1))
                    for t in range(HT):
                        last = nc.tensor.matmul(d_bank[:, 0:P], hidden_t[i][:, t, :],
                                                w_d[:, bass.ds(e, 1), t, :].rearrange("p e c -> p (e c)"),
                                                start=(t == 0), stop=(t == HT - 1))
                    last.then_inc(down_done, 1)

                turn(0, 0)
                turn(0, 1)
                up(0, 0, digit(word(0), 0))
                with pe.Fori(0, (TILES - TAIL) // PACK) as n:
                    w, k = word(n), n * PACK
                    for u in range(PACK):
                        turn(k, u + 2)
                        turn_hidden(k, u)
                        up(k, u + 1, digit(w, u + 1))
                        project(k, u, digit(w, u))
                w = word(WORDS - 1)
                turn_hidden(LAST, 0)
                up(LAST, 1, digit(w, 1))
                project(LAST, 0, digit(w, 0))
                turn_hidden(LAST, 1)
                project(LAST, 1, digit(w, 1))

            @block.scalar
            def _(act):
                act.sem_inc(attn_t_ready, CREDIT)
                act.sem_inc(proj_ready, CREDIT)
                act.sem_inc(rows_t_ready, 1)
                act.sem_inc(hidden_t_ready, CREDIT)
                for b in range(B):
                    for half in range(2):
                        act.wait_ge(attn_transposed, b * 2 + half + 1)
                        if b > 0:
                            act.wait_ge(projected, (b - 1) * 2 + half + 1)
                        nc.scalar.activation(attn_t[:, half, :], at_bank[half], ACT.Copy
                                             ).then_inc(attn_t_ready, 1)
                    for half in range(2):
                        act.wait_ge(projected, b * 2 + half + 1)
                        at = b * KT + half * CH
                        nc.scalar.activation(proj[:, at:at + CH, :].rearrange("p t c -> p (t c)"),
                                             pr_bank[half], ACT.Copy).then_inc(proj_ready, 1)

                def standard_deviations(n, at, count):
                    act.wait_ge(post_var_ready, n + 1)
                    nc.scalar.activation(std[:, at:at + count], var_eps[:, at:at + count], ACT.Sqrt
                                         ).then_inc(post_std_ready, 1)

                def copy_tokens(q):
                    act.wait_ge(x2_transposed, q + 1)
                    nc.scalar.activation(x2_t[:, q * CH:(q + 1) * CH, :].rearrange("p t c -> p (t c)"),
                                         xt_bank[q % 2], ACT.Copy).then_inc(x2_t_ready, 1)

                def shared_take(q, ts):
                    for t in ts:
                        if q * HT + t >= 2:
                            act.wait_ge(s_hidden_ready, q * HT + t - 1)
                        act.wait_ge(s_gate_done, q * HT + t + 1)
                        nc.scalar.activation(s_gate[t % 2][:, :], g_bank[t % 2], ACT.Silu
                                             ).then_inc(s_gate_ready, 1)
                        act.wait_ge(s_up_done, q * HT + t + 1)
                        act.wait_ge(s_gate_ready, q * HT + t + 1)
                        nc.scalar.activation(s_up[t % 2][:, :], u_bank[t % 2], ACT.Copy
                                             ).then_inc(s_up_ready, 1)

                def shared_result(q):
                    act.wait_ge(s_down_done, q + 1 + 2)
                    nc.scalar.activation(mixed[:, q * CH:(q + 1) * CH, :].rearrange("p t c -> p (t c)"),
                                         d_bank, ACT.Copy).then_inc(s_down_taken, 1)

                standard_deviations(0, 0, NT)
                standard_deviations(1, 0, KT)
                copy_tokens(0)
                copy_tokens(1)
                standard_deviations(2, KT, KT)
                shared_take(0, range(HT))
                copy_tokens(2)
                copy_tokens(3)
                for q in range(1, CHUNKS):
                    shared_take(q, [0])
                    shared_result(q - 1)
                    shared_take(q, [1, 2, 3])
                shared_result(CHUNKS - 1)
                act.wait_ge(gap_ready, 1)
                nc.scalar.activation(gap_exp[:, :], gap[:, :], ACT.Exp).then_inc(gap_exp_ready, 1)

                def copy_rows(pair, u):
                    k, i = pair * 2 + u, u % 2
                    act.wait_ge(rows_turned, k + 1 + CREDIT)
                    nc.scalar.activation(rows_t[i][:, :], t_bank[:, i * P:(i + 1) * P], ACT.Copy
                                         ).then_inc(rows_t_ready, 1)

                def gate_rows(pair, u):
                    k, i = pair * 2 + u, u % 2
                    act.wait_ge(gate_done, k + 1)
                    act.wait_ge(hidden_ready, k + 1)
                    nc.scalar.activation(gate[i][:, :], g_bank[i], ACT.Silu).then_inc(gate_ready, 1)

                def copy_hidden(pair, u):
                    k, i = pair * 2 + u, u % 2
                    act.wait_ge(hidden_turned, k + 1)
                    nc.scalar.activation(hidden_t[i][:, :, :].rearrange("p t c -> p (t c)"), turn_bank[i],
                                         ACT.Copy).then_inc(hidden_t_ready, 1)

                copy_rows(0, 0)
                copy_rows(0, 1)
                gate_rows(0, 0)
                with act.Fori(0, PAIRS) as pair:
                    for u in range(2):
                        copy_rows(pair, u + 2)
                        copy_hidden(pair, u)
                        gate_rows(pair, u + 1)
                copy_hidden(PAIRS, 0)
                gate_rows(PAIRS, 1)
                copy_hidden(PAIRS, 1)
                for b in range(B):
                    act.wait_ge(fin_var, b + 1)
                    nc.scalar.activation(std[:, b * KT:(b + 1) * KT], var_eps[:, b * KT:(b + 1) * KT], ACT.Sqrt
                                         ).then_inc(fin_std, 1)

            @block.vector
            def _(dve):
                step = Count()
                dve.sem_inc(hidden_ready, CREDIT)
                dve.sem_inc(result_ready, 1)

                def done():
                    dve.wait_ge(steps, step.now())

                nc.vector.memset(logits[:, :, E:8], NEG).then_inc(steps, step.one())
                for buf in before + ends:
                    nc.vector.memset(buf[:], 0.0).then_inc(steps, step.one())

                def layer_norm(src, at, count, var_sem, std_sem, n):
                    part = slice(at, at + count)
                    for t in range(at, at + count):
                        nc.vector.bn_stats(stats[:, t, :], src[:, t, :]).then_inc(steps, step.one())
                    done()
                    for t in range(at, at + count):
                        nc.vector.bn_aggr(mean_var[:, t, :], stats[:, t, :]).then_inc(steps, step.one())
                    done()
                    nc.vector.tensor_scalar(var_eps[:, part], mean_var[:, part, 1], EPS, None, ALU.add
                                            ).then_inc(var_sem, 1)
                    dve.wait_ge(std_sem, n)
                    nc.vector.reciprocal(rstd[:, part], std[:, part]).then_inc(steps, step.one())
                    done()

                dve.wait_ge(proj_ready, 4 + CREDIT)
                layer_norm(proj, 0, NT, post_var_ready, post_std_ready, 1)
                for t in range(NT):
                    nc.vector.tensor_scalar(proj[:, t, :], proj[:, t, :], mean_var[:, t, 0:1],
                                            rstd[:, t:t + 1], ALU.subtract, ALU.mult
                                            ).then_inc(steps, step.one())
                done()
                for b in range(B):
                    part = slice(b * KT, (b + 1) * KT)
                    nc.vector.tensor_tensor(x_sb[:, part, :], x_sb[:, part, :], proj[:, part, :], ALU.add
                                            ).then_inc(steps, step.one())
                done()
                for b in range(B):
                    layer_norm(x_sb, b * KT, KT, post_var_ready, post_std_ready, 2 + b)
                    for t in range(b * KT, (b + 1) * KT):
                        last = nc.vector.tensor_scalar(x2[:, t, :], x_sb[:, t, :], mean_var[:, t, 0:1],
                                                       rstd[:, t:t + 1], ALU.subtract, ALU.mult)
                        if t % CH == CH - 1:
                            last.then_inc(x2_ready, 1)
                dve.wait_ge(logits_done, CHUNKS)
                nc.vector.tensor_copy(logits[:, :, 0:E],
                                      lg_bank.rearrange("p (t e) -> p t e", e=8)[:, :, 0:E]
                                      ).then_inc(steps, step.one())
                done()
                for t in range(NT):
                    nc.vector.max(top[:, t, :], logits[:, t, :]).then_inc(steps, step.one())
                done()
                nc.vector.tensor_tensor(gap[:, :], top[:, :, 1], top[:, :, 0], ALU.subtract
                                        ).then_inc(gap_ready, 1)
                for t in range(NT):
                    nc.vector.max_index(top_at[:, t, :], top[:, t, :], logits[:, t, :]
                                        ).then_inc(steps, step.one())
                done()
                nc.vector.tensor_copy(top_at_f[:, :, :], top_at[:, :, 0:2]).then_inc(steps, step.one())
                done()
                dve.wait_ge(route_consts, 8)
                for i in range(2):
                    nc.vector.tensor_tensor(
                        pick[i][:, :, :], iota[:, 0:E].unsqueeze(2).broadcast_to([P, E, NT]),
                        top_at_f[:, :, i].unsqueeze(1).broadcast_to([P, E, NT]), ALU.is_equal
                    ).then_inc(steps, step.one())
                done()
                nc.vector.tensor_tensor(picked[:, :, :], pick[0][:, :, :], pick[1][:, :, :], ALU.add
                                        ).then_inc(picked_ready, 1)
                dve.wait_ge(counted, 2)
                nc.vector.tensor_copy(before[0][:, :, KT:], total_bank.rearrange("p (e t) -> p e t", e=E)
                                      ).then_inc(steps, step.one())
                for i, shift in enumerate((1, 2, 4, 8)):
                    src, dst = before[i % 2], before[(i + 1) % 2]
                    done()
                    nc.vector.tensor_tensor(dst[:, :, KT:], src[:, :, KT:], src[:, :, KT - shift:KT + NT - shift],
                                            ALU.add).then_inc(steps, step.one())
                done()
                sums = before[0]
                nc.vector.tensor_tensor(over[:, :, :], sums[:, :, KT + NT - 1:KT + NT].broadcast_to([P, E, NT]),
                                        thresholds[:, :].unsqueeze(1).broadcast_to([P, E, NT]), ALU.is_gt
                                        ).then_inc(steps, step.one())
                nc.vector.tensor_tensor(slot_in[:, :, :], rank_bank.rearrange("p (e t) -> p e t", e=E),
                                        sums[:, :, KT - 1:KT + NT - 1], ALU.add).then_inc(steps, step.one())
                done()
                nc.vector.tensor_reduce(ends[0][:, 4:], over[:, :, :], AX.X, ALU.add
                                        ).then_inc(steps, step.one())
                for i, shift in enumerate((1, 2, 4)):
                    src, dst = ends[i % 2], ends[(i + 1) % 2]
                    done()
                    nc.vector.tensor_tensor(dst[:, 4:], src[:, 4:], src[:, 4 - shift:4 + E - shift], ALU.add
                                            ).then_inc(steps, step.one())
                done()
                end = ends[1]
                nc.vector.scalar_tensor_tensor(slot_all[:, :, :], end[:, 3:3 + E].unsqueeze(2).broadcast_to([P, E, NT]),
                                               float(P), slot_in[:, :, :], ALU.mult, ALU.add
                                               ).then_inc(steps, step.one())
                done()
                for i in range(2):
                    nc.vector.tensor_tensor(slot_pick[i][:, :, :], slot_all[:, :, :], pick[i][:, :, :], ALU.mult
                                            ).then_inc(steps, step.one())
                done()
                for i in range(2):
                    nc.vector.tensor_reduce(slot_f[:, i, :], slot_pick[i][:, :, :].rearrange("p e t -> p t e"),
                                            AX.X, ALU.add).then_inc(steps, step.one())
                done()
                nc.vector.tensor_copy(slot_u[:, :], slot_f[:, :, :].rearrange("p i t -> p (i t)")
                                      ).then_inc(steps, step.one())
                done()
                nc.vector.tensor_scalar(slot_part[:, 0, :], slot_u[:, :], 7, None, ALU.logical_shift_right
                                        ).then_inc(steps, step.one())
                nc.vector.tensor_scalar(slot_part[:, 1, :], slot_u[:, :], P - 1, None, ALU.bitwise_and
                                        ).then_inc(steps, step.one())
                done()
                nc.vector.tensor_copy(slot_part_f[:, :, :], slot_part[:, :, :]).then_inc(steps, step.one())
                done()
                for i in range(2):
                    part = slice(i * NT, (i + 1) * NT)
                    nc.vector.tensor_tensor(
                        tile_hot[:, part, 2, :], iota[:, 0:TILES].unsqueeze(1).broadcast_to([P, NT, TILES]),
                        slot_part_f[:, 0, part].unsqueeze(2).broadcast_to([P, NT, TILES]), ALU.is_equal
                    ).then_inc(steps, step.one())
                    done()
                    nc.vector.tensor_scalar(tile_hot[:, part, 0, :], tile_hot[:, part, 2, :], iota_p[:, 0:1],
                                            None, ALU.mult).then_inc(steps, step.one())
                    nc.vector.tensor_tensor(
                        tile_hot[:, part, 1, :], tile_hot[:, part, 2, :],
                        iota_ct[:, part].unsqueeze(2).broadcast_to([P, NT, TILES]), ALU.mult
                    ).then_inc(steps, step.one())
                    nc.vector.tensor_tensor(
                        row_hot[:, part, :], iota[:, :].unsqueeze(1).broadcast_to([P, NT, P]),
                        slot_part_f[:, 1, part].unsqueeze(2).broadcast_to([P, NT, P]), ALU.is_equal
                    ).then_inc(steps, step.one())
                    done()
                    nc.vector.memset(spare[:, 0:1], 0.0).then_inc(hot_ready, 1)
                nc.vector.tensor_tensor(passed[:, :, :], iota[0:1, 0:PADDED].unsqueeze(2).broadcast_to([1, PADDED, E]),
                                        end[0:1, 4:].unsqueeze(1).broadcast_to([1, PADDED, E]), ALU.is_ge
                                        ).then_inc(steps, step.one())
                done()
                nc.vector.tensor_reduce(tile_f[:, :], passed[:, :, :], AX.X, ALU.add
                                        ).then_inc(steps, step.one())
                done()
                nc.vector.tensor_scalar(tile_f[:, :], tile_f[:, :], float(E - 1), None, ALU.min
                                        ).then_inc(steps, step.one())

                def every(i):
                    return tile_f[:, i:i + WORDS * PACK].rearrange("o (w s) -> o w s", s=PACK)[:, :, 0]

                done()
                dve.wait_ge(table_done, 1)
                nc.vector.tensor_copy(table[:, :, :], t_out.rearrange("p (v a) -> p v a", v=3)
                                      ).then_inc(steps, step.one())
                done()
                nc.vector.scalar_tensor_tensor(place_f[:, :], table[:, 1, :], float(P), table[:, 0, :],
                                               ALU.mult, ALU.add).then_inc(steps, step.one())
                nc.vector.tensor_scalar(spare[:, :], table[:, 2, :], -1.0, 1.0, ALU.mult, ALU.add
                                        ).then_inc(steps, step.one())
                done()
                nc.vector.tensor_copy(place_u[:, :], place_f[:, :]).then_inc(steps, step.one())
                nc.vector.tensor_tensor(spare[:, :], spare[:, :], spare_at[:, :], ALU.mult
                                        ).then_inc(steps, step.one())
                done()
                nc.vector.tensor_scalar(source[:, :], place_u[:, :], B * T - 1, None, ALU.bitwise_and
                                        ).then_inc(places_ready, 1)
                nc.vector.tensor_tensor(target[:, :], place_f[:, :], spare[:, :], ALU.add
                                        ).then_inc(places_ready, 1)
                nc.vector.tensor_copy(words_f[:, :], every(PACK)).then_inc(steps, step.one())
                for i in reversed(range(PACK)):
                    done()
                    nc.vector.scalar_tensor_tensor(words_f[:, :], words_f[:, :], 8.0, every(i),
                                                   ALU.mult, ALU.add).then_inc(steps, step.one())
                done()
                nc.vector.tensor_copy(words[:, :], words_f[:, :]).then_inc(words_ready, 1)
                dve.wait_ge(gap_exp_ready, 1)
                nc.vector.tensor_scalar(gap_sum[:, :], gap_exp[:, :], 1.0, None, ALU.add
                                        ).then_inc(steps, step.one())
                done()
                nc.vector.reciprocal(weight[:, 0, :], gap_sum[:, :]).then_inc(steps, step.one())
                done()
                nc.vector.tensor_tensor(weight[:, 1, :], gap_exp[:, :], weight[:, 0, :], ALU.mult
                                        ).then_inc(steps, step.one())

                def multiply(pair, u):
                    k, i = pair * 2 + u, u % 2
                    dve.wait_ge(gate_ready, k + 1)
                    dve.wait_ge(up_done, k + 1)
                    nc.vector.tensor_tensor(hidden[i][:, :], u_bank[i], gate[i][:, :], ALU.mult
                                            ).then_inc(hidden_ready, 1)

                def take_result(pair, u, first=False):
                    k, i = pair * 2 + u, u % 2
                    dve.wait_ge(down_done, k + 1)
                    if not first:
                        dve.wait_ge(result_stored[i], pair * 16)
                    nc.vector.tensor_copy(result[i][:, :], d_bank[:, 0:P]).then_inc(result_ready, 1)

                multiply(0, 0)
                for u in range(2):
                    multiply(0, u + 1)
                    take_result(0, u, first=True)
                with dve.Fori(1, PAIRS) as pair:
                    for u in range(2):
                        multiply(pair, u + 1)
                        take_result(pair, u)
                multiply(PAIRS, 1)
                for u in range(2):
                    take_result(PAIRS, u)

                dve.wait_ge(s_down_taken, CHUNKS)
                for b in range(B):
                    part = slice(b * KT, (b + 1) * KT)
                    dve.wait_ge(returned[b], 32)
                    for i in range(2):
                        done()
                        for t in range(b * KT, (b + 1) * KT):
                            nc.vector.scalar_tensor_tensor(
                                mixed[:, t, :], back[i][:, t, :], weight[:, i, t:t + 1], mixed[:, t, :],
                                ALU.mult, ALU.add).then_inc(steps, step.one())
                    done()
                    layer_norm(mixed, b * KT, KT, fin_var, fin_std, b + 1)
                    for t in range(b * KT, (b + 1) * KT):
                        nc.vector.tensor_scalar(mixed[:, t, :], mixed[:, t, :], mean_var[:, t, 0:1],
                                                rstd[:, t:t + 1], ALU.subtract, ALU.mult
                                                ).then_inc(steps, step.one())
                    done()
                    nc.vector.tensor_tensor(mixed[:, part, :], mixed[:, part, :], x_sb[:, part, :], ALU.add
                                            ).then_inc(half_done, 1)



def kernel(**inputs):
    import concourse.bacc as bacc
    from concourse.bass_utils import run_bass_kernel_spmd

    a = {k: np.asarray(v) for k, v in inputs.items()}
    wqkv = a["L0_attn_w_qkv"]
    arrays = {
        "x": a["L0_attn_x"],
        "wqkv": wqkv,
        "wq_t": wqkv[:, :C].T,
        "dirs": a["L0_attn_head_dirs"].reshape(1, H * HD),
        "scales": a["L0_attn_head_scales"].reshape(1, H),
        "w_out": a["L0_attn_w_out"],
        "router_t": a["L0_ffn_router_w"].T,
        "w_gate": np.concatenate([a["L0_ffn_w_gate"], a["L0_ffn_sw_gate"]]),
        "w_up": np.concatenate([a["L0_ffn_w_up"], a["L0_ffn_sw_up"]]),
        "w_down": np.concatenate([a["L0_ffn_w_down"], a["L0_ffn_sw_down"]]),
    }
    arrays = {f"in_{k}": np.ascontiguousarray(v) for k, v in arrays.items()}
    nc = bacc.Bacc("TRN2", target_bir_lowering=False, num_devices=1)
    args = [nc.dram_tensor(k, v.shape, mybir.dt.from_np(v.dtype), kind="ExternalInput").ap()
            for k, v in arrays.items()]
    out = nc.dram_tensor("out", (B, T, C), F32, kind="ExternalOutput").ap()
    program(nc, *args, out)
    r = run_bass_kernel_spmd(nc, [arrays], core_ids=[0])
    return r.results[0]["out"]
```

```python
from contextlib import ExitStack

import numpy as np

import concourse.bass as bass
from concourse import mybir

F32 = mybir.dt.float32
BF16 = mybir.dt.bfloat16
U32 = mybir.dt.uint32
ALU = mybir.AluOpType
ACT = mybir.ActivationFunctionType
AX = mybir.AxisListType

B, T, C, H = 2, 1024, 128, 16
HD = C // H
SCALE = 1.0 / float(np.sqrt(HD))
P = 128
KT = T // P
NT = B * KT
HG = 4
NG = H // HG
GROUPS = B * NG
HQ = 32
COMBOS = ((0, 0), (0, 1), (0, 2), (1, 0), (1, 1), (2, 0))
KR = HD * len(COMBOS)
MR = KR + 3
BANK = 512
NEG = -3.0e38
ONES_BITS = float(np.array([0x3F803F80], np.uint32).view(np.float32)[0])
EPS = 1e-5
RSQRT_BITS = float(0x5F3759DF)
NEWTON = 4
E, HID = 7, 512
NE = E + 1
HT = HID // P
TILES = (2 * B * T + E * (P - 1)) // P
TILES += TILES % 2
PACK = 6
WORDS = -(-TILES // PACK)
PADDED = (WORDS + 1) * PACK
TAIL = 2
assert (TILES - TAIL) % PACK == 0 and PACK % 2 == 0
CH = BANK // P
STACKS = 3
CREDIT = 2
BURST = 256
SKEW = 8
K_RUNS = ((0, 3), (3, 2), (5, 1))
LOADS = len(COMBOS) + len(K_RUNS) + 1
KEPT = 9
FILLED = 5
RING = 3
LEAD = 512
EARLY = 1.5


class Count:

    def __init__(self):
        self.base, self.n, self.outer = 0, 0, []

    def one(self):
        self.n += 1
        return 1

    def now(self):
        return self.base + self.n

    def enter(self, i, per_turn):
        self.outer.append((self.base, self.n, per_turn))
        self.base, self.n = self.base + self.n + i * per_turn, 0

    def leave(self, turns):
        base, n, per_turn = self.outer.pop()
        assert self.n == per_turn, (self.n, per_turn)
        self.base, self.n = base, n + per_turn * turns


def units():
    return [(j, h) for j in range(KT) for h in range(HG)]


def pieces(width):
    return [(a, min(a + BANK, width)) for a in range(0, width, BANK)]


def bursts(j):
    return [(max(j * P, a), a + BURST) for a in range(0, T, BURST) if a + BURST > j * P]


SCORE_WORK = [T - P * j + P + (4 * BURST if j > 0 and h < len(bursts(j - 1)) else 0) for j, h in units()]

PIECES_BEFORE = [0]
for _j, _h in units():
    PIECES_BEFORE.append(PIECES_BEFORE[-1] + len(pieces(T - P * _j)))
PIECES = PIECES_BEFORE[-1]
TURNED = ((0, 3), (3, 6), (6, 8))
SLOTS = PIECES + len(TURNED)
assert PIECES % RING == 0 and SLOTS % RING == 0


def program(nc, x, wqkv, wq_t, dirs, scales, w_out, router_t, w_gate, w_up, w_down, out):
    ctx = ExitStack()
    with ctx:
        def sb(name, shape, dt=F32):
            return ctx.enter_context(nc.sbuf_tensor(name, shape, dt))

        front = ctx.enter_context(ExitStack())

        def sb_front(name, shape, dt=F32):
            return front.enter_context(nc.sbuf_tensor(name, shape, dt))

        def sem(name):
            return ctx.enter_context(nc.semaphore(name))

        q_parts = nc.dram_tensor("q_parts", [B * H, 3, HD, T], BF16, kind="Internal").ap()
        k_parts = nc.dram_tensor("k_parts", [B * H, 3, HD, T], BF16, kind="Internal").ap()

        tokens = nc.dram_tensor("tokens", [B * T, C], F32, kind="Internal").ap()
        results = nc.dram_tensor("results", [2 * B * T + TILES * P, C], F32, kind="Internal").ap()

        x_sb = sb("x_sb", [P, NT, C])
        w_out_sb = sb("w_out_sb", [C, C])
        router_sb = sb("router_sb", [C, E])
        ident = sb("ident", [P, P])
        ident_b = sb("ident_b", [P, P], BF16)
        attn = sb("attn", [P, KT, (1 + GROUPS) * HG * HD])
        x2 = sb("x2", [P, NT, C])
        x2_t = sb("x2_t", [C, NT, P])
        logits = sb("logits", [P, NT, 8])
        stats = sb("stats", [P, NT, 6])
        mean_var = sb("mean_var", [P, NT, 2])
        var_eps = sb("var_eps", [P, NT])
        std = sb("std", [P, NT])
        rstd = sb("rstd", [P, NT])

        xn_stage = sb_front("xn_stage", [P, 2, CH, C])
        xn_t = sb_front("xn_t", [C, 2, BANK])
        wqkv_sb = sb_front("wqkv_sb", [C, 3 * C])
        wq_t_sb = sb_front("wq_t_sb", [C, C])
        wq_fold = sb_front("wq_fold", [C, C])
        dirs_sb = sb_front("dirs_sb", [1, C])
        scales_sb = sb_front("scales_sb", [1, H])
        dirs_scaled = sb_front("dirs_scaled", [1, C])
        zeros = sb_front("zeros", [P, P])
        mask_qk = sb_front("mask_qk", [P, P], BF16)
        mask_kq = sb_front("mask_kq", [P, P], BF16)
        same_head = sb_front("same_head", [C, H, HD])
        fold = sb_front("fold", [C, C])
        rest = x2[:, :, :].rearrange("p t c -> p (t c)").rearrange("p (h i t) -> p h i t", h=2, i=2)
        zero_rows = sb_front("zero_rows", [MR - KR, HG * T], BF16)
        v_all = sb_front("v_all", [P, GROUPS, KT, HG * HD])
        q_st = [sb_front(f"q_st{r}", [P, HG, T], BF16) for r in range(STACKS)]
        k_st = [sb_front(f"k_st{r}", [P, HG, T], BF16) for r in range(STACKS)]
        v_pad = [sb_front(f"v_pad{r}", [P, KT, HG, HQ]) for r in range(STACKS)]
        mx_part = [sb_front(f"mx_part{r}", [P, HG * KT, 2]) for r in range(STACKS)]
        mx = sb_front("mx", [P, HG * KT])
        mx_t = sb_front("mx_t", [P, HG * KT])
        mx_neg = sb_front("mx_neg", [P, HG * KT])
        mx_rest = sb_front("mx_rest", [P, HG * KT])
        mx_rows = [sb_front(f"mx_rows{r}", [P, 3, HG * KT], BF16) for r in range(STACKS)]
        probs = [sb_front(f"probs{i}", [P, HG, T]) for i in range(2)]
        parts = [p[:, :, :].rearrange("p h t -> p (h t)").bitcast(BF16)[:, 0:2 * 2 * 3 * BANK].rearrange(
            "p (h i s t) -> p h i s t", h=2, i=2, s=3) for p in probs]
        o_cols = sb_front("o_cols", [P, T])
        half_bits = sb_front("half_bits", [P, KT], U32)
        o_raw = sb_front("o_raw", [P, 1 + GROUPS, KT * HG, HD + 1])
        den = sb_front("den", [P, KT * HG])

        banks = ctx.enter_context(nc.psum_tensor("banks", [P, 8 * BANK], F32))

        def bank(i, n=1):
            return banks[:, i * BANK:(i + n) * BANK]

        max_bank = [bank(i) for i in range(RING)]
        score_bank = [bank(RING + i) for i in range(RING)]
        first_proj_bank, first_x2_bank, first_lg_bank = [bank(2), bank(0)], [bank(1), bank(2)], bank(0)
        o_bank = [bank(6), bank(7)]

        x_loaded = sem("x_loaded")
        weights_loaded = sem("weights_loaded")
        consts_ready = sem("consts_ready")
        pool_steps = sem("pool_steps")
        vector_steps = sem("vector_steps")
        dirs_scaled_ready = sem("dirs_scaled_ready")
        outer_ready = sem("outer_ready")
        fold_ready = sem("fold_ready")
        wq_folded = sem("wq_folded")
        wq_fold_ready = sem("wq_fold_ready")
        var_ready = sem("var_ready")
        std_ready = sem("std_ready")
        xn_ready = sem("xn_ready")
        xn_transposed = sem("xn_transposed")
        xn_t_ready = sem("xn_t_ready")
        q_projected = sem("q_projected")
        k_projected = sem("k_projected")
        v_projected = sem("v_projected")
        high_ready = sem("high_ready")
        v_stored = sem("v_stored")
        parts_ready = sem("parts_ready")
        parts_stored = sem("parts_stored")
        stacks_padded = sem("stacks_padded")
        stacks_loaded = [sem(f"stacks_loaded{r}") for r in range(STACKS)]
        v_padded = sem("v_padded")
        max_filled = sem("max_filled")
        max_taken = sem("max_taken")
        rows_split = sem("rows_split")
        rows_ready = sem("rows_ready")
        slot_filled = sem("slot_filled")
        slot_taken = sem("slot_taken")
        first_attn_ready = sem("first_attn_ready")
        first_turned = sem("first_turned")
        first_attn_t_ready = sem("first_attn_t_ready")
        first_projected = sem("first_projected")
        first_logits_done = sem("first_logits_done")
        post_var_ready = sem("post_var_ready")
        post_std_ready = sem("post_std_ready")
        x2_ready = sem("x2_ready")
        x2_transposed = sem("x2_transposed")
        x2_t_ready = sem("x2_t_ready")
        pv_done = sem("pv_done")
        o_taken = sem("o_taken")

        block = front.enter_context(nc.Block())

        TURNS, PER_TURN = 2, STACKS

        @block.sync
        def _(sp):
            for b in range(B):
                sp.dma_start(x_sb[:, b * KT:(b + 1) * KT, :],
                             x[b].rearrange("(t p) c -> p t c", p=P)).then_inc(x_loaded, 16)
            for dst, src in ((dirs_sb[:, :], dirs), (scales_sb[:, :], scales), (wq_t_sb[:, :], wq_t),
                             (wqkv_sb[:, :], wqkv), (w_out_sb[:, :], w_out), (router_sb[:, :], router_t)):
                sp.dma_start(dst, src).then_inc(weights_loaded, 16)

            def store_parts(b):
                for half in range(2):
                    sp.wait_ge(parts_ready, b * 2 + half + 1 + CREDIT)
                    for qk, dst in ((0, q_parts), (1, k_parts)):
                        for part in range(3):
                            sp.dma_start(
                                dst[b * H:(b + 1) * H, part, :, half * BANK:(half + 1) * BANK],
                                parts[b][:, half, qk, part, :]).then_inc(parts_stored, 16)

            def load_stacks(turn, u):
                n, r = turn * STACKS + u, u % STACKS
                for row, (pq, pk) in enumerate(COMBOS):
                    sp.dma_start(q_st[r][row * HD:(row + 1) * HD, :, :],
                                 q_parts[bass.ds(n * HG, HG), pq, :, :].rearrange("h d t -> d h t")
                                 ).then_inc(stacks_loaded[r], 16)
                for row, count in K_RUNS:
                    sp.dma_start(k_st[r][row * HD:(row + count) * HD, :, :],
                                 k_parts[bass.ds(n * HG, HG), 0:count, :, :].rearrange(
                                     "h s d t -> (s d) h t")).then_inc(stacks_loaded[r], 16)

            def clear_maxima(r):
                sp.dma_start(q_st[r][KR:MR, :, :].rearrange("r h t -> r (h t)"), zero_rows[:, :]
                             ).then_inc(stacks_loaded[r], 16)

            def send_rows(n, r):
                sp.wait_ge(rows_split, n + 1)
                for part in range(3):
                    for b in range(4):
                        sp.dma_start(
                            q_st[r][KR + part:KR + part + 1, :, :].rearrange(
                                "o h (i b c) -> o b (h i) c", i=KT, c=32)[:, b, :, :],
                            mx_rows[r][b * 32:(b + 1) * 32, part, :]).then_inc(rows_ready, 16)

            sp.wait_ge(consts_ready, 1)
            sp.wait_ge(stacks_padded, 2 * STACKS)
            clear_maxima(0)
            clear_maxima(1)
            store_parts(0)
            sp.wait_ge(parts_stored, 16 * 6 * 2)
            load_stacks(0, 0)
            store_parts(1)
            load_stacks(0, 1)
            sp.wait_ge(parts_stored, 16 * 6 * 4)
            send_rows(0, 0)
            with sp.Fori(0, TURNS) as turn:
                for u in range(PER_TURN):
                    n = turn * PER_TURN + u
                    sp.wait_ge(pv_done, n * KT + CREDIT)
                    load_stacks(turn, u + 2)
                    clear_maxima((u + 2) % STACKS)
                    send_rows(n + 1, (u + 1) % STACKS)
            send_rows(GROUPS - 1, (GROUPS - 1) % STACKS)

        @block.gpsimd
        def _(pool):
            nc.gpsimd.memset(zeros[:, :], 0.0).then_inc(pool_steps, 1)
            nc.gpsimd.memset(same_head[:, :, :], 1.0).then_inc(pool_steps, 1)
            pool.wait_ge(pool_steps, 2)
            nc.gpsimd.affine_select(out=ident[:, :], in_=zeros[:, :], compare_op=ALU.not_equal, fill=1.0,
                                    base=0, pattern=[[-1, P]], channel_multiplier=1).then_inc(pool_steps, 1)
            nc.gpsimd.affine_select(out=ident_b[:, :], in_=zeros[:, :], compare_op=ALU.not_equal, fill=1.0,
                                    base=0, pattern=[[-1, P]], channel_multiplier=1).then_inc(pool_steps, 1)
            nc.gpsimd.affine_select(out=mask_qk[:, :], in_=zeros[:, :], compare_op=ALU.is_ge, fill=NEG,
                                    base=0, pattern=[[-1, P]], channel_multiplier=1).then_inc(pool_steps, 1)
            nc.gpsimd.affine_select(out=mask_kq[:, :], in_=zeros[:, :], compare_op=ALU.is_ge, fill=NEG,
                                    base=0, pattern=[[1, P]], channel_multiplier=-1).then_inc(pool_steps, 1)
            nc.gpsimd.affine_select(out=same_head[:, :, :], in_=same_head[:, :, :], compare_op=ALU.is_ge,
                                    fill=0.0, base=0, pattern=[[-HD, H], [0, HD]],
                                    channel_multiplier=1).then_inc(pool_steps, 1)
            pool.wait_ge(pool_steps, 7)
            nc.gpsimd.affine_select(out=same_head[:, :, :], in_=same_head[:, :, :], compare_op=ALU.is_ge,
                                    fill=0.0, base=HD - 1, pattern=[[HD, H], [0, HD]],
                                    channel_multiplier=-1).then_inc(pool_steps, 1)
            pool.wait_ge(pool_steps, 8)
            nc.gpsimd.memset(zero_rows[:, :], 0.0).then_inc(pool_steps, 1)
            for r in range(STACKS):
                nc.gpsimd.memset(v_pad[r][:, :, :, :], 0.0).then_inc(pool_steps, 1)
                nc.gpsimd.memset(mx_part[r][:, :, :], NEG).then_inc(pool_steps, 1)
            pool.wait_ge(pool_steps, 9 + 2 * STACKS)
            for r in range(STACKS):
                nc.gpsimd.memset(v_pad[r][:, :, :, HD:HD + 1], 1.0).then_inc(pool_steps, 1)
            pool.wait_ge(pool_steps, 9 + 3 * STACKS)
            nc.gpsimd.memset(zeros[:, 0:1], 0.0).then_inc(consts_ready, 1)

            for r in range(STACKS):
                nc.gpsimd.memset(q_st[r][:, :, :].bitcast(F32), 0.0).then_inc(stacks_padded, 1)
                nc.gpsimd.memset(k_st[r][:, :, :].bitcast(F32), ONES_BITS).then_inc(stacks_padded, 1)

            def pad_v(n, r):
                nc.gpsimd.tensor_copy(
                    v_pad[r][:, :, :, 0:HD],
                    v_all[:, bass.ds(n, 1), :, :].rearrange("p g k (h d) -> p (g k) h d", d=HD)
                ).then_inc(v_padded, 1)

            pool.wait_ge(v_stored, 4 + CREDIT)
            pad_v(0, 0)
            pad_v(1, 1)
            with pool.Fori(0, TURNS) as turn:
                for u in range(PER_TURN):
                    n = turn * PER_TURN + u
                    pool.wait_ge(pv_done, n * KT + CREDIT)
                    pad_v(n + 2, (u + 2) % STACKS)

        @block.tensor
        def _(pe):
            pe.sem_inc(pv_done, CREDIT)
            pe.sem_inc(xn_transposed, CREDIT)
            pe.wait_ge(weights_loaded, 16 * 6)
            pe.wait_ge(dirs_scaled_ready, 1)
            nc.tensor.matmul(bank(0)[:, 0:C], dirs_sb[:, :], dirs_scaled[:, :], start=True, stop=True
                             ).then_inc(outer_ready, 1)
            pe.wait_ge(fold_ready, 1)
            nc.tensor.matmul(bank(1)[:, 0:C], wq_t_sb[:, :], fold[:, :], start=True, stop=True
                             ).then_inc(wq_folded, 1)
            pe.wait_ge(wq_fold_ready, 1)
            pe.wait_ge(consts_ready, 1)
            with pe.Fori(0, B) as b:
                for half in range(2):
                    done = b * 2 + half
                    bt, bq, bk, bv = (bank(4 * half + i) for i in range(4))
                    pe.wait_ge(xn_ready, done + 1)
                    pe.wait_ge(xn_t_ready, done + 1)
                    for j in range(CH):
                        last = nc.tensor.transpose(bt[:, j * P:(j + 1) * P], xn_stage[:, half, j, :],
                                                   ident[:, :])
                    last.then_inc(xn_transposed, 1)
                for half in range(2):
                    done = b * 2 + half
                    bt, bq, bk, bv = (bank(4 * half + i) for i in range(4))
                    pe.wait_ge(xn_t_ready, done + 1 + CREDIT)
                    pe.wait_ge(parts_ready, done + 1)
                    nc.tensor.matmul(bq, wq_fold[:, :], xn_t[:, half, :], start=True, stop=True
                                     ).then_inc(q_projected, 1)
                    nc.tensor.matmul(bk, wqkv_sb[:, C:2 * C], xn_t[:, half, :], start=True, stop=True
                                     ).then_inc(k_projected, 1)
                    pe.wait_ge(v_stored, done + 1)
                    for j in range(CH):
                        last = nc.tensor.matmul(bv[:, j * P:(j + 1) * P],
                                                xn_t[:, half, j * P:(j + 1) * P],
                                                wqkv_sb[:, 2 * C:3 * C], start=True, stop=True)
                    last.then_inc(v_projected, 1)

            def max_unit(turn, u, idx):
                m, r = turn * STACKS + u, u % STACKS
                j, h = units()[idx]
                i = KT - 1 - j
                width = T - P * j
                if idx == 0:
                    pe.wait_ge(stacks_loaded[r], (turn + (u // STACKS + 1)) * (16 * LOADS))
                for piece, (a, z) in enumerate(pieces(width)):
                    k = PIECES_BEFORE[idx] + piece
                    dst = max_bank[k % RING]
                    pe.wait_ge(max_taken, m * PIECES + k + 1)
                    last = nc.tensor.matmul(dst[:, 0:z - a], q_st[r][:, h, i * P:(i + 1) * P],
                                            k_st[r][:, h, a:z], start=True, stop=(z < width))
                    if z == width:
                        last = nc.tensor.matmul(dst[:, z - a - P:z - a], ident_b[:, :], mask_qk[:, :],
                                                start=False, stop=True)
                    last.then_inc(max_filled, 1)
                    yield

            def score_unit(n, r, idx):
                j, h = units()[idx]
                for piece, (a, z) in enumerate(pieces(T - P * j)):
                    k = PIECES_BEFORE[idx] + piece
                    dst = score_bank[k % RING]
                    pe.wait_ge(slot_taken, n * SLOTS + k + 1)
                    last = nc.tensor.matmul(dst[:, 0:z - a], k_st[r][:, h, j * P:(j + 1) * P],
                                            q_st[r][:, h, j * P + a:j * P + z],
                                            start=True, stop=(a > 0))
                    if a == 0:
                        last = nc.tensor.matmul(dst[:, 0:P], ident_b[:, :], mask_kq[:, :],
                                                start=False, stop=True)
                    last.then_inc(slot_filled, 1)
                    yield

            def weighted_values(n, r, j, which):
                for k in which:
                    if k >= len(bursts(j)):
                        continue
                    a, z = bursts(j)[k]
                    if k == 0:
                        pe.wait_ge(slot_taken, n * SLOTS + PIECES_BEFORE[HG * (j + 1)] + RING)
                    if j == 0 and k == 0:
                        pe.wait_ge(o_taken, n * 2 + 1)
                        pe.wait_ge(v_padded, n + 1)
                    c = a // BANK
                    for h in range(HG):
                        last = nc.tensor.matmul(
                            o_bank[c][h * HQ:(h + 1) * HQ, a - c * BANK:z - c * BANK],
                            v_pad[r][:, j, h, :], probs[j % 2][:, h, a - j * P:z - j * P],
                            start=(j == 0 and a % BANK == 0), stop=(j == (c + 1) * CH - 1),
                            skip_group_check=True)
                    if k == len(bursts(j)) - 1:
                        last.then_inc(pv_done, 1)

            def first_turn_attn():
                pe.wait_ge(max_taken, GROUPS * PIECES + RING)
                pe.wait_ge(first_attn_ready, 1)
                for half in range(2):
                    for j in range(CH):
                        last = nc.tensor.transpose(max_bank[half][:, j * P:(j + 1) * P],
                                                   attn[:, half * CH + j, HG * HD:HG * HD + C], ident[:, :])
                    last.then_inc(first_turned, 1)

            def first_project():
                for half in range(2):
                    pe.wait_ge(first_attn_t_ready, half + 1)
                    for j in range(CH):
                        last = nc.tensor.matmul(first_proj_bank[half][:, j * P:(j + 1) * P],
                                                xn_t[:, half, j * P:(j + 1) * P], w_out_sb[:, :],
                                                start=True, stop=True)
                    last.then_inc(first_projected, 1)

            def first_turn_tokens():
                for q in range(2):
                    pe.wait_ge(x2_ready, q + 1)
                    for j in range(CH):
                        last = nc.tensor.transpose(first_x2_bank[q][:, j * P:(j + 1) * P],
                                                   x2[:, q * CH + j, :], ident[:, :])
                    last.then_inc(x2_transposed, 1)

            def first_route():
                pe.wait_ge(x2_t_ready, 2)
                for t in range(KT):
                    last = nc.tensor.matmul(first_lg_bank[:, t * 8:t * 8 + E], x2_t[:, t, :], router_sb[:, :],
                                            start=True, stop=True)
                last.then_inc(first_logits_done, 1)

            FIRST_BATCH = {0: first_turn_attn, 3: first_project, 28: first_turn_tokens}

            def group(turn, u, ahead):
                n, r = turn * STACKS + u, u % STACKS
                pe.wait_ge(rows_ready, (n + 1) * (16 * 12))
                todo = [(turn, u + 1, i) for i in range(SKEW, KT * HG)] if ahead > 0 else []
                if ahead > 1:
                    todo += [(turn, u + 2, i) for i in range(SKEW)]
                sizes = [z - a for _, _, i in todo for a, z in pieces(T - P * units()[i][0])]
                kept = KEPT if ahead > 1 else 0
                share = sum(sizes) / sum(SCORE_WORK) * (1.0 if ahead > 1 else EARLY)
                stream = (None for unit in todo for _ in max_unit(*unit))
                work, given = 0, 0
                for idx in range(KT * HG):
                    unit = score_unit(n, r, idx)
                    for part in range(len(pieces(T - P * units()[idx][0]))):
                        next(unit)
                        work += SCORE_WORK[idx] / len(pieces(T - P * units()[idx][0]))
                        if given < len(sizes) - kept and sum(sizes[:given + 1]) <= work * share + LEAD:
                            next(stream)
                            given += 1
                    if ahead == 0 and idx in FIRST_BATCH:
                        FIRST_BATCH[idx]()
                    if idx % HG == 0 and idx >= FILLED * HG and given < len(sizes):
                        next(stream)
                        given += 1
                    if idx >= HG:
                        weighted_values(n, r, idx // HG - 1, [idx % HG])
                    while given < len(sizes) - kept and sum(sizes[:given + 1]) <= work * share + LEAD:
                        next(stream)
                        given += 1
                if kept:
                    next(stream)
                    given += 1
                if ahead == 0:
                    first_route()
                weighted_values(n, r, KT - 1, range(HG))
                for _ in sizes[given:len(sizes) - len(TURNED)]:
                    next(stream)
                pe.wait_ge(o_taken, n * 2 + 3)
                for s, (t0, t1) in enumerate(TURNED):
                    next(stream, None)
                    dst = score_bank[(PIECES + s) % RING]
                    pe.wait_ge(slot_taken, n * SLOTS + PIECES + s + 1)
                    for t in range(t0, t1):
                        last = nc.tensor.transpose(dst[:, (t - t0) * P:(t - t0 + 1) * P],
                                                   o_cols[:, t * P:(t + 1) * P], ident[:, :])
                    last.then_inc(slot_filled, 1)
                for _ in stream:
                    pass

            pe.wait_ge(parts_ready, 4 + CREDIT)
            pe.wait_ge(v_stored, 4 + CREDIT)
            for u, idx in [(0, i) for i in range(KT * HG)] + [(1, i) for i in range(SKEW)]:
                for _ in max_unit(0, u, idx):
                    pass
            with pe.Fori(0, TURNS) as turn:
                for u in range(PER_TURN):
                    group(turn, u, 2)
            group(TURNS, 0, 1)
            group(TURNS, 1, 0)

        @block.scalar
        def _(act):
            act.sem_inc(xn_t_ready, CREDIT)
            act.sem_inc(v_stored, CREDIT)
            act.sem_inc(o_taken, 1)
            act.sem_inc(slot_taken, RING)
            def standard_deviations(b):
                act.wait_ge(var_ready, b + 1)
                part = slice(b * KT, (b + 1) * KT)
                nc.scalar.activation(std[:, part], var_eps[:, part], ACT.Sqrt).then_inc(std_ready, 1)

            standard_deviations(0)
            for b in range(B):
                for half in range(2):
                    act.wait_ge(xn_transposed, b * 2 + half + 1 + CREDIT)
                    nc.scalar.activation(xn_t[:, half, :], bank(4 * half), ACT.Copy).then_inc(xn_t_ready, 1)
                if b == 0:
                    standard_deviations(1)
                for half in range(2):
                    bt, bq, bk, bv = (bank(4 * half + i) for i in range(4))
                    act.wait_ge(q_projected, b * 2 + half + 1)
                    nc.scalar.activation(parts[b][:, half, 0, 0, :], bq, ACT.Copy).then_inc(high_ready, 1)
                    act.wait_ge(k_projected, b * 2 + half + 1)
                    nc.scalar.activation(parts[b][:, half, 1, 0, :], bk, ACT.Copy).then_inc(high_ready, 1)
                    act.wait_ge(v_projected, b * 2 + half + 1)
                    for j in range(CH):
                        last = nc.scalar.activation(
                            v_all[:, b * NG:(b + 1) * NG, half * CH + j, :],
                            bv[:, j * P:(j + 1) * P].rearrange("p (g c) -> p g c", g=NG), ACT.Copy)
                    last.then_inc(v_stored, 1)

            def group(n):
                for idx, (j, h) in enumerate(units()):
                    if h == 0:
                        act.wait_ge(pv_done, n * KT + j + 1)
                    for piece, (a, z) in enumerate(pieces(T - P * j)):
                        k = PIECES_BEFORE[idx] + piece
                        act.wait_ge(slot_filled, n * SLOTS + k + 1)
                        nc.scalar.activation(probs[j % 2][:, h, a:z], score_bank[k % RING][:, 0:z - a],
                                             ACT.Exp).then_inc(slot_taken, 1)
                act.wait_ge(pv_done, n * KT + KT + CREDIT)
                for c in range(2):
                    nc.scalar.activation(o_cols[:, c * BANK:(c + 1) * BANK], o_bank[c], ACT.Copy
                                         ).then_inc(o_taken, 1)
                for s, (t0, t1) in enumerate(TURNED):
                    act.wait_ge(slot_filled, n * SLOTS + PIECES + s + 1)
                    nc.scalar.activation(
                        o_raw[:, bass.ds(n + 1, 1), t0 * HG:t1 * HG, :].rearrange("p g j d -> p (g j) d"),
                        score_bank[(PIECES + s) % RING][:, 0:(t1 - t0) * P].rearrange(
                            "p (j d) -> p j d", d=HQ)[:, :, 0:HD + 1],
                        ACT.Copy).then_inc(slot_taken, 1)

            with act.Fori(0, TURNS) as turn:
                for u in range(PER_TURN):
                    group(turn * PER_TURN + u)
            group(GROUPS - 2)
            group(GROUPS - 1)

        @block.vector
        def _(dve):
            step = Count()
            dve.sem_inc(parts_ready, CREDIT)
            dve.sem_inc(max_taken, RING)
            dve.wait_ge(weights_loaded, 16 * 6)
            nc.vector.tensor_tensor(dirs_scaled[:, :].rearrange("o (h d) -> o h d", d=HD),
                                    dirs_sb[:, :].rearrange("o (h d) -> o h d", d=HD),
                                    scales_sb[:, :].unsqueeze(2).broadcast_to([1, H, HD]),
                                    ALU.mult).then_inc(dirs_scaled_ready, 1)

            def variances(b):
                tiles = range(b * KT, (b + 1) * KT)
                for t in tiles:
                    nc.vector.bn_stats(stats[:, t, :], x_sb[:, t, :]).then_inc(vector_steps, step.one())
                dve.wait_ge(vector_steps, step.now())
                for t in tiles:
                    nc.vector.bn_aggr(mean_var[:, t, :], stats[:, t, :]).then_inc(vector_steps, step.one())
                dve.wait_ge(vector_steps, step.now())
                nc.vector.tensor_scalar(var_eps[:, b * KT:(b + 1) * KT], mean_var[:, b * KT:(b + 1) * KT, 1],
                                        EPS, None, ALU.add).then_inc(var_ready, 1)

            def normalise_tokens(b):
                dve.wait_ge(std_ready, b + 1)
                nc.vector.reciprocal(rstd[:, b * KT:(b + 1) * KT], std[:, b * KT:(b + 1) * KT]
                                     ).then_inc(vector_steps, step.one())
                dve.wait_ge(vector_steps, step.now())
                for half in range(2):
                    dve.wait_ge(xn_transposed, b * 2 + half + 1)
                    for j in range(CH):
                        t = b * KT + half * CH + j
                        last = nc.vector.tensor_scalar(xn_stage[:, half, j, :], x_sb[:, t, :],
                                                       mean_var[:, t, 0:1], rstd[:, t:t + 1],
                                                       ALU.subtract, ALU.mult)
                    last.then_inc(xn_ready, 1)

            dve.wait_ge(x_loaded, 32)
            variances(0)
            dve.wait_ge(outer_ready, 1)
            dve.wait_ge(consts_ready, 1)
            nc.vector.tensor_tensor(fold[:, :], bank(0)[:, 0:C],
                                    same_head[:, :, :].rearrange("p h d -> p (h d)"), ALU.mult
                                    ).then_inc(vector_steps, step.one())
            dve.wait_ge(vector_steps, step.now())
            nc.vector.scalar_tensor_tensor(fold[:, :], ident[:, :], SCALE, fold[:, :], ALU.mult, ALU.add
                                           ).then_inc(fold_ready, 1)
            dve.wait_ge(wq_folded, 1)
            nc.vector.tensor_copy(wq_fold[:, :], bank(1)[:, 0:C]).then_inc(wq_fold_ready, 1)
            normalise_tokens(0)
            variances(1)
            normalise_tokens(1)
            for b in range(B):
                for half in range(2):
                    for qk in range(2):
                        src = bank(4 * half + 1 + qk)
                        high, mid, low = (parts[b][:, half, qk, i, :] for i in range(3))
                        left = rest[:, half, qk, :]
                        dve.wait_ge(high_ready, b * 4 + half * 2 + qk + 1)
                        nc.vector.tensor_tensor(left, src, high, ALU.subtract
                                                ).then_inc(vector_steps, step.one())
                        dve.wait_ge(vector_steps, step.now())
                        nc.vector.tensor_copy(mid, left).then_inc(vector_steps, step.one())
                        dve.wait_ge(vector_steps, step.now())
                        last = nc.vector.tensor_tensor(low, left, mid, ALU.subtract)
                    last.then_inc(parts_ready, 1)

            def max_unit(m, r, idx):
                j, h = units()[idx]
                i = KT - 1 - j
                for s, (a, z) in enumerate(pieces(T - P * j)):
                    k = PIECES_BEFORE[idx] + s
                    dve.wait_ge(max_filled, m * PIECES + k + 1)
                    nc.vector.tensor_reduce(mx_part[r][:, h * KT + i, s:s + 1], max_bank[k % RING][:, 0:z - a],
                                            AX.X, ALU.max).then_inc(max_taken, 1)

            def split_maxima(m, r):
                dve.wait_ge(max_taken, m * PIECES + PIECES + RING)
                nc.vector.tensor_reduce(mx[:, :], mx_part[r][:, :, :], AX.X, ALU.max
                                        ).then_inc(vector_steps, step.one())
                dve.wait_ge(vector_steps, step.now())
                nc.vector.transpose(mx_t[:, :], mx[:, :]).then_inc(vector_steps, step.one())
                dve.wait_ge(vector_steps, step.now())
                nc.vector.tensor_scalar(mx_neg[:, :], mx_t[:, :], -1.0, None, ALU.mult
                                        ).then_inc(vector_steps, step.one())
                dve.wait_ge(vector_steps, step.now())
                nc.vector.tensor_copy(mx_rows[r][:, 0, :], mx_neg[:, :]).then_inc(vector_steps, step.one())
                dve.wait_ge(vector_steps, step.now())
                nc.vector.tensor_tensor(mx_rest[:, :], mx_neg[:, :], mx_rows[r][:, 0, :], ALU.subtract
                                        ).then_inc(vector_steps, step.one())
                dve.wait_ge(vector_steps, step.now())
                nc.vector.tensor_copy(mx_rows[r][:, 1, :], mx_rest[:, :]).then_inc(vector_steps, step.one())
                dve.wait_ge(vector_steps, step.now())
                nc.vector.tensor_tensor(mx_rows[r][:, 2, :], mx_rest[:, :], mx_rows[r][:, 1, :], ALU.subtract
                                        ).then_inc(rows_split, 1)

            def normalise(slot):
                raw = o_raw[:, bass.ds(slot, 1), :, :].rearrange("p g j d -> p (g j) d")
                dve.wait_ge(vector_steps, step.now())
                dve.wait_ge(slot_taken, slot * SLOTS + RING)
                nc.vector.reciprocal(den[:, :], raw[:, :, HD]).then_inc(vector_steps, step.one())
                dve.wait_ge(vector_steps, step.now())
                nc.vector.tensor_tensor(
                    attn[:, :, bass.ds(slot * (HG * HD), HG * HD)].rearrange("p t (h d) -> p t h d", d=HD),
                    raw[:, :, 0:HD].rearrange("p (t h) d -> p t h d", h=HG),
                    den[:, :].rearrange("p (t h) -> p t h", h=HG).unsqueeze(3).broadcast_to([P, KT, HG, HD]),
                    ALU.mult
                ).then_inc(vector_steps, step.one())

            nc.vector.memset(o_raw[:, 0, :, :], 1.0).then_inc(vector_steps, step.one())
            for idx in range(KT * HG):
                max_unit(0, 0, idx)
            split_maxima(0, 0)
            for idx in range(SKEW):
                max_unit(1, 1, idx)
            with dve.Fori(0, TURNS) as turn:
                step.enter(turn, 8 * PER_TURN)
                for u in range(PER_TURN):
                    n = turn * PER_TURN + u
                    for idx in range(SKEW, KT * HG):
                        if idx == SKEW + HG:
                            normalise(n)
                        max_unit(n + 1, (u + 1) % STACKS, idx)
                    split_maxima(n + 1, (u + 1) % STACKS)
                    for idx in range(SKEW):
                        max_unit(n + 2, (u + 2) % STACKS, idx)
                step.leave(TURNS)
            for idx in range(SKEW, KT * HG):
                if idx == SKEW + HG:
                    normalise(GROUPS - 2)
                max_unit(GROUPS - 1, (GROUPS - 1) % STACKS, idx)
            split_maxima(GROUPS - 1, (GROUPS - 1) % STACKS)
            dve.wait_ge(vector_steps, step.now())
            dve.sem_inc(first_attn_ready, 1)
            normalise(GROUPS - 1)
            for half in range(2):
                dve.wait_ge(first_turned, half + 1)
                nc.vector.tensor_copy(xn_t[:, half, :], max_bank[half]).then_inc(first_attn_t_ready, 1)

            def layer_norm(src):
                for t in range(KT):
                    nc.vector.bn_stats(stats[:, t, :], src(t)).then_inc(vector_steps, step.one())
                dve.wait_ge(vector_steps, step.now())
                for t in range(KT):
                    nc.vector.bn_aggr(mean_var[:, t, :], stats[:, t, :]).then_inc(vector_steps, step.one())
                dve.wait_ge(vector_steps, step.now())
                v, y, e = var_eps[:, 0:KT], rstd[:, 0:KT], std[:, 0:KT]
                nc.vector.tensor_scalar(v, mean_var[:, 0:KT, 1], EPS, None, ALU.add
                                        ).then_inc(vector_steps, step.one())
                dve.wait_ge(vector_steps, step.now())
                nc.vector.tensor_scalar(half_bits[:, :], v.bitcast(U32), 1, None, ALU.logical_shift_right
                                        ).then_inc(vector_steps, step.one())
                dve.wait_ge(vector_steps, step.now())
                nc.vector.tensor_scalar(y.bitcast(U32), half_bits[:, :], -1.0, RSQRT_BITS, ALU.mult, ALU.add
                                        ).then_inc(vector_steps, step.one())
                for _ in range(NEWTON):
                    dve.wait_ge(vector_steps, step.now())
                    nc.vector.scalar_tensor_tensor(e, y, -0.5, y, ALU.mult, ALU.mult
                                                   ).then_inc(vector_steps, step.one())
                    dve.wait_ge(vector_steps, step.now())
                    nc.vector.tensor_tensor(e, e, v, ALU.mult).then_inc(vector_steps, step.one())
                    dve.wait_ge(vector_steps, step.now())
                    nc.vector.scalar_tensor_tensor(y, e, 1.5, y, ALU.add, ALU.mult
                                                   ).then_inc(vector_steps, step.one())
                dve.wait_ge(vector_steps, step.now())

            def first_proj(t):
                return first_proj_bank[t // CH][:, t % CH * P:(t % CH + 1) * P]

            dve.wait_ge(first_projected, 2)
            layer_norm(first_proj)
            for t in range(KT):
                nc.vector.tensor_scalar(xn_stage[:, t // CH, t % CH, :], first_proj(t), mean_var[:, t, 0:1],
                                        rstd[:, t:t + 1], ALU.subtract, ALU.mult
                                        ).then_inc(vector_steps, step.one())
            dve.wait_ge(vector_steps, step.now())
            nc.vector.tensor_tensor(x_sb[:, 0:KT, :], x_sb[:, 0:KT, :],
                                    xn_stage[:, :, :, :].rearrange("p h j c -> p (h j) c"), ALU.add
                                    ).then_inc(vector_steps, step.one())
            dve.wait_ge(vector_steps, step.now())
            layer_norm(lambda t: x_sb[:, t, :])
            for t in range(KT):
                last = nc.vector.tensor_scalar(x2[:, t, :], x_sb[:, t, :], mean_var[:, t, 0:1],
                                               rstd[:, t:t + 1], ALU.subtract, ALU.mult)
                if t % CH == CH - 1:
                    last.then_inc(x2_ready, 1)
            for q in range(2):
                dve.wait_ge(x2_transposed, q + 1)
                nc.vector.tensor_copy(x2_t[:, q * CH:(q + 1) * CH, :].rearrange("p t c -> p (t c)"),
                                      first_x2_bank[q]).then_inc(x2_t_ready, 1)
            dve.wait_ge(first_logits_done, 1)
            nc.vector.tensor_copy(logits[:, 0:KT, 0:E],
                                  first_lg_bank[:, 0:KT * 8].rearrange("p (t e) -> p t e", e=8)[:, :, 0:E]
                                  ).then_inc(vector_steps, step.one())
            normalise(GROUPS)

        front.close()
        w_g = sb("w_g", [C, NE, HID])
        w_u = sb("w_u", [C, NE, HID])
        w_d = sb("w_d", [P, NE, HT, C])
        proj = sb("proj", [P, KT, C])
        attn_t = sb("attn_t", [C, 2, BANK])
        mixed = sb("mixed", [P, NT, C])
        weight = sb("weight", [P, 2, NT])
        upper = sb("upper", [P, P], BF16)
        ones_b = sb("ones_b", [P, P], BF16)
        zeros2 = sb("zeros2", [P, P])
        top = sb("top", [P, NT, 8])
        top_at = sb("top_at", [P, NT, 8], U32)
        iota = sb("iota", [P, P])
        iota_p = sb("iota_p", [P, 1])
        iota_ct = sb("iota_ct", [P, 2 * NT])
        spare_at = sb("spare_at", [P, TILES])
        thresholds = sb("thresholds", [P, NT])
        top_at_f = sb("top_at_f", [P, NT, 2])
        gap = sb("gap", [P, NT])
        gap_exp = sb("gap_exp", [P, NT])
        gap_sum = sb("gap_sum", [P, NT])
        pick = [sb(f"pick{i}", [P, E, NT]) for i in range(2)]
        picked = sb("picked", [P, E, NT], BF16)
        before = [sb(f"before{i}", [P, E, KT + NT]) for i in range(2)]
        over = sb("over", [P, E, NT])
        ends = [sb(f"ends{i}", [P, 4 + E]) for i in range(2)]
        slot_in = sb("slot_in", [P, E, NT])
        slot_all = sb("slot_all", [P, E, NT])
        slot_pick = [sb(f"slot_pick{i}", [P, E, NT]) for i in range(2)]
        slot_f = sb("slot_f", [P, 2, NT])
        slot_u = sb("slot_u", [P, 2 * NT], U32)
        slot_part = sb("slot_part", [P, 2, 2 * NT], U32)
        slot_part_f = sb("slot_part_f", [P, 2, 2 * NT])
        row_hot = sb("row_hot", [P, 2 * NT, P], BF16)
        tile_hot = sb("tile_hot", [P, 2 * NT, 3, TILES], BF16)
        table = sb("table", [P, 3, TILES])
        spare = sb("spare", [P, TILES])
        place_f = sb("place_f", [P, TILES])
        place_u = sb("place_u", [P, TILES], U32)
        source = sb("source", [P, TILES], U32)
        target = sb("target", [P, TILES], U32)
        passed = sb("passed", [1, PADDED, E])
        tile_f = sb("tile_f", [1, PADDED])
        words_f = sb("words_f", [1, WORDS])
        words = sb("words", [1, WORDS], U32)
        s_gate = [sb(f"s_gate{i}", [P, BANK]) for i in range(2)]
        s_up = [sb(f"s_up{i}", [P, BANK]) for i in range(2)]
        s_hidden = [sb(f"s_hidden{i}", [P, HT, BANK]) for i in range(2)]
        source_now = [sb(f"source_now{i}", [P, 1], U32) for i in range(2)]
        target_now = [sb(f"target_now{i}", [P, 1], U32) for i in range(2)]
        rows = [sb(f"rows{i}", [P, C]) for i in range(2)]
        rows_t = [sb(f"rows_t{i}", [C, P]) for i in range(2)]
        gate = [sb(f"gate{i}", [P, HID]) for i in range(2)]
        hidden = [sb(f"hidden{i}", [P, HID]) for i in range(2)]
        hidden_t = [sb(f"hidden_t{i}", [P, HT, P]) for i in range(2)]
        result = [sb(f"result{i}", [P, C]) for i in range(2)]
        root_table = sb("root_table", [P, 1])
        back = [sb(f"back{i}", [P, NT, C]) for i in range(2)]

        route_consts = sem("route_consts")
        shared_loaded = sem("shared_loaded")
        experts_loaded = sem("experts_loaded")
        attn_transposed = sem("attn_transposed")
        attn_t_ready = sem("attn_t_ready")
        projected = sem("projected")
        proj_ready = sem("proj_ready")
        tokens_stored = sem("tokens_stored")
        logits_done = sem("logits_done")
        gap_ready = sem("gap_ready")
        gap_exp_ready = sem("gap_exp_ready")
        picked_ready = sem("picked_ready")
        counted = sem("counted")
        hot_ready = sem("hot_ready")
        table_done = sem("table_done")
        places_ready = sem("places_ready")
        words_ready = sem("words_ready")
        steps = sem("steps")
        s_gate_done = sem("s_gate_done")
        s_up_done = sem("s_up_done")
        s_gate_ready = sem("s_gate_ready")
        s_up_ready = sem("s_up_ready")
        s_hidden_ready = sem("s_hidden_ready")
        s_last_ready = sem("s_last_ready")
        s_down_done = sem("s_down_done")
        s_down_taken = sem("s_down_taken")
        rows_loaded = [sem(f"rows_loaded{i}") for i in range(2)]
        copied = sem("copied")
        offsets_in_place = sem("offsets_in_place")
        rows_turned = sem("rows_turned")
        rows_t_ready = sem("rows_t_ready")
        gate_done = sem("gate_done")
        up_done = sem("up_done")
        gate_ready = sem("gate_ready")
        hidden_ready = sem("hidden_ready")
        hidden_turned = sem("hidden_turned")
        hidden_t_ready = sem("hidden_t_ready")
        down_done = sem("down_done")
        result_ready = sem("result_ready")
        result_stored = [sem(f"result_stored{i}") for i in range(2)]
        returned = [sem(f"returned{q}") for q in range(NT // CH)]
        fin_var = sem("fin_var")
        fin_std = sem("fin_std")
        half_done = [sem(f"half_done{b}") for b in range(B)]
        weight_ready = sem("weight_ready")
        weighted = sem("weighted")
        pool_mixed = sem("pool_mixed")
        first_scaled = sem("first_scaled")
        out_stored = sem("out_stored")
        CHUNKS = NT // CH
        QC = KT // CH
        PAIRS = (TILES - TAIL) // 2
        LAST = TILES - TAIL

        with nc.Block() as block:
            at_bank, pr_bank = [bank(0), bank(1)], [bank(2), bank(3)]
            g_bank, u_bank = [bank(0), bank(1)], [bank(2), bank(3)]
            xt_bank = turn_bank = [bank(4), bank(5)]
            d_bank, t_bank = bank(6), bank(7)
            cut = NT * 8
            lg_bank, t_out = t_bank[:, 0:cut], t_bank[:, 2 * P:2 * P + 3 * TILES]
            total_bank = t_bank[:, cut:cut + E * NT]
            rank_bank = t_bank[:, 2 * P + 3 * TILES:2 * P + 3 * TILES + E * NT]

            @block.sync
            def _(sp):
                for e in [E] + list(range(E)):
                    loaded = shared_loaded if e == E else experts_loaded
                    sp.dma_start(w_g[:, e, :], w_gate[e]).then_inc(loaded, 16)
                    sp.dma_start(w_u[:, e, :], w_up[e]).then_inc(loaded, 16)
                    sp.dma_start(w_d[:, e, :, :], w_down[e].rearrange("(t p) c -> p t c", p=P)
                                 ).then_inc(loaded, 16)
                for b in range(B):
                    sp.wait_ge(x2_ready, (b + 1) * QC)
                    sp.dma_start(tokens[b * T:(b + 1) * T, :].rearrange("(t p) c -> p t c", p=P),
                                 x2[:, b * KT:(b + 1) * KT, :]).then_inc(tokens_stored, 16)
                for i in range(2):
                    sp.wait_ge(result_stored[i], 16 * (TILES // 2))
                for q in range(CHUNKS):
                    for i in range(2):
                        at = i * B * T + q * BANK
                        sp.dma_start(back[i][:, q * CH:(q + 1) * CH, :],
                                     results[at:at + BANK, :].rearrange("(t p) c -> p t c", p=P)
                                     ).then_inc(returned[q], 16)
                sp.wait_ge(half_done[0], 1)
                sp.dma_start(out[0].rearrange("(t p) c -> p t c", p=P), mixed[:, 0:KT, :]
                             ).then_inc(out_stored, 16)
                for q in range(QC):
                    sp.wait_ge(half_done[1], q + 1)
                    sp.dma_start(out[1][q * BANK:(q + 1) * BANK, :].rearrange("(t p) c -> p t c", p=P),
                                 mixed[:, KT + q * CH:KT + (q + 1) * CH, :]).then_inc(out_stored, 16)
                sp.wait_ge(out_stored, 16 * (1 + QC))

            @block.gpsimd
            def _(pool):
                for dst, pattern, base, down in ((iota[:, :], [[1, P]], 0, 0), (iota_p[:, :], [[0, 1]], 0, 1),
                                                 (iota_ct[:, :], [[1, 2 * NT]], 0, 0),
                                                 (spare_at[:, :], [[P, TILES]], 2 * B * T, 1),
                                                 (thresholds[:, :], [[P, NT]], 0, 0)):
                    nc.gpsimd.iota(dst, pattern=pattern, base=base, channel_multiplier=down,
                                   allow_small_or_imprecise_dtypes=True).then_inc(route_consts, 1)
                nc.gpsimd.memset(zeros2[:, :], 0.0).then_inc(route_consts, 1)
                nc.gpsimd.memset(ones_b[:, :], 1.0).then_inc(route_consts, 1)
                pool.wait_ge(route_consts, 7)
                nc.gpsimd.affine_select(out=upper[:, :], in_=zeros2[:, :], compare_op=ALU.is_ge, fill=1.0,
                                        base=0, pattern=[[-1, P]], channel_multiplier=1
                                        ).then_inc(route_consts, 1)
                for q in range(CHUNKS - 1):
                    if q >= 2:
                        pool.wait_ge(s_down_done, q - 1)
                    for t in range(HT):
                        pool.wait_ge(s_up_ready, q * HT + t + 1)
                        nc.gpsimd.tensor_tensor(s_hidden[q % 2][:, t, :], s_up[t % 2][:, :],
                                                s_gate[t % 2][:, :], ALU.mult).then_inc(s_hidden_ready, 1)

                def gather(pair, u, count):
                    k, i = pair * 2 + u, u % 2
                    pool.wait_ge(rows_turned, k + 1)
                    nc.gpsimd.tensor_copy(source_now[i][:, :], source[:, bass.ds(k, 1)]).then_inc(copied, 1)
                    pool.wait_ge(copied, count)
                    pool.sem_inc(offsets_in_place, 1)
                    nc.gpsimd.indirect_dma_start(
                        rows[i][:, :], None, tokens,
                        bass.IndirectOffsetOnAxis(ap=source_now[i][:, 0:1], axis=0)
                    ).then_inc(rows_loaded[i], 16)

                def scatter(pair, u, count):
                    k, i = pair * 2 + u, u % 2
                    pool.wait_ge(result_ready, k + 1 + 1)
                    nc.gpsimd.tensor_copy(target_now[i][:, :], target[:, bass.ds(k, 1)]).then_inc(copied, 1)
                    pool.wait_ge(copied, count)
                    pool.sem_inc(offsets_in_place, 1)
                    nc.gpsimd.indirect_dma_start(
                        results, bass.IndirectOffsetOnAxis(ap=target_now[i][:, 0:1], axis=0),
                        result[i][:, :], None).then_inc(result_stored[i], 16)

                pool.wait_ge(tokens_stored, 16 * B)
                pool.wait_ge(places_ready, 2)
                AHEAD = 4
                for u in range(AHEAD):
                    gather(0, u, u + 1)
                with pool.Fori(0, PAIRS - 1) as pair:
                    for u in range(2):
                        gather(pair, u + AHEAD, pair * 4 + (AHEAD + 2 * u + 1))
                        scatter(pair, u, pair * 4 + (AHEAD + 2 * u + 2))
                for u in range(AHEAD):
                    scatter(PAIRS - 1, u, (PAIRS - 1) * 4 + AHEAD + u + 1)
                for q in range(QC, CHUNKS):
                    for i in range(2):
                        n, part = (q - QC) * 2 + i, slice(q * CH, (q + 1) * CH)
                        if n > 0:
                            pool.wait_ge(pool_mixed, n)
                        pool.wait_ge(weighted, n + 1)
                        nc.gpsimd.tensor_tensor(mixed[:, part, :], mixed[:, part, :], back[i][:, part, :],
                                                ALU.add).then_inc(pool_mixed, 1)
                pool.wait_ge(first_scaled, 1)
                nc.gpsimd.tensor_tensor(mixed[:, 0:KT, :], mixed[:, 0:KT, :], x_sb[:, 0:KT, :], ALU.add
                                        ).then_inc(half_done[0], 1)

            @block.tensor
            def _(pe):
                pe.sem_inc(rows_turned, CREDIT)
                for half in range(2):
                    for j in range(CH):
                        first = HG * HD + C
                        last = nc.tensor.transpose(at_bank[half][:, j * P:(j + 1) * P],
                                                   attn[:, half * CH + j, first:first + C], ident[:, :])
                    last.then_inc(attn_transposed, 1)
                for half in range(2):
                    pe.wait_ge(attn_t_ready, half + 1)
                    for j in range(CH):
                        last = nc.tensor.matmul(pr_bank[half][:, j * P:(j + 1) * P],
                                                attn_t[:, half, j * P:(j + 1) * P], w_out_sb[:, :],
                                                start=True, stop=True)
                    last.then_inc(projected, 1)

                def turn_tokens(q):
                    pe.wait_ge(x2_ready, q + 1)
                    for j in range(CH):
                        last = nc.tensor.transpose(xt_bank[q % 2][:, j * P:(j + 1) * P],
                                                   x2[:, q * CH + j, :], ident[:, :])
                    last.then_inc(x2_transposed, 1)

                def route(q):
                    pe.wait_ge(x2_t_ready, q + 1)
                    for t in range(q * CH, (q + 1) * CH):
                        last = nc.tensor.matmul(lg_bank[:, t * 8:t * 8 + E], x2_t[:, t, :], router_sb[:, :],
                                                start=True, stop=True)
                    last.then_inc(logits_done, 1)

                def shared_up(q, ts):
                    x_at = x2_t[:, q * CH:(q + 1) * CH, :].rearrange("c t p -> c (t p)")
                    for t in ts:
                        if q == CHUNKS - 1 and t >= 2:
                            pe.wait_ge(s_last_ready, t - 1)
                        elif q * HT + t >= 2:
                            pe.wait_ge(s_up_ready, q * HT + t - 1)
                        nc.tensor.matmul(g_bank[t % 2], w_g[:, E, t * P:(t + 1) * P], x_at,
                                         start=True, stop=True).then_inc(s_gate_done, 1)
                        nc.tensor.matmul(u_bank[t % 2], w_u[:, E, t * P:(t + 1) * P], x_at,
                                         start=True, stop=True).then_inc(s_up_done, 1)

                def shared_down(q):
                    if q < CHUNKS - 1:
                        pe.wait_ge(s_hidden_ready, (q + 1) * HT)
                    else:
                        pe.wait_ge(s_last_ready, HT)
                    if q >= 1:
                        pe.wait_ge(s_down_taken, q)
                    for j in range(CH):
                        for t in range(HT):
                            last = nc.tensor.matmul(
                                d_bank[:, j * P:(j + 1) * P],
                                s_hidden[q % 2][:, t, j * P:(j + 1) * P], w_d[:, E, t, :],
                                start=(t == 0), stop=(t == HT - 1))
                    last.then_inc(s_down_done, 1)

                pe.wait_ge(shared_loaded, 16 * 3)
                pe.wait_ge(proj_ready, 2)
                shared_up(0, range(HT))
                shared_up(1, [0])
                shared_down(0)
                shared_up(1, [1])
                turn_tokens(2)
                turn_tokens(3)
                route(2)
                route(3)
                shared_up(1, [2, 3])
                shared_up(2, [0])
                pe.wait_ge(picked_ready, 1)
                pe.wait_ge(route_consts, 8)
                flat = picked[:, :, :].rearrange("p e t -> p (e t)")
                nc.tensor.matmul(rank_bank, upper[:, :], flat, start=True, stop=True).then_inc(counted, 1)
                nc.tensor.matmul(total_bank, ones_b[:, :], flat, start=True, stop=True).then_inc(counted, 1)
                shared_down(1)
                shared_up(2, [1, 2, 3])
                shared_up(3, [0])
                shared_down(2)
                for k in range(2 * NT):
                    if k % NT == 0:
                        pe.wait_ge(hot_ready, k // NT + 1)
                    last = nc.tensor.matmul(t_out, row_hot[:, k, :],
                                            tile_hot[:, k, :, :].rearrange("p v a -> p (v a)"),
                                            start=(k == 0), stop=(k == 2 * NT - 1))
                last.then_inc(table_done, 1)
                shared_up(3, [1, 2, 3])

                def word(turn):
                    return pe.value_load(words[0:1, bass.ds(turn, 1)], min_val=0, max_val=8 ** (PACK + 1) - 1)

                def digit(w, u):
                    return (w >> (3 * u)) & 7

                def turn(k, u):
                    i = u % 2
                    pe.wait_ge(rows_loaded[i], k * 8 + (u // 2 + 1) * 16)
                    pe.wait_ge(rows_t_ready, k + (u + 1))
                    nc.tensor.transpose(t_bank[:, i * P:(i + 1) * P], rows[i][:, :], ident[:, :]
                                        ).then_inc(rows_turned, 1)

                def turn_hidden(k, u):
                    i = u % 2
                    pe.wait_ge(hidden_ready, k + (u + 1 + CREDIT))
                    pe.wait_ge(hidden_t_ready, k + (u + 1))
                    for t in range(HT):
                        last = nc.tensor.transpose(turn_bank[i][:, t * P:(t + 1) * P],
                                                   hidden[i][:, t * P:(t + 1) * P], ident[:, :])
                    last.then_inc(hidden_turned, 1)

                def up(k, u, e):
                    i = u % 2
                    pe.wait_ge(rows_t_ready, k + (u + 1 + 1))
                    pe.wait_ge(hidden_ready, k + (u + 1))
                    nc.tensor.matmul(g_bank[i], rows_t[i][:, :],
                                     w_g[:, bass.ds(e, 1), :].rearrange("c e h -> c (e h)"),
                                     start=True, stop=True).then_inc(gate_done, 1)
                    nc.tensor.matmul(u_bank[i], rows_t[i][:, :],
                                     w_u[:, bass.ds(e, 1), :].rearrange("c e h -> c (e h)"),
                                     start=True, stop=True).then_inc(up_done, 1)

                def project(k, u, e):
                    i = u % 2
                    pe.wait_ge(hidden_t_ready, k + (u + 1 + CREDIT))
                    pe.wait_ge(result_ready, k + (u + 1))
                    for t in range(HT):
                        last = nc.tensor.matmul(d_bank[:, 0:P], hidden_t[i][:, t, :],
                                                w_d[:, bass.ds(e, 1), t, :].rearrange("p e c -> p (e c)"),
                                                start=(t == 0), stop=(t == HT - 1))
                    last.then_inc(down_done, 1)

                pe.wait_ge(places_ready, 2)
                turn(0, 0)
                turn(0, 1)
                shared_down(CHUNKS - 1)
                pe.wait_ge(words_ready, 1)
                pe.wait_ge(experts_loaded, 16 * 3 * E)
                first_expert = digit(word(0), 0)
                up(0, 0, first_expert)
                pe.wait_ge(s_down_taken, CHUNKS)
                with pe.Fori(0, (TILES - TAIL) // PACK) as n:
                    w, k = word(n), n * PACK
                    for u in range(PACK):
                        turn(k, u + 2)
                        turn_hidden(k, u)
                        up(k, u + 1, digit(w, u + 1))
                        project(k, u, digit(w, u))
                w = word(WORDS - 1)
                turn_hidden(LAST, 0)
                up(LAST, 1, digit(w, 1))
                project(LAST, 0, digit(w, 0))
                turn_hidden(LAST, 1)
                project(LAST, 1, digit(w, 1))

            @block.scalar
            def _(act):
                act.sem_inc(rows_t_ready, 1)
                act.sem_inc(hidden_t_ready, CREDIT)
                for half in range(2):
                    act.wait_ge(attn_transposed, half + 1)
                    nc.scalar.activation(attn_t[:, half, :], at_bank[half], ACT.Copy
                                         ).then_inc(attn_t_ready, 1)
                for half in range(2):
                    act.wait_ge(projected, half + 1)
                    nc.scalar.activation(proj[:, half * CH:(half + 1) * CH, :].rearrange("p t c -> p (t c)"),
                                         pr_bank[half], ACT.Copy).then_inc(proj_ready, 1)

                def standard_deviations(n, at, count):
                    act.wait_ge(post_var_ready, n + 1)
                    nc.scalar.activation(std[:, at:at + count], var_eps[:, at:at + count], ACT.Sqrt
                                         ).then_inc(post_std_ready, 1)

                def copy_tokens(q):
                    act.wait_ge(x2_transposed, q + 1)
                    nc.scalar.activation(x2_t[:, q * CH:(q + 1) * CH, :].rearrange("p t c -> p (t c)"),
                                         xt_bank[q % 2], ACT.Copy).then_inc(x2_t_ready, 1)

                def shared_take(q, ts):
                    for t in ts:
                        if q == CHUNKS - 1 and t >= 2:
                            act.wait_ge(s_last_ready, t - 1)
                        elif q * HT + t >= 2:
                            act.wait_ge(s_hidden_ready, q * HT + t - 1)
                        act.wait_ge(s_gate_done, q * HT + t + 1)
                        nc.scalar.activation(s_gate[t % 2][:, :], g_bank[t % 2], ACT.Silu
                                             ).then_inc(s_gate_ready, 1)
                        if q == CHUNKS - 1:
                            continue
                        act.wait_ge(s_up_done, q * HT + t + 1)
                        nc.scalar.activation(s_up[t % 2][:, :], u_bank[t % 2], ACT.Copy
                                             ).then_inc(s_up_ready, 1)

                def shared_result(q):
                    act.wait_ge(s_down_done, q + 1)
                    nc.scalar.activation(mixed[:, q * CH:(q + 1) * CH, :].rearrange("p t c -> p (t c)"),
                                         d_bank, ACT.Copy).then_inc(s_down_taken, 1)

                shared_take(0, [0])
                standard_deviations(0, KT, KT)
                shared_take(0, [1, 2, 3])
                standard_deviations(1, KT, KT)
                shared_take(1, [0])
                shared_result(0)
                shared_take(1, [1])
                copy_tokens(2)
                copy_tokens(3)
                shared_take(1, [2, 3])
                shared_take(2, [0])
                shared_result(1)
                act.wait_ge(gap_ready, 1)
                nc.scalar.activation(gap_exp[:, :], gap[:, :], ACT.Exp).then_inc(gap_exp_ready, 1)
                shared_take(2, [1, 2, 3])
                shared_take(3, [0])
                shared_result(2)
                shared_take(3, [1, 2, 3])

                def copy_rows(pair, u):
                    k, i = pair * 2 + u, u % 2
                    act.wait_ge(rows_turned, k + 1 + CREDIT)
                    nc.scalar.activation(rows_t[i][:, :], t_bank[:, i * P:(i + 1) * P], ACT.Copy
                                         ).then_inc(rows_t_ready, 1)

                def gate_rows(pair, u):
                    k, i = pair * 2 + u, u % 2
                    act.wait_ge(gate_done, k + 1)
                    act.wait_ge(hidden_ready, k + 1)
                    nc.scalar.activation(gate[i][:, :], g_bank[i], ACT.Silu).then_inc(gate_ready, 1)

                def copy_hidden(pair, u):
                    k, i = pair * 2 + u, u % 2
                    act.wait_ge(hidden_turned, k + 1)
                    nc.scalar.activation(hidden_t[i][:, :, :].rearrange("p t c -> p (t c)"), turn_bank[i],
                                         ACT.Copy).then_inc(hidden_t_ready, 1)

                copy_rows(0, 0)
                copy_rows(0, 1)
                shared_result(CHUNKS - 1)
                gate_rows(0, 0)
                with act.Fori(0, PAIRS) as pair:
                    for u in range(2):
                        copy_rows(pair, u + 2)
                        copy_hidden(pair, u)
                        gate_rows(pair, u + 1)
                copy_hidden(PAIRS, 0)
                gate_rows(PAIRS, 1)
                copy_hidden(PAIRS, 1)
                act.wait_ge(weight_ready, 1)
                nc.scalar.activation(root_table[:, :], weight[:, 0, 0:1], ACT.Sqrt)
                for q in range(QC, CHUNKS):
                    act.wait_ge(returned[q], 32)
                    for i in range(2):
                        for t in range(q * CH, (q + 1) * CH):
                            last = nc.scalar.activation(back[i][:, t, :], back[i][:, t, :], ACT.Copy,
                                                        scale=weight[:, i, t:t + 1])
                        last.then_inc(weighted, 1)
                for b in range(B):
                    act.wait_ge(fin_var, b + 1)
                    nc.scalar.activation(std[:, b * KT:(b + 1) * KT], var_eps[:, b * KT:(b + 1) * KT], ACT.Sqrt
                                         ).then_inc(fin_std, 1)

            @block.vector
            def _(dve):
                step = Count()
                dve.sem_inc(hidden_ready, CREDIT)
                dve.sem_inc(result_ready, 1)

                def done():
                    dve.wait_ge(steps, step.now())

                nc.vector.memset(logits[:, :, E:8], NEG).then_inc(steps, step.one())
                for buf in before + ends:
                    nc.vector.memset(buf[:], 0.0).then_inc(steps, step.one())

                def layer_norm(src, at, count, var_sem, std_sem, n):
                    part = slice(at, at + count)
                    for t in range(at, at + count):
                        nc.vector.bn_stats(stats[:, t, :], src(t)).then_inc(steps, step.one())
                    done()
                    for t in range(at, at + count):
                        nc.vector.bn_aggr(mean_var[:, t, :], stats[:, t, :]).then_inc(steps, step.one())
                    done()
                    nc.vector.tensor_scalar(var_eps[:, part], mean_var[:, part, 1], EPS, None, ALU.add
                                            ).then_inc(var_sem, 1)
                    dve.wait_ge(std_sem, n)
                    nc.vector.reciprocal(rstd[:, part], std[:, part]).then_inc(steps, step.one())
                    done()

                dve.wait_ge(proj_ready, 2)
                layer_norm(lambda t: proj[:, t - KT, :], KT, KT, post_var_ready, post_std_ready, 1)
                for t in range(KT, NT):
                    nc.vector.tensor_scalar(proj[:, t - KT, :], proj[:, t - KT, :], mean_var[:, t, 0:1],
                                            rstd[:, t:t + 1], ALU.subtract, ALU.mult
                                            ).then_inc(steps, step.one())
                done()
                nc.vector.tensor_tensor(x_sb[:, KT:, :], x_sb[:, KT:, :], proj[:, :, :], ALU.add
                                        ).then_inc(steps, step.one())
                done()
                layer_norm(lambda t: x_sb[:, t, :], KT, KT, post_var_ready, post_std_ready, 2)
                for t in range(KT, NT):
                    last = nc.vector.tensor_scalar(x2[:, t, :], x_sb[:, t, :], mean_var[:, t, 0:1],
                                                   rstd[:, t:t + 1], ALU.subtract, ALU.mult)
                    if t % CH == CH - 1:
                        last.then_inc(x2_ready, 1)
                dve.wait_ge(logits_done, QC)
                nc.vector.tensor_copy(logits[:, KT:, 0:E],
                                      lg_bank.rearrange("p (t e) -> p t e", e=8)[:, KT:, 0:E]
                                      ).then_inc(steps, step.one())
                done()
                for t in range(NT):
                    nc.vector.max(top[:, t, :], logits[:, t, :]).then_inc(steps, step.one())
                done()
                nc.vector.tensor_tensor(gap[:, :], top[:, :, 1], top[:, :, 0], ALU.subtract
                                        ).then_inc(gap_ready, 1)
                for t in range(NT):
                    nc.vector.max_index(top_at[:, t, :], top[:, t, :], logits[:, t, :]
                                        ).then_inc(steps, step.one())
                done()
                nc.vector.tensor_copy(top_at_f[:, :, :], top_at[:, :, 0:2]).then_inc(steps, step.one())
                done()
                dve.wait_ge(route_consts, 8)
                for i in range(2):
                    nc.vector.tensor_tensor(
                        pick[i][:, :, :], iota[:, 0:E].unsqueeze(2).broadcast_to([P, E, NT]),
                        top_at_f[:, :, i].unsqueeze(1).broadcast_to([P, E, NT]), ALU.is_equal
                    ).then_inc(steps, step.one())
                done()
                nc.vector.tensor_tensor(picked[:, :, :], pick[0][:, :, :], pick[1][:, :, :], ALU.add
                                        ).then_inc(picked_ready, 1)
                dve.wait_ge(counted, 2)
                nc.vector.tensor_copy(before[0][:, :, KT:], total_bank.rearrange("p (e t) -> p e t", e=E)
                                      ).then_inc(steps, step.one())
                for i, shift in enumerate((1, 2, 4, 8)):
                    src, dst = before[i % 2], before[(i + 1) % 2]
                    done()
                    nc.vector.tensor_tensor(dst[:, :, KT:], src[:, :, KT:], src[:, :, KT - shift:KT + NT - shift],
                                            ALU.add).then_inc(steps, step.one())
                done()
                sums = before[0]
                nc.vector.tensor_tensor(over[:, :, :], sums[:, :, KT + NT - 1:KT + NT].broadcast_to([P, E, NT]),
                                        thresholds[:, :].unsqueeze(1).broadcast_to([P, E, NT]), ALU.is_gt
                                        ).then_inc(steps, step.one())
                nc.vector.tensor_tensor(slot_in[:, :, :], rank_bank.rearrange("p (e t) -> p e t", e=E),
                                        sums[:, :, KT - 1:KT + NT - 1], ALU.add).then_inc(steps, step.one())
                done()
                nc.vector.tensor_reduce(ends[0][:, 4:], over[:, :, :], AX.X, ALU.add
                                        ).then_inc(steps, step.one())
                for i, shift in enumerate((1, 2, 4)):
                    src, dst = ends[i % 2], ends[(i + 1) % 2]
                    done()
                    nc.vector.tensor_tensor(dst[:, 4:], src[:, 4:], src[:, 4 - shift:4 + E - shift], ALU.add
                                            ).then_inc(steps, step.one())
                done()
                end = ends[1]
                nc.vector.scalar_tensor_tensor(slot_all[:, :, :], end[:, 3:3 + E].unsqueeze(2).broadcast_to([P, E, NT]),
                                               float(P), slot_in[:, :, :], ALU.mult, ALU.add
                                               ).then_inc(steps, step.one())
                done()
                for i in range(2):
                    nc.vector.tensor_tensor(slot_pick[i][:, :, :], slot_all[:, :, :], pick[i][:, :, :], ALU.mult
                                            ).then_inc(steps, step.one())
                done()
                for i in range(2):
                    nc.vector.tensor_reduce(slot_f[:, i, :], slot_pick[i][:, :, :].rearrange("p e t -> p t e"),
                                            AX.X, ALU.add).then_inc(steps, step.one())
                done()
                nc.vector.tensor_copy(slot_u[:, :], slot_f[:, :, :].rearrange("p i t -> p (i t)")
                                      ).then_inc(steps, step.one())
                done()
                nc.vector.tensor_scalar(slot_part[:, 0, :], slot_u[:, :], 7, None, ALU.logical_shift_right
                                        ).then_inc(steps, step.one())
                nc.vector.tensor_scalar(slot_part[:, 1, :], slot_u[:, :], P - 1, None, ALU.bitwise_and
                                        ).then_inc(steps, step.one())
                done()
                nc.vector.tensor_copy(slot_part_f[:, :, :], slot_part[:, :, :]).then_inc(steps, step.one())
                done()
                for i in range(2):
                    part = slice(i * NT, (i + 1) * NT)
                    nc.vector.tensor_tensor(
                        tile_hot[:, part, 2, :], iota[:, 0:TILES].unsqueeze(1).broadcast_to([P, NT, TILES]),
                        slot_part_f[:, 0, part].unsqueeze(2).broadcast_to([P, NT, TILES]), ALU.is_equal
                    ).then_inc(steps, step.one())
                    done()
                    nc.vector.tensor_scalar(tile_hot[:, part, 0, :], tile_hot[:, part, 2, :], iota_p[:, 0:1],
                                            None, ALU.mult).then_inc(steps, step.one())
                    nc.vector.tensor_tensor(
                        tile_hot[:, part, 1, :], tile_hot[:, part, 2, :],
                        iota_ct[:, part].unsqueeze(2).broadcast_to([P, NT, TILES]), ALU.mult
                    ).then_inc(steps, step.one())
                    nc.vector.tensor_tensor(
                        row_hot[:, part, :], iota[:, :].unsqueeze(1).broadcast_to([P, NT, P]),
                        slot_part_f[:, 1, part].unsqueeze(2).broadcast_to([P, NT, P]), ALU.is_equal
                    ).then_inc(steps, step.one())
                    done()
                    nc.vector.memset(spare[:, 0:1], 0.0).then_inc(hot_ready, 1)
                def shared_last(ts):
                    q = CHUNKS - 1
                    dve.wait_ge(s_down_done, q - 1)
                    for t in ts:
                        dve.wait_ge(s_up_done, q * HT + t + 1)
                        dve.wait_ge(s_gate_ready, q * HT + t + 1)
                        nc.vector.tensor_tensor(s_hidden[q % 2][:, t, :], u_bank[t % 2], s_gate[t % 2][:, :],
                                                ALU.mult).then_inc(s_last_ready, 1)

                nc.vector.tensor_tensor(passed[:, :, :], iota[0:1, 0:PADDED].unsqueeze(2).broadcast_to([1, PADDED, E]),
                                        end[0:1, 4:].unsqueeze(1).broadcast_to([1, PADDED, E]), ALU.is_ge
                                        ).then_inc(steps, step.one())
                done()
                nc.vector.tensor_reduce(tile_f[:, :], passed[:, :, :], AX.X, ALU.add
                                        ).then_inc(steps, step.one())
                done()
                nc.vector.tensor_scalar(tile_f[:, :], tile_f[:, :], float(E - 1), None, ALU.min
                                        ).then_inc(steps, step.one())

                def every(i):
                    return tile_f[:, i:i + WORDS * PACK].rearrange("o (w s) -> o w s", s=PACK)[:, :, 0]

                done()
                shared_last([0])
                dve.wait_ge(table_done, 1)
                nc.vector.tensor_copy(table[:, :, :], t_out.rearrange("p (v a) -> p v a", v=3)
                                      ).then_inc(steps, step.one())
                done()
                nc.vector.scalar_tensor_tensor(place_f[:, :], table[:, 1, :], float(P), table[:, 0, :],
                                               ALU.mult, ALU.add).then_inc(steps, step.one())
                nc.vector.tensor_scalar(spare[:, :], table[:, 2, :], -1.0, 1.0, ALU.mult, ALU.add
                                        ).then_inc(steps, step.one())
                done()
                nc.vector.tensor_copy(place_u[:, :], place_f[:, :]).then_inc(steps, step.one())
                nc.vector.tensor_tensor(spare[:, :], spare[:, :], spare_at[:, :], ALU.mult
                                        ).then_inc(steps, step.one())
                done()
                nc.vector.tensor_scalar(source[:, :], place_u[:, :], B * T - 1, None, ALU.bitwise_and
                                        ).then_inc(places_ready, 1)
                nc.vector.tensor_tensor(target[:, :], place_f[:, :], spare[:, :], ALU.add
                                        ).then_inc(places_ready, 1)
                nc.vector.tensor_copy(words_f[:, :], every(PACK)).then_inc(steps, step.one())
                for i in reversed(range(PACK)):
                    done()
                    nc.vector.scalar_tensor_tensor(words_f[:, :], words_f[:, :], 8.0, every(i),
                                                   ALU.mult, ALU.add).then_inc(steps, step.one())
                done()
                nc.vector.tensor_copy(words[:, :], words_f[:, :]).then_inc(words_ready, 1)
                shared_last([1, 2, 3])
                dve.wait_ge(gap_exp_ready, 1)
                nc.vector.tensor_scalar(gap_sum[:, :], gap_exp[:, :], 1.0, None, ALU.add
                                        ).then_inc(steps, step.one())
                done()
                nc.vector.reciprocal(weight[:, 0, :], gap_sum[:, :]).then_inc(steps, step.one())
                done()
                nc.vector.tensor_tensor(weight[:, 1, :], gap_exp[:, :], weight[:, 0, :], ALU.mult
                                        ).then_inc(weight_ready, 1)

                def multiply(pair, u):
                    k, i = pair * 2 + u, u % 2
                    dve.wait_ge(gate_ready, k + 1)
                    dve.wait_ge(up_done, k + 1)
                    nc.vector.tensor_tensor(hidden[i][:, :], u_bank[i], gate[i][:, :], ALU.mult
                                            ).then_inc(hidden_ready, 1)

                def take_result(pair, u, first=False):
                    k, i = pair * 2 + u, u % 2
                    dve.wait_ge(down_done, k + 1)
                    if not first:
                        dve.wait_ge(result_stored[i], pair * 16)
                    nc.vector.tensor_copy(result[i][:, :], d_bank[:, 0:P]).then_inc(result_ready, 1)

                multiply(0, 0)
                for u in range(2):
                    multiply(0, u + 1)
                    take_result(0, u, first=True)
                with dve.Fori(1, PAIRS) as pair:
                    for u in range(2):
                        multiply(pair, u + 1)
                        take_result(pair, u)
                multiply(PAIRS, 1)
                for u in range(2):
                    take_result(PAIRS, u)

                dve.wait_ge(s_down_taken, CHUNKS)
                dve.wait_ge(weight_ready, 1)
                for q in range(QC):
                    dve.wait_ge(returned[q], 32)
                    for i in range(2):
                        done()
                        for t in range(q * CH, (q + 1) * CH):
                            nc.vector.scalar_tensor_tensor(
                                mixed[:, t, :], back[i][:, t, :], weight[:, i, t:t + 1], mixed[:, t, :],
                                ALU.mult, ALU.add).then_inc(steps, step.one())
                done()
                for b in range(B):
                    if b == 1:
                        dve.wait_ge(pool_mixed, 2 * QC)
                    layer_norm(lambda t: mixed[:, t, :], b * KT, KT, fin_var, fin_std, b + 1)
                    for t in range(b * KT, (b + 1) * KT):
                        nc.vector.tensor_scalar(mixed[:, t, :], mixed[:, t, :], mean_var[:, t, 0:1],
                                                rstd[:, t:t + 1], ALU.subtract, ALU.mult
                                                ).then_inc(steps, step.one())
                    done()
                    if b == 0:
                        dve.sem_inc(first_scaled, 1)
                for q in range(QC, CHUNKS):
                    part = slice(q * CH, (q + 1) * CH)
                    nc.vector.tensor_tensor(mixed[:, part, :], mixed[:, part, :], x_sb[:, part, :], ALU.add
                                            ).then_inc(half_done[1], 1)


def kernel(**inputs):
    import concourse.bacc as bacc
    from concourse.bass_utils import run_bass_kernel_spmd

    a = {k: np.asarray(v) for k, v in inputs.items()}
    wqkv = a["L0_attn_w_qkv"]
    arrays = {
        "x": a["L0_attn_x"],
        "wqkv": wqkv,
        "wq_t": wqkv[:, :C].T,
        "dirs": a["L0_attn_head_dirs"].reshape(1, H * HD),
        "scales": a["L0_attn_head_scales"].reshape(1, H),
        "w_out": a["L0_attn_w_out"],
        "router_t": a["L0_ffn_router_w"].T,
        "w_gate": np.concatenate([a["L0_ffn_w_gate"], a["L0_ffn_sw_gate"]]),
        "w_up": np.concatenate([a["L0_ffn_w_up"], a["L0_ffn_sw_up"]]),
        "w_down": np.concatenate([a["L0_ffn_w_down"], a["L0_ffn_sw_down"]]),
    }
    arrays = {f"in_{k}": np.ascontiguousarray(v) for k, v in arrays.items()}
    nc = bacc.Bacc("TRN2", target_bir_lowering=False, num_devices=1)
    args = [nc.dram_tensor(k, v.shape, mybir.dt.from_np(v.dtype), kind="ExternalInput").ap()
            for k, v in arrays.items()]
    out = nc.dram_tensor("out", (B, T, C), F32, kind="ExternalOutput").ap()
    program(nc, *args, out)
    r = run_bass_kernel_spmd(nc, [arrays], core_ids=[0])
    return r.results[0]["out"]
```
